# Optimizing a Trainium2 kernel written in Bass

```python
import numpy as np
import jax
import jax.numpy as jnp

def _softmax(x, axis=-1):
    return jax.nn.softmax(x, axis=axis)

def _gelu(x):
    return jax.nn.gelu(x, approximate=True)

def _silu(x):
    return jax.nn.silu(x)

def _sigmoid(x):
    return jax.nn.sigmoid(x)

def _layernorm(x, axis=-1, eps=1e-05):
    m = jnp.mean(x, axis=axis, keepdims=True)
    v = jnp.var(x, axis=axis, keepdims=True)
    return (x - m) / jnp.sqrt(v + eps)

def _scatter_add(tgt, idx, src, axis=0):
    return tgt.at[idx].add(src)

def _segment_sum(src, seg, n):
    return jax.ops.segment_sum(src, seg, n)
kernel_name = 'mk_pixart_seq_d4_seqx_r4_d05e4d'

def setup_inputs(seed: int=0):
    np.random.seed(seed)
    _w = jnp.asarray

    def _rec_inputs():
        import jax
        import jax.numpy as jnp
        _rk = jax.random.key(seed)
        x = -0.0003929 + 0.9999 * jax.random.normal(jax.random.fold_in(_rk, 1), (2, 1024, 256), jnp.float32)
        _lenS = 1024 - jax.random.randint(jax.random.fold_in(_rk, 7), (2,), 0, max(1, 1024 // 4) + 1, jnp.int32)
        _lenS2 = 64 - jax.random.randint(jax.random.fold_in(_rk, 8), (2,), 0, max(1, 64 // 4) + 1, jnp.int32)
        _ctx_1024P = jax.random.normal(jax.random.fold_in(_rk, 11), (2, 16, 256), jnp.float32)
        _ctx_1024c = jax.random.dirichlet(jax.random.fold_in(_rk, 511), 0.3 * jnp.ones((16,), jnp.float32), (2, 64))
        _ctx_1024t = jnp.einsum('bsk,bkd->bsd', _ctx_1024c, _ctx_1024P)
        _ctx_1024t = _ctx_1024t * jax.lax.rsqrt(jnp.mean(jnp.square(_ctx_1024t)) + 1e-12) * 0.953939
        ctx_1024 = -1.39393e-06 + 0.999914 * (_ctx_1024t + 0.3 * jax.random.normal(jax.random.fold_in(_rk, 611), (2, 64, 256), jnp.float32))
        cond_1024 = -0.00920427 + 1.00102 * jax.random.normal(jax.random.fold_in(_rk, 12), (2, 256), jnp.float32)
        return (x, ctx_1024, cond_1024)
    x, ctx_1024, cond_1024 = _rec_inputs()

    def _L0_xcond_setup():
        import jax, jax.numpy as jnp
        import numpy as np
        EPS = 1e-05

        def _ada_ln(x, c, W_ss, b_ss):
            mu = jnp.mean(x, axis=-1, keepdims=True)
            var = jnp.mean((x - mu) ** 2, axis=-1, keepdims=True)
            h = (x - mu) / jnp.sqrt(var + EPS)
            ss = jax.nn.silu(c) @ W_ss + b_ss
            scale, bias = jnp.split(ss, 2, axis=-1)
            return (1.0 + scale)[:, None, :] * h + bias[:, None, :]
        key = jax.random.key(seed)
        ks = jax.random.split(key, 12)
        B, Lq, Lkv, H = (8, 512, 128, 256)
        s = 0.02
        return {'x_q': jax.random.normal(ks[0], (B, Lq, H), jnp.float32), 'x_kv': jax.random.normal(ks[1], (B, Lkv, H), jnp.float32), 't_vec': jax.random.normal(ks[2], (B, H), jnp.float32), 'Wq': jax.random.normal(ks[3], (H, H), jnp.float32) * s, 'bq': jnp.zeros((H,), jnp.float32), 'Wkv': jax.random.normal(ks[4], (H, 2 * H), jnp.float32) * s, 'bkv': jnp.zeros((2 * H,), jnp.float32), 'Wp': jax.random.normal(ks[5], (H, H), jnp.float32) * s, 'bp': jnp.zeros((H,), jnp.float32), 'Wss_q': jax.random.normal(ks[6], (H, 2 * H), jnp.float32) * s, 'bss_q': jnp.zeros((2 * H,), jnp.float32), 'Wss_kv': jax.random.normal(ks[7], (H, 2 * H), jnp.float32) * s, 'bss_kv': jnp.zeros((2 * H,), jnp.float32)}
    _L0_xcond_all = _L0_xcond_setup()
    _L0_xcond_in = {k: v for k, v in _L0_xcond_all.items() if k in ('Wq', 'bq', 'Wkv', 'bkv', 'Wp', 'bp', 'Wss_q', 'bss_q', 'Wss_kv', 'bss_kv')}
    del _L0_xcond_all

    def _L1_xcond_setup():
        import jax, jax.numpy as jnp
        import numpy as np
        H = 256
        RH = 2 * H
        E = 3
        B, T, P = (8, 512, 64)
        LN_EPS = 1e-05

        def _layer_norm(x, gamma, beta):
            mu = jnp.mean(x, axis=-1, keepdims=True)
            var = jnp.mean(jnp.square(x - mu), axis=-1, keepdims=True)
            return (x - mu) * jax.lax.rsqrt(var + LN_EPS) * gamma + beta
        key = jax.random.key(seed)
        ks = jax.random.split(key, 24)
        s = lambda fan_in: 1.0 / np.sqrt(fan_in)
        inp = {'mix_hidden_states': jax.random.normal(ks[0], (B, T, H), jnp.float32), 'global_anchor': jax.random.normal(ks[1], (B, H), jnp.float32), 'prototype_bank': jax.random.normal(ks[2], (B, P, H), jnp.float32), 'ln_gamma': jnp.ones((H,), jnp.float32), 'ln_beta': jnp.zeros((H,), jnp.float32), 'Wq': jax.random.normal(ks[3], (H, H), jnp.float32) * s(H), 'Wk': jax.random.normal(ks[4], (H, H), jnp.float32) * s(H), 'Wv': jax.random.normal(ks[5], (H, H), jnp.float32) * s(H), 'router_W': jax.random.normal(ks[6], (3 * H, E), jnp.float32) * s(3 * H), 'router_b': jnp.zeros((E,), jnp.float32), 'e_w1': jax.random.normal(ks[7], (E, 3 * H, RH), jnp.float32) * s(3 * H), 'e_b1': jnp.zeros((E, RH), jnp.float32), 'e_w2': jax.random.normal(ks[8], (E, RH, H), jnp.float32) * s(RH), 'e_b2': jnp.zeros((E, H), jnp.float32), 'gate_w1': jax.random.normal(ks[9], (3 * H, H), jnp.float32) * s(3 * H), 'gate_b1': jnp.zeros((H,), jnp.float32), 'gate_w2': jax.random.normal(ks[10], (H, H), jnp.float32) * s(H), 'gate_b2': jnp.zeros((H,), jnp.float32), 'out_w': jax.random.normal(ks[11], (H, H), jnp.float32) * s(H), 'out_b': jnp.zeros((H,), jnp.float32)}
        return inp
    _L1_xcond_all = _L1_xcond_setup()
    _L1_xcond_in = {k: v for k, v in _L1_xcond_all.items() if k in ('ln_gamma', 'ln_beta', 'Wq', 'Wk', 'Wv', 'router_W', 'router_b', 'e_w1', 'e_b1', 'e_w2', 'e_b2', 'gate_w1', 'gate_b1', 'gate_w2', 'gate_b2', 'out_w', 'out_b')}
    del _L1_xcond_all

    def _L2_xcond_setup():
        import jax, jax.numpy as jnp
        import numpy as np
        LN_EPS = 1e-06

        def _ln(x):
            mu = jnp.mean(x, axis=-1, keepdims=True)
            var = jnp.var(x, axis=-1, keepdims=True)
            return (x - mu) * jax.lax.rsqrt(var + LN_EPS)
        key = jax.random.key(seed)
        H, NH = (256, 16)
        B, N, S = (4, 256, 77)
        MLP = int(H * 4.0)
        ks = jax.random.split(key, 20)
        s = 1.0 / np.sqrt(H)
        return {'x': jax.random.normal(ks[0], (B, N, H), jnp.float32), 'c': jax.random.normal(ks[1], (B, H), jnp.float32), 'context': jax.random.normal(ks[2], (B, S, H), jnp.float32), 'W_mod': jax.random.normal(ks[3], (H, 6 * H), jnp.float32) * s, 'b_mod': jnp.zeros((6 * H,), jnp.float32), 'W_qkv': jax.random.normal(ks[4], (H, 3 * H), jnp.float32) * s, 'b_qkv': jnp.zeros((3 * H,), jnp.float32), 'W_proj': jax.random.normal(ks[5], (H, H), jnp.float32) * s, 'b_proj': jnp.zeros((H,), jnp.float32), 'W_qc': jax.random.normal(ks[6], (H, H), jnp.float32) * s, 'b_qc': jnp.zeros((H,), jnp.float32), 'W_kvc': jax.random.normal(ks[7], (H, 2 * H), jnp.float32) * s, 'b_kvc': jnp.zeros((2 * H,), jnp.float32), 'W_cproj': jax.random.normal(ks[8], (H, H), jnp.float32) * s, 'b_cproj': jnp.zeros((H,), jnp.float32), 'W_mlp1': jax.random.normal(ks[9], (H, MLP), jnp.float32) * s, 'b_mlp1': jnp.zeros((MLP,), jnp.float32), 'W_mlp2': jax.random.normal(ks[10], (MLP, H), jnp.float32) * (1.0 / np.sqrt(MLP)), 'b_mlp2': jnp.zeros((H,), jnp.float32)}
    _L2_xcond_all = _L2_xcond_setup()
    _L2_xcond_in = {k: v for k, v in _L2_xcond_all.items() if k in ('W_mod', 'b_mod', 'W_qkv', 'b_qkv', 'W_proj', 'b_proj', 'W_qc', 'b_qc', 'W_kvc', 'b_kvc', 'W_cproj', 'b_cproj', 'W_mlp1', 'b_mlp1', 'W_mlp2', 'b_mlp2')}
    del _L2_xcond_all

    def _L3_xcond_setup():
        import jax, jax.numpy as jnp
        import numpy as np
        C = 256
        H = 16
        D = C // H
        WIN = 128
        SHIFT = 64
        TOPK = 16
        HID = 1024
        EPS = 1e-06

        def _ln(x):
            x32 = x.astype(jnp.float32)
            m = x32.mean(-1, keepdims=True)
            v = jnp.mean((x32 - m) ** 2, axis=-1, keepdims=True)
            return ((x32 - m) * jax.lax.rsqrt(v + EPS)).astype(x.dtype)

        def _self_attn(h, w_qkv, b_qkv, w_so, b_so):
            B, L, _ = h.shape
            qkv = h @ w_qkv + b_qkv
            qkv = jnp.roll(qkv, -SHIFT, axis=1)
            nw = L // WIN
            qkv = qkv.reshape(B, nw, WIN, 3, H, D)
            q, k, v = (qkv[:, :, :, 0], qkv[:, :, :, 1], qkv[:, :, :, 2])
            scores = jnp.einsum('bnqhd,bnkhd->bnhqk', q, k) / jnp.sqrt(jnp.float32(D)).astype(h.dtype)
            attn = jax.nn.softmax(scores, axis=-1)
            o = jnp.einsum('bnhqk,bnkhd->bnqhd', attn, v).reshape(B, L, C)
            o = jnp.roll(o, SHIFT, axis=1)
            return o @ w_so + b_so

        def _topk_cross_attn(h, ctx, w_q, b_q, w_kv, b_kv, w_co, b_co):
            B, L, _ = h.shape
            Lc = ctx.shape[1]
            q = (h @ w_q + b_q).reshape(B, L, H, D)
            kv = (ctx @ w_kv + b_kv).reshape(B, Lc, 2, H, D)
            k, v = (kv[:, :, 0], kv[:, :, 1])
            scores = jnp.einsum('bqhd,bkhd->bhqk', q, k) / jnp.sqrt(jnp.float32(D)).astype(h.dtype)
            top_s, top_i = jax.lax.top_k(scores, TOPK)
            attn = jax.nn.softmax(top_s, axis=-1)
            v_bh = jnp.transpose(v, (0, 2, 1, 3))
            vg = jnp.take_along_axis(v_bh[:, :, None, :, :], top_i[..., None], axis=3)
            o = jnp.einsum('bhqk,bhqkd->bqhd', attn, vg).reshape(B, L, C)
            return o @ w_co + b_co

        def _swiglu(h, w_m1, b_m1, w_m2, b_m2):
            u = h @ w_m1 + b_m1
            a, b = (u[..., :HID], u[..., HID:])
            return jax.nn.silu(a) * b @ w_m2 + b_m2
        key = jax.random.key(seed)
        ks = jax.random.split(key, 24)
        s = 0.02
        inp = {'x': jax.random.normal(ks[0], (2, 1024, C), jnp.float32), 'mod': jax.random.normal(ks[1], (2, C), jnp.float32), 'context': jax.random.normal(ks[2], (2, 256, C), jnp.float32), 'w_ada': jax.random.normal(ks[3], (C, 9 * C), jnp.float32) * s, 'b_ada': jnp.zeros((9 * C,), jnp.float32), 'w_qkv': jax.random.normal(ks[4], (C, 3 * C), jnp.float32) * s, 'b_qkv': jnp.zeros((3 * C,), jnp.float32), 'w_so': jax.random.normal(ks[5], (C, C), jnp.float32) * s, 'b_so': jnp.zeros((C,), jnp.float32), 'w_q': jax.random.normal(ks[6], (C, C), jnp.float32) * s, 'b_q': jnp.zeros((C,), jnp.float32), 'w_kv': jax.random.normal(ks[7], (C, 2 * C), jnp.float32) * s, 'b_kv': jnp.zeros((2 * C,), jnp.float32), 'w_co': jax.random.normal(ks[8], (C, C), jnp.float32) * s, 'b_co': jnp.zeros((C,), jnp.float32), 'w_m1': jax.random.normal(ks[9], (C, 2 * HID), jnp.float32) * s, 'b_m1': jnp.zeros((2 * HID,), jnp.float32), 'w_m2': jax.random.normal(ks[10], (HID, C), jnp.float32) * s, 'b_m2': jnp.zeros((C,), jnp.float32)}
        return inp
    _L3_xcond_all = _L3_xcond_setup()
    _L3_xcond_in = {k: v for k, v in _L3_xcond_all.items() if k in ('w_ada', 'b_ada', 'w_qkv', 'b_qkv', 'w_so', 'b_so', 'w_q', 'b_q', 'w_kv', 'b_kv', 'w_co', 'b_co', 'w_m1', 'b_m1', 'w_m2', 'b_m2')}
    del _L3_xcond_all
    return {'x': x, 'ctx_1024': ctx_1024, 'cond_1024': cond_1024, 'L0_xcond_Wq': _L0_xcond_in['Wq'], 'L0_xcond_bq': _L0_xcond_in['bq'], 'L0_xcond_Wkv': _L0_xcond_in['Wkv'], 'L0_xcond_bkv': _L0_xcond_in['bkv'], 'L0_xcond_Wp': _L0_xcond_in['Wp'], 'L0_xcond_bp': _L0_xcond_in['bp'], 'L0_xcond_Wss_q': _L0_xcond_in['Wss_q'], 'L0_xcond_bss_q': _L0_xcond_in['bss_q'], 'L0_xcond_Wss_kv': _L0_xcond_in['Wss_kv'], 'L0_xcond_bss_kv': _L0_xcond_in['bss_kv'], 'L1_xcond_ln_gamma': _L1_xcond_in['ln_gamma'], 'L1_xcond_ln_beta': _L1_xcond_in['ln_beta'], 'L1_xcond_Wq': _L1_xcond_in['Wq'], 'L1_xcond_Wk': _L1_xcond_in['Wk'], 'L1_xcond_Wv': _L1_xcond_in['Wv'], 'L1_xcond_router_W': _L1_xcond_in['router_W'], 'L1_xcond_router_b': _L1_xcond_in['router_b'], 'L1_xcond_e_w1': _L1_xcond_in['e_w1'], 'L1_xcond_e_b1': _L1_xcond_in['e_b1'], 'L1_xcond_e_w2': _L1_xcond_in['e_w2'], 'L1_xcond_e_b2': _L1_xcond_in['e_b2'], 'L1_xcond_gate_w1': _L1_xcond_in['gate_w1'], 'L1_xcond_gate_b1': _L1_xcond_in['gate_b1'], 'L1_xcond_gate_w2': _L1_xcond_in['gate_w2'], 'L1_xcond_gate_b2': _L1_xcond_in['gate_b2'], 'L1_xcond_out_w': _L1_xcond_in['out_w'], 'L1_xcond_out_b': _L1_xcond_in['out_b'], 'L2_xcond_W_mod': _L2_xcond_in['W_mod'], 'L2_xcond_b_mod': _L2_xcond_in['b_mod'], 'L2_xcond_W_qkv': _L2_xcond_in['W_qkv'], 'L2_xcond_b_qkv': _L2_xcond_in['b_qkv'], 'L2_xcond_W_proj': _L2_xcond_in['W_proj'], 'L2_xcond_b_proj': _L2_xcond_in['b_proj'], 'L2_xcond_W_qc': _L2_xcond_in['W_qc'], 'L2_xcond_b_qc': _L2_xcond_in['b_qc'], 'L2_xcond_W_kvc': _L2_xcond_in['W_kvc'], 'L2_xcond_b_kvc': _L2_xcond_in['b_kvc'], 'L2_xcond_W_cproj': _L2_xcond_in['W_cproj'], 'L2_xcond_b_cproj': _L2_xcond_in['b_cproj'], 'L2_xcond_W_mlp1': _L2_xcond_in['W_mlp1'], 'L2_xcond_b_mlp1': _L2_xcond_in['b_mlp1'], 'L2_xcond_W_mlp2': _L2_xcond_in['W_mlp2'], 'L2_xcond_b_mlp2': _L2_xcond_in['b_mlp2'], 'L3_xcond_w_ada': _L3_xcond_in['w_ada'], 'L3_xcond_b_ada': _L3_xcond_in['b_ada'], 'L3_xcond_w_qkv': _L3_xcond_in['w_qkv'], 'L3_xcond_b_qkv': _L3_xcond_in['b_qkv'], 'L3_xcond_w_so': _L3_xcond_in['w_so'], 'L3_xcond_b_so': _L3_xcond_in['b_so'], 'L3_xcond_w_q': _L3_xcond_in['w_q'], 'L3_xcond_b_q': _L3_xcond_in['b_q'], 'L3_xcond_w_kv': _L3_xcond_in['w_kv'], 'L3_xcond_b_kv': _L3_xcond_in['b_kv'], 'L3_xcond_w_co': _L3_xcond_in['w_co'], 'L3_xcond_b_co': _L3_xcond_in['b_co'], 'L3_xcond_w_m1': _L3_xcond_in['w_m1'], 'L3_xcond_b_m1': _L3_xcond_in['b_m1'], 'L3_xcond_w_m2': _L3_xcond_in['w_m2'], 'L3_xcond_b_m2': _L3_xcond_in['b_m2']}

def reference(x, ctx_1024, cond_1024, L0_xcond_Wq, L0_xcond_bq, L0_xcond_Wkv, L0_xcond_bkv, L0_xcond_Wp, L0_xcond_bp, L0_xcond_Wss_q, L0_xcond_bss_q, L0_xcond_Wss_kv, L0_xcond_bss_kv, L1_xcond_ln_gamma, L1_xcond_ln_beta, L1_xcond_Wq, L1_xcond_Wk, L1_xcond_Wv, L1_xcond_router_W, L1_xcond_router_b, L1_xcond_e_w1, L1_xcond_e_b1, L1_xcond_e_w2, L1_xcond_e_b2, L1_xcond_gate_w1, L1_xcond_gate_b1, L1_xcond_gate_w2, L1_xcond_gate_b2, L1_xcond_out_w, L1_xcond_out_b, L2_xcond_W_mod, L2_xcond_b_mod, L2_xcond_W_qkv, L2_xcond_b_qkv, L2_xcond_W_proj, L2_xcond_b_proj, L2_xcond_W_qc, L2_xcond_b_qc, L2_xcond_W_kvc, L2_xcond_b_kvc, L2_xcond_W_cproj, L2_xcond_b_cproj, L2_xcond_W_mlp1, L2_xcond_b_mlp1, L2_xcond_W_mlp2, L2_xcond_b_mlp2, L3_xcond_w_ada, L3_xcond_b_ada, L3_xcond_w_qkv, L3_xcond_b_qkv, L3_xcond_w_so, L3_xcond_b_so, L3_xcond_w_q, L3_xcond_b_q, L3_xcond_w_kv, L3_xcond_b_kv, L3_xcond_w_co, L3_xcond_b_co, L3_xcond_w_m1, L3_xcond_b_m1, L3_xcond_w_m2, L3_xcond_b_m2):
    import jax
    import jax.numpy as jnp

    def _L0_xcond_ref(x_q, x_kv, t_vec, Wq, bq, Wkv, bkv, Wp, bp, Wss_q, bss_q, Wss_kv, bss_kv):
        import jax, jax.numpy as jnp
        import numpy as np
        EPS = 1e-05

        def _ada_ln(x, c, W_ss, b_ss):
            mu = jnp.mean(x, axis=-1, keepdims=True)
            var = jnp.mean((x - mu) ** 2, axis=-1, keepdims=True)
            h = (x - mu) / jnp.sqrt(var + EPS)
            ss = jax.nn.silu(c) @ W_ss + b_ss
            scale, bias = jnp.split(ss, 2, axis=-1)
            return (1.0 + scale)[:, None, :] * h + bias[:, None, :]
        B, Lq, H = x_q.shape
        Lkv = x_kv.shape[1]
        nh = 16
        dh = H // nh
        xq = _ada_ln(x_q, t_vec, Wss_q, bss_q)
        xkv = _ada_ln(x_kv, t_vec, Wss_kv, bss_kv)
        q = (xq @ Wq + bq).reshape(B, Lq, nh, dh)
        kv = (xkv @ Wkv + bkv).reshape(B, Lkv, 2, nh, dh)
        k = kv[:, :, 0]
        v = kv[:, :, 1]
        scores = jnp.einsum('bqhd,bkhd->bhqk', q, k) / jnp.sqrt(jnp.float32(dh))
        attn = jax.nn.softmax(scores, axis=-1)
        out = jnp.einsum('bhqk,bkhd->bqhd', attn, v).reshape(B, Lq, H)
        return x_q + (out @ Wp + bp)

    def _L1_xcond_ref(mix_hidden_states, global_anchor, prototype_bank, ln_gamma, ln_beta, Wq, Wk, Wv, router_W, router_b, e_w1, e_b1, e_w2, e_b2, gate_w1, gate_b1, gate_w2, gate_b2, out_w, out_b):
        import jax, jax.numpy as jnp
        import numpy as np
        H = 256
        RH = 2 * H
        E = 3
        B, T, P = (8, 512, 64)
        LN_EPS = 1e-05

        def _layer_norm(x, gamma, beta):
            mu = jnp.mean(x, axis=-1, keepdims=True)
            var = jnp.mean(jnp.square(x - mu), axis=-1, keepdims=True)
            return (x - mu) * jax.lax.rsqrt(var + LN_EPS) * gamma + beta
        x = mix_hidden_states
        nx = _layer_norm(x, ln_gamma, ln_beta)
        q = nx @ Wq
        k = prototype_bank @ Wk
        v = prototype_bank @ Wv
        scores = jnp.einsum('bth,bph->btp', q, k) * H ** (-0.5)
        weights = jax.nn.softmax(scores, axis=-1)
        evidence = jnp.einsum('btp,bph->bth', weights, v)
        anchor = jnp.broadcast_to(global_anchor[:, None, :], nx.shape)
        combined = jnp.concatenate([nx, evidence, anchor], axis=-1)
        router_logits = combined @ router_W + router_b
        router_probs = jax.nn.softmax(router_logits, axis=-1)
        h = jax.nn.silu(jnp.einsum('btc,ecr->bter', combined, e_w1) + e_b1)
        expert_out = jnp.einsum('bter,erh->bteh', h, e_w2) + e_b2
        routed = jnp.sum(expert_out * router_probs[..., None], axis=-2)
        g = jax.nn.sigmoid(jax.nn.silu(combined @ gate_w1 + gate_b1) @ gate_w2 + gate_b2)
        refined_delta = g * (routed @ out_w + out_b)
        return x + refined_delta

    def _L2_xcond_ref(x, c, context, W_mod, b_mod, W_qkv, b_qkv, W_proj, b_proj, W_qc, b_qc, W_kvc, b_kvc, W_cproj, b_cproj, W_mlp1, b_mlp1, W_mlp2, b_mlp2):
        import jax, jax.numpy as jnp
        import numpy as np
        LN_EPS = 1e-06

        def _ln(x):
            mu = jnp.mean(x, axis=-1, keepdims=True)
            var = jnp.var(x, axis=-1, keepdims=True)
            return (x - mu) * jax.lax.rsqrt(var + LN_EPS)
        B, N, H = x.shape
        NH = 16
        hd = H // NH
        scale = hd ** (-0.5)
        c_proj = jax.nn.silu(c) @ W_mod + b_mod
        shift_a, scale_a, gate_a, shift_m, scale_m, gate_m = jnp.split(c_proj, 6, axis=-1)

        def modulate(t, shift, sc):
            return t * (1 + sc[:, None]) + shift[:, None]
        x_norm = modulate(_ln(x), shift_a, scale_a)
        qkv = x_norm @ W_qkv + b_qkv
        q, k, v = jnp.split(qkv, 3, axis=-1)
        q = q.reshape(B, N, NH, hd).transpose(0, 2, 1, 3)
        k = k.reshape(B, N, NH, hd).transpose(0, 2, 1, 3)
        v = v.reshape(B, N, NH, hd).transpose(0, 2, 1, 3)
        attn_w = jax.nn.softmax(jnp.einsum('bhqd,bhkd->bhqk', q, k) * scale, axis=-1)
        attn_out = jnp.einsum('bhqk,bhkd->bhqd', attn_w, v)
        attn_out = attn_out.transpose(0, 2, 1, 3).reshape(B, N, H)
        attn_out = attn_out @ W_proj + b_proj
        x = x + gate_a[:, None] * attn_out
        S = context.shape[1]
        q_c = _ln(x) @ W_qc + b_qc
        kv_c = _ln(context) @ W_kvc + b_kvc
        k_c, v_c = jnp.split(kv_c, 2, axis=-1)
        q_c = q_c.reshape(B, N, NH, hd).transpose(0, 2, 1, 3)
        k_c = k_c.reshape(B, S, NH, hd).transpose(0, 2, 1, 3)
        v_c = v_c.reshape(B, S, NH, hd).transpose(0, 2, 1, 3)
        c_attn_w = jax.nn.softmax(jnp.einsum('bhqd,bhsd->bhqs', q_c, k_c) * scale, axis=-1)
        c_attn_out = jnp.einsum('bhqs,bhsd->bhqd', c_attn_w, v_c)
        c_attn_out = c_attn_out.transpose(0, 2, 1, 3).reshape(B, N, H)
        c_attn_out = c_attn_out @ W_cproj + b_cproj
        x = x + c_attn_out
        x_norm2 = modulate(_ln(x), shift_m, scale_m)
        h = jax.nn.gelu(x_norm2 @ W_mlp1 + b_mlp1)
        h = h @ W_mlp2 + b_mlp2
        x = x + gate_m[:, None] * h
        return x

    def _L3_xcond_ref(x, mod, context, w_ada, b_ada, w_qkv, b_qkv, w_so, b_so, w_q, b_q, w_kv, b_kv, w_co, b_co, w_m1, b_m1, w_m2, b_m2):
        import jax, jax.numpy as jnp
        import numpy as np
        C = 256
        H = 16
        D = C // H
        WIN = 128
        SHIFT = 64
        TOPK = 16
        HID = 1024
        EPS = 1e-06

        def _ln(x):
            x32 = x.astype(jnp.float32)
            m = x32.mean(-1, keepdims=True)
            v = jnp.mean((x32 - m) ** 2, axis=-1, keepdims=True)
            return ((x32 - m) * jax.lax.rsqrt(v + EPS)).astype(x.dtype)

        def _self_attn(h, w_qkv, b_qkv, w_so, b_so):
            B, L, _ = h.shape
            qkv = h @ w_qkv + b_qkv
            qkv = jnp.roll(qkv, -SHIFT, axis=1)
            nw = L // WIN
            qkv = qkv.reshape(B, nw, WIN, 3, H, D)
            q, k, v = (qkv[:, :, :, 0], qkv[:, :, :, 1], qkv[:, :, :, 2])
            scores = jnp.einsum('bnqhd,bnkhd->bnhqk', q, k) / jnp.sqrt(jnp.float32(D)).astype(h.dtype)
            attn = jax.nn.softmax(scores, axis=-1)
            o = jnp.einsum('bnhqk,bnkhd->bnqhd', attn, v).reshape(B, L, C)
            o = jnp.roll(o, SHIFT, axis=1)
            return o @ w_so + b_so

        def _topk_cross_attn(h, ctx, w_q, b_q, w_kv, b_kv, w_co, b_co):
            B, L, _ = h.shape
            Lc = ctx.shape[1]
            q = (h @ w_q + b_q).reshape(B, L, H, D)
            kv = (ctx @ w_kv + b_kv).reshape(B, Lc, 2, H, D)
            k, v = (kv[:, :, 0], kv[:, :, 1])
            scores = jnp.einsum('bqhd,bkhd->bhqk', q, k) / jnp.sqrt(jnp.float32(D)).astype(h.dtype)
            top_s, top_i = jax.lax.top_k(scores, TOPK)
            attn = jax.nn.softmax(top_s, axis=-1)
            v_bh = jnp.transpose(v, (0, 2, 1, 3))
            vg = jnp.take_along_axis(v_bh[:, :, None, :, :], top_i[..., None], axis=3)
            o = jnp.einsum('bhqk,bhqkd->bqhd', attn, vg).reshape(B, L, C)
            return o @ w_co + b_co

        def _swiglu(h, w_m1, b_m1, w_m2, b_m2):
            u = h @ w_m1 + b_m1
            a, b = (u[..., :HID], u[..., HID:])
            return jax.nn.silu(a) * b @ w_m2 + b_m2
        m = jax.nn.silu(mod) @ w_ada + b_ada
        sh_msa, sc_msa, g_msa, sh_mca, sc_mca, g_mca, sh_mlp, sc_mlp, g_mlp = [m[:, i * C:(i + 1) * C][:, None, :] for i in range(9)]
        h = _ln(x) * (1 + sc_msa) + sh_msa
        h = _self_attn(h, w_qkv, b_qkv, w_so, b_so)
        x = x + h * g_msa
        h = _ln(x) * (1 + sc_mca) + sh_mca
        h = _topk_cross_attn(h, context, w_q, b_q, w_kv, b_kv, w_co, b_co)
        x = x + h * g_mca
        h = _ln(x) * (1 + sc_mlp) + sh_mlp
        h = _swiglu(h, w_m1, b_m1, w_m2, b_m2)
        x = x + h * g_mlp
        return x
    x = _L0_xcond_ref(x, ctx_1024, cond_1024, L0_xcond_Wq, L0_xcond_bq, L0_xcond_Wkv, L0_xcond_bkv, L0_xcond_Wp, L0_xcond_bp, L0_xcond_Wss_q, L0_xcond_bss_q, L0_xcond_Wss_kv, L0_xcond_bss_kv)
    x = _L1_xcond_ref(x, cond_1024, ctx_1024, L1_xcond_ln_gamma, L1_xcond_ln_beta, L1_xcond_Wq, L1_xcond_Wk, L1_xcond_Wv, L1_xcond_router_W, L1_xcond_router_b, L1_xcond_e_w1, L1_xcond_e_b1, L1_xcond_e_w2, L1_xcond_e_b2, L1_xcond_gate_w1, L1_xcond_gate_b1, L1_xcond_gate_w2, L1_xcond_gate_b2, L1_xcond_out_w, L1_xcond_out_b)
    x = _L2_xcond_ref(x, cond_1024, ctx_1024, L2_xcond_W_mod, L2_xcond_b_mod, L2_xcond_W_qkv, L2_xcond_b_qkv, L2_xcond_W_proj, L2_xcond_b_proj, L2_xcond_W_qc, L2_xcond_b_qc, L2_xcond_W_kvc, L2_xcond_b_kvc, L2_xcond_W_cproj, L2_xcond_b_cproj, L2_xcond_W_mlp1, L2_xcond_b_mlp1, L2_xcond_W_mlp2, L2_xcond_b_mlp2)
    x = _L3_xcond_ref(x, cond_1024, ctx_1024, L3_xcond_w_ada, L3_xcond_b_ada, L3_xcond_w_qkv, L3_xcond_b_qkv, L3_xcond_w_so, L3_xcond_b_so, L3_xcond_w_q, L3_xcond_b_q, L3_xcond_w_kv, L3_xcond_b_kv, L3_xcond_w_co, L3_xcond_b_co, L3_xcond_w_m1, L3_xcond_b_m1, L3_xcond_w_m2, L3_xcond_b_m2)
    return x

_drawn_inputs = setup_inputs


def setup_inputs(seed=0):
    import zlib

    import numpy as np

    out = dict(_drawn_inputs(seed))
    spreads = {'L0_xcond_bq': (0.0, 2.0),
     'L0_xcond_bkv': (0.0, 0.1),
     'L0_xcond_bp': (0.0, 0.1),
     'L0_xcond_bss_q': (0.0, 0.8),
     'L0_xcond_bss_kv': (0.0, 0.606),
     'L1_xcond_ln_gamma': (1.0, 0.6),
     'L1_xcond_ln_beta': (0.0, 0.617),
     'L1_xcond_router_b': (0.0, 0.433),
     'L1_xcond_e_b1': (0.0, 0.468),
     'L1_xcond_e_b2': (0.0, 0.1),
     'L1_xcond_gate_b1': (0.0, 0.8),
     'L1_xcond_gate_b2': (0.0, 0.8),
     'L1_xcond_out_b': (0.0, 0.1),
     'L2_xcond_b_mod': (0.0, 0.1),
     'L2_xcond_b_qkv': (0.0, 0.1),
     'L2_xcond_b_proj': (0.0, 0.1),
     'L2_xcond_b_qc': (0.0, 0.531),
     'L2_xcond_b_kvc': (0.0, 0.1),
     'L2_xcond_b_cproj': (0.0, 0.1),
     'L2_xcond_b_mlp1': (0.0, 0.1),
     'L2_xcond_b_mlp2': (0.0, 0.1),
     'L3_xcond_b_ada': (0.0, 0.514),
     'L3_xcond_b_qkv': (0.0, 0.8),
     'L3_xcond_b_so': (0.0, 0.454),
     'L3_xcond_b_q': (0.0, 0.8),
     'L3_xcond_b_kv': (0.0, 0.8),
     'L3_xcond_b_co': (0.0, 0.459),
     'L3_xcond_b_m1': (0.0, 0.8),
     'L3_xcond_b_m2': (0.0, 2.0)}
    factors = {'L0_xcond_Wq': 8.0,
     'L0_xcond_Wss_q': 8.0,
     'L3_xcond_w_qkv': 5.186,
     'L3_xcond_w_so': 4.705,
     'L3_xcond_w_q': 8.0,
     'L3_xcond_w_kv': 5.975,
     'L3_xcond_w_co': 5.452,
     'L3_xcond_w_m1': 8.0,
     'L3_xcond_w_m2': 8.0}
    for name, (base, spread) in spreads.items():
        noise = np.random.default_rng([zlib.crc32(name.encode()), seed]).standard_normal(out[name].shape)
        drawn = base * np.exp(spread * noise) if base else spread * noise
        out[name] = jnp.asarray(drawn.astype(out[name].dtype))
    for name, factor in factors.items():
        out[name] = (out[name] * factor).astype(out[name].dtype)
    return out
```

```python
from contextlib import ExitStack

import numpy as np
import concourse.bass as bass
import concourse.mybir as mybir

F32 = mybir.dt.float32
F32R = mybir.dt.float32r
ALU = mybir.AluOpType
ACT = mybir.ActivationFunctionType
X = mybir.AxisListType.X

P = 128
D = 256
KC = D // P
B = 2
L = 1024
T = L // P
NB = 2
TB = T // NB
BLK = TB * P
H = 16
HD = D // H
HC = P // HD
S = 64
SHIFT = 64
E = 3
RH = 512
MC = E * RH // P
HID = 1024
NC_HID = HID // P
TOPK = 16
VS = HD + 1
QK_SCALE = float(HD) ** -0.5
L1_SCALE = float(D) ** -0.5
EPS5, EPS6 = 1e-5, 1e-6
LOWEST = -3.4028234663852886e38

M_SC_Q, M_SH_Q, M_SC_KV, M_SH_KV = 0, 2, 4, 6
M_SH_A, M_SC_A, M_G_A, M_SH_M, M_SC_M, M_G_M = 8, 10, 12, 14, 16, 18
M3_SH_SA, M3_SC_SA, M3_G_SA, M3_SH_CA, M3_SC_CA, M3_G_CA, M3_SH_ML, M3_SC_ML, M3_G_ML = range(20, 38, 2)
N_MOD = 38
M_BG = 38
GATED = (M_G_A, M_G_M, M3_G_SA, M3_G_CA, M3_G_ML)
SCALES = (M_SC_Q, M_SC_KV, M_SC_A, M_SC_M, M3_SC_SA, M3_SC_CA, M3_SC_ML)
M_HB = 48
N_MC = 62
C_BQ0, C_BP0, C_BK0, C_GAMMA, C_BETA, C_GB2, C_OUTB = range(62, 76, 2)
C_BQ2, C_BK2, C_BQC, C_BKC, C_BCP, C_BM1 = 76, 78, 80, 82, 84, 86
C_BQ3, C_BK3, C_BQ3C, C_BK3C, C_BM13 = 94, 96, 98, 100, 102
C_COND = 118
N_COL = 122

N_LN, N_Q, N_RES, N_CA = 8, 3, 8, 3
N_RING = 2 * 4 + 8 * 4 + H * T * 2 + 8 * 2 + 4 * 2
N_RA = 12 * 16
N_UNIT = T * KC


def build(nc, out, g):
    es = ExitStack()
    with es:
        base = (nc.sbuf_base + 63) // 64 * 64
        top = [base]

        def at(name, shape, dt, offset):
            return nc.alloc_sbuf_tensor_at(name, shape, dt, offset=offset)

        def keep(name, shape, dt=F32):
            size = int(np.prod(shape[1:])) * 4
            o = top[0]
            top[0] = o + (size + 31) // 32 * 32
            return at(name, shape, dt, o)

        def region(size):
            o = top[0]
            top[0] += size
            return o

        def sem(name):
            return es.enter_context(nc.semaphore(name))

        ident = keep("ident", [P, P])
        head_mask = keep("head_mask", [P, HC])
        ones_ctx = keep("ones_ctx", [P, 32])
        ones_win = keep("ones_win", [P, 2, 32])
        sel = keep("sel", [P, 4, 4, P], F32R)
        k_aug = keep("k_aug", [P, 1])
        minus_half = keep("minus_half", [P, TB])
        sel3 = keep("sel3", [E, E, P])
        b2 = keep("b2", [E, D])
        vb2 = keep("vb2", [P, D])
        vb3 = keep("vb3", [P, D])
        rb = keep("rb", [P, E])
        colT = keep("colT", [P, N_COL])
        mod2 = keep("mod2", [P, B, N_MC])
        kT2 = keep("kT2", [P, 3, KC, B, S])
        v_ctx2 = keep("v_ctx2", [P, B, 3, HC, 32])
        kw2 = keep("kw2", [P, KC, B, S])
        N_VW = E * RH + D + E
        vw2 = keep("vw2", [S, B, N_VW])
        rc2 = keep("rc2", [P, B, E])
        mod = keep("mod", [P, N_MC])
        v_ctx = keep("v_ctx", [P, 3, HC, 32])
        kw = keep("kw", [P, KC, S])
        kT = keep("kT", [P, 3, KC, S])
        rc = keep("rc", [P, E])
        x = keep("x", [P, T, D])
        s_sel = at("s_sel", [P, 4, 4, P], F32, top[0])
        hT = keep("hT", [P, NB, KC, BLK])
        st = keep("st", [P, NB, TB, 6])
        mv = keep("mv", [P, NB, TB, 2])
        ve = keep("ve", [P, NB, TB])
        rstd = keep("rstd", [P, NB, TB])
        mx = keep("mx", [P, 2, H])
        mxp = keep("mxp", [P, 4, T, 2])
        mm = keep("mm", [P, 4, T])
        mh = keep("mh", [P, 4, T], F32R)
        ml = keep("ml", [P, 4, T])
        fr = keep("fr", [P, 2, TB, 4])
        r1m = keep("r1m", [P, NB, TB])
        lg = keep("lg", [P, NB, TB, E])
        rm = keep("rm", [P, NB, TB])

        RA = region(40 * 1024 + 64)
        RC1 = region(34 * 1024)
        RC2 = region(24 * 1024)
        RF = region(48 * 1024)
        assert top[0] <= nc.sbuf_usable_end, (top[0], nc.sbuf_usable_end)
        K1 = 1024

        def weights(start, items):
            made, o = [], start
            for name, shape in items:
                made.append(at(name, shape, F32, o))
                o += (int(np.prod(shape[1:])) * 4 + 31) // 32 * 32
            return made, o

        (wq0, wp0, w1, wg1, wr, w2, wg2, wout, wv2, wqk2), e0 = weights(RA, [
            ("wq0", [P, KC, D]), ("wp0", [P, KC, D]), ("w1", [P, E, KC, RH]), ("wg1", [P, KC, D]),
            ("wr", [P, KC, E]), ("w2", [P, MC, D]), ("wg2", [P, KC, D]), ("wout", [P, KC, D]),
            ("wv2", [P, KC, D]), ("wqk2", [P, KC, 2 * D])])
        assert e0 <= RC1
        (wproj, wqc, wcp, wm1, wm2, wqkv3, wso, wq3, wco), e1 = weights(RC1, [
            ("wproj", [P, KC, D]), ("wqc", [P, KC, D]), ("wcp", [P, KC, D]), ("wm1", [P, KC, HID]),
            ("wm2", [P, NC_HID, D]), ("wqkv3", [P, KC, 3 * D]), ("wso", [P, KC, D]), ("wq3", [P, KC, D]),
            ("wco", [P, KC, D])])
        assert e1 <= RC2
        (w3a, w3b), e2 = weights(RC2, [("w3a", [P, KC, 2 * HID]), ("w3b", [P, NC_HID, D])])
        assert e2 <= RF

        (s_ss_q, s_ss_kv, s_mod, s_ada, s_kv0, s_q1, s_k1, s_v1, s_ev, s_an, s_gev, s_gan, s_rev, s_ran, s_kvc, s_kv3,
         s_rows, s_ctx, s_xh, s_ctxT, s_k1T, s_wqT, s_vT, s_crep, s_vb, s_silu, s_st), e3 = weights(RC1, [
             ("s_ss_q", [P, KC, 2 * D]), ("s_ss_kv", [P, KC, 2 * D]), ("s_mod", [P, KC, 6 * D]),
             ("s_ada", [P, KC, 9 * D]), ("s_kv0", [P, KC, 2 * D]), ("s_q1", [P, KC, D]), ("s_k1", [P, KC, D]),
             ("s_v1", [P, KC, D]), ("s_ev", [P, E, KC, RH]), ("s_an", [P, E, KC, RH]), ("s_gev", [P, KC, D]),
             ("s_gan", [P, KC, D]), ("s_rev", [P, KC, E]), ("s_ran", [P, KC, E]), ("s_kvc", [P, KC, 2 * D]),
             ("s_kv3", [P, KC, 2 * D]), ("s_rows", [P, P]), ("s_ctx", [P, D]), ("s_xh", [P, 3, D]),
             ("s_ctxT", [P, 3, KC, B, 2, S]), ("s_k1T", [P, KC, B * S]), ("s_wqT", [P, KC, D]),
             ("s_vT", [P, KC, B * S]), ("s_crep", [P, KC, B, P]), ("s_vb", [P, 3, D]), ("s_silu", [P, B * KC]),
             ("s_st", [P, 16])])
        assert e3 <= top[0], (e3, top[0])

        xhat = at("xhat", [P, T, D], F32, RF)
        yT = at("yT", [P, NB, KC, BLK], F32, RF)
        taken = at("taken", [P, 2, H * S], F32, RF)
        qT = at("qT", [P, NB, KC, BLK], F32, RF + 8 * K1)
        oT = at("oT", [P, NB, KC, BLK], F32, RF + 8 * K1)
        ring = at("ring", [P, 4, BLK], F32, RF + 16 * K1)
        kblk = at("kblk", [P, KC, HC, S], F32, RF + 16 * K1)
        rs = at("rs", [P, BLK], F32, RF + 20 * K1)
        m8 = at("m8", [P, 2, H, TOPK], F32, RF + 22 * K1)
        prob = at("prob", [P, 2, 1024], F32, RF + 24 * K1)
        probT = at("probT", [P, HC, BLK], F32, RF + 32 * K1)
        wprobT = at("wprobT", [P, 2, HC, P], F32, RF + 32 * K1)
        wkblk = at("wkblk", [P, 2, HC, P], F32, RF + 40 * K1)
        vw = at("vw", [S, N_VW], F32, RC2)
        p1T = at("p1T", [S, NB, BLK], F32, RC2 + 8 * K1)
        gT = at("gT", [P, NB, KC, BLK], F32, RC2 + 12 * K1)
        g1 = [at("g1_0", [P, KC, BLK], F32, RC2 + 20 * K1), at("g1_1", [P, KC, BLK], F32, RF + 44 * K1)]
        p1 = at("p1", [P, NB, TB, S], F32, RF + 24 * K1)
        pT = at("pT", [E, NB, BLK], F32, RF + 26 * K1)
        p_bc = at("p_bc", [P, NB, E, BLK], F32, RF + 32 * K1)
        rT = [at("rT_0", [P, KC, BLK], F32, RF + 44 * K1), at("rT_1", [P, KC, BLK], F32, RC2 + 20 * K1)]
        qx = at("qx", [P, 4, L], F32R, RA)
        kx = at("kx", [P, 4, L], F32R, RA + 16 * K1)
        dense = [at(n, [P, L], F32R, o) for n, o in (("q_hi", RC2 + 8 * K1), ("q_lo", RA + 32 * K1),
                                                     ("k_hi", RC2), ("k_lo", RC2 + 4 * K1))]
        v2 = at("v2", [P, T, H * VS + HD], F32, RC2 + 12 * K1)
        pt = at("pt", [P, 8, L], F32, RF + 16 * K1)
        accS = at("accS", [P, L], F32, RF + 8 * K1)
        mt = at("mt", [P, T, P], F32, RF + 12 * K1)
        v3 = at("v3", [P, T, H, 32], F32, RA)
        kT3 = at("kT3", [P, NB, KC, BLK], F32, RA + 16 * K1)

        ps = es.enter_context(nc.psum_tensor("ps", [P, 8, 512], F32))

        consts_ld, rows_ld, ctx_ld = sem("consts_ld"), sem("rows_ld"), sem("ctx_ld")
        s_mod_ld, s_kv_ld, s_l1_ld, rc1_ld = sem("s_mod_ld"), sem("s_kv_ld"), sem("s_l1_ld"), sem("rc1_ld")
        ra_ld, rc2_ld, out_stored = sem("ra_ld"), sem("rc2_ld"), sem("out_stored")
        x_ld = [sem("x_ld0"), sem("x_ld1")]
        set_pe, set_act, set_dve, set_pool = sem("set_pe"), sem("set_act"), sem("set_dve"), sem("set_pool")
        dve_step, ctx_var, ctx_rstd = sem("dve_step"), sem("ctx_var"), sem("ctx_rstd")
        begun = sem("begun")
        ve_ready, rstd_ready, xhat_ready = sem("ve_ready"), sem("rstd_ready"), sem("xhat_ready")
        ln_turned, hT_ready = sem("ln_turned"), sem("hT_ready")
        q_done, qT_ready = sem("q_done"), sem("qT_ready")
        kblk_ready, s_ready, s_read, p_exp, p_turned, pT_ready = (sem(n) for n in (
            "kblk_ready", "s_ready", "s_read", "p_exp", "p_turned", "pT_ready"))
        top_exp = sem("top_exp")
        pv_done, oT_ready = sem("pv_done"), sem("oT_ready")
        y_done, yT_ready, y_turned, x_final = sem("y_done"), sem("yT_ready"), sem("y_turned"), sem("x_final")
        p1s_done, p1_sub, p1_exp, p1_ready, p1_turned, p1T_ready = (sem(n) for n in (
            "p1s_done", "p1_sub", "p1_exp", "p1_ready", "p1_turned", "p1T_ready"))
        lg_done, lg_sub, lg_exp, lg_ready, lg_turned, pT_made = (sem(n) for n in (
            "lg_done", "lg_sub", "lg_exp", "lg_ready", "lg_turned", "pT_made"))
        g1_done, g1_ready, g2_done, gT_ready, pbc_done, pbc_ready = (sem(n) for n in (
            "g1_done", "g1_ready", "g2_done", "gT_ready", "pbc_done", "pbc_ready"))
        mt_clear, ot_turned, passed = sem("mt_clear"), sem("ot_turned"), sem("passed")
        h1_done, h1_act, h1_ready, w2_done, rT_ready = (sem(n) for n in (
            "h1_done", "h1_act", "h1_ready", "w2_done", "rT_ready"))
        h2_done, h2_ready, w22_done = sem("h2_done"), sem("h2_ready"), sem("w22_done")
        h3_done, h3_act, h3_ready, w32_done = sem("h3_done"), sem("h3_act"), sem("h3_ready"), sem("w32_done")
        v_done, v_ready, v2_clear = sem("v_done"), sem("v_ready"), sem("v2_clear")
        ring_ready, ring_read, hi_ready = sem("ring_ready"), sem("ring_read"), sem("hi_ready")
        st_ready, pt_ready, pv2_done, acc_read, mt_ready = (sem(n) for n in (
            "st_ready", "pt_ready", "pv2_done", "acc_read", "mt_ready"))
        qk3_done, qk3_ready, v3_done, v3_ready, v3_clear = (sem(n) for n in (
            "qk3_done", "qk3_ready", "v3_done", "v3_ready", "v3_clear"))
        wk_ready, ws_ready, ws_read, wp_exp, wp_turned, wpT_ready, wpv_done, wo_ready = (sem(n) for n in (
            "wk_ready", "ws_ready", "ws_read", "wp_exp", "wp_turned", "wpT_ready", "wpv_done", "wo_ready"))

        block = es.enter_context(nc.Block())

        def rows(a):
            return a.rearrange("(k p) n -> p k n", p=P)

        @block.sync
        def _(sp):
            sp.dma_start(ident[:, :], g["c_ident"]).then_inc(consts_ld, 16)
            sp.dma_start(head_mask[:, :], g["c_head_mask"]).then_inc(consts_ld, 16)
            sp.dma_start(ones_ctx[:, :], g["c_ones_ctx"]).then_inc(consts_ld, 16)
            sp.dma_start(ones_win[:, :, :], g["c_ones_win"]).then_inc(consts_ld, 16)
            sp.dma_start(s_sel[:, :, :, :], g["c_sel"]).then_inc(consts_ld, 16)
            sp.dma_start(k_aug[:, :], g["c_k_aug"]).then_inc(consts_ld, 16)
            sp.dma_start(sel3[:, :, :], g["c_sel3"]).then_inc(consts_ld, 16)
            r = 0
            for name in ("L0_xcond_bss_q", "L0_xcond_bss_kv", "L2_xcond_b_mod", "L3_xcond_b_ada", "L2_xcond_b_proj",
                         "L2_xcond_b_mlp2", "L3_xcond_b_so", "L3_xcond_b_co", "L3_xcond_b_m2", "L1_xcond_e_b1",
                         "L1_xcond_gate_b1", "L0_xcond_bq", "L0_xcond_bp", "L0_xcond_bkv", "L1_xcond_ln_gamma",
                         "L1_xcond_ln_beta", "L1_xcond_gate_b2", "L1_xcond_out_b", "L2_xcond_b_qkv", "L2_xcond_b_qc",
                         "L2_xcond_b_kvc", "L2_xcond_b_cproj", "L2_xcond_b_mlp1", "L3_xcond_b_qkv", "L3_xcond_b_q",
                         "L3_xcond_b_kv", "L3_xcond_b_m1", "cond_1024"):
                a = g[name]
                if len(a.shape) == 2:
                    a = a.rearrange("e n -> (e n)")
                n = a.shape[0] // P
                if name in ("L0_xcond_bkv", "L2_xcond_b_kvc", "L3_xcond_b_kv"):
                    n = KC
                if name in ("L2_xcond_b_qkv", "L3_xcond_b_qkv"):
                    n = 2 * KC
                sp.dma_start(s_rows[r:r + n, :], a[0:n * P].rearrange("(n p) -> n p", p=P)).then_inc(rows_ld, 16)
                r += n
            assert r == N_COL
            sp.dma_start(s_ctx[:, :], g["ctx_1024"].rearrange("b s d -> (b s) d")).then_inc(ctx_ld, 16)
            for tile, name, a, z in ((vb2, "L2_xcond_b_qkv", 2 * D, 3 * D), (vb3, "L3_xcond_b_qkv", 2 * D, 3 * D),
                                     (rb, "L1_xcond_router_b", 0, E)):
                sp.dma_start(tile[:, :], g[name][a:z].unsqueeze(0).broadcast_to([P, z - a])).then_inc(consts_ld, 16)
            for i, name in enumerate(("L0_xcond_bkv", "L2_xcond_b_kvc", "L3_xcond_b_kv")):
                sp.dma_start(s_vb[:, i, :], g[name][D:2 * D].unsqueeze(0).broadcast_to([P, D])).then_inc(consts_ld, 16)
            sp.dma_start(b2[:, :], g["L1_xcond_e_b2"]).then_inc(consts_ld, 16)
            for tile, name in ((s_ss_q, "L0_xcond_Wss_q"), (s_ss_kv, "L0_xcond_Wss_kv"), (s_mod, "L2_xcond_W_mod"),
                               (s_ada, "L3_xcond_w_ada")):
                sp.dma_start(tile[:, :, :], rows(g[name])).then_inc(s_mod_ld, 16)
            for tile, name in ((s_kv0, "L0_xcond_Wkv"), (s_kvc, "L2_xcond_W_kvc"), (s_kv3, "L3_xcond_w_kv")):
                sp.dma_start(tile[:, :, :], rows(g[name])).then_inc(s_kv_ld, 16)
            for tile, name in ((s_q1, "L1_xcond_Wq"), (s_k1, "L1_xcond_Wk"), (s_v1, "L1_xcond_Wv")):
                sp.dma_start(tile[:, :, :], rows(g[name])).then_inc(s_l1_ld, 16)
            for e in range(E):
                sp.dma_start(s_ev[:, e, :, :], rows(g["L1_xcond_e_w1"][e, D:2 * D, :])).then_inc(s_l1_ld, 16)
                sp.dma_start(s_an[:, e, :, :], rows(g["L1_xcond_e_w1"][e, 2 * D:3 * D, :])).then_inc(s_l1_ld, 16)
            for tile, name, part in ((s_gev, "L1_xcond_gate_w1", 1), (s_gan, "L1_xcond_gate_w1", 2),
                                     (s_rev, "L1_xcond_router_W", 1), (s_ran, "L1_xcond_router_W", 2)):
                sp.dma_start(tile[:, :, :], rows(g[name][part * D:(part + 1) * D, :])).then_inc(s_l1_ld, 16)

            def load_ra():
                for tile, name in ((wq0, "L0_xcond_Wq"), (wp0, "L0_xcond_Wp"), (wg2, "L1_xcond_gate_w2"),
                                   (wout, "L1_xcond_out_w")):
                    sp.dma_start(tile[:, :, :], rows(g[name])).then_inc(ra_ld, 16)
                sp.dma_start(wqk2[:, :, :], rows(g["L2_xcond_W_qkv"][:, 0:2 * D])).then_inc(ra_ld, 16)
                sp.dma_start(wv2[:, :, :], rows(g["L2_xcond_W_qkv"][:, 2 * D:3 * D])).then_inc(ra_ld, 16)
                for e in range(E):
                    sp.dma_start(w1[:, e, :, :], rows(g["L1_xcond_e_w1"][e, 0:D, :])).then_inc(ra_ld, 16)
                sp.dma_start(wg1[:, :, :], rows(g["L1_xcond_gate_w1"][0:D, :])).then_inc(ra_ld, 16)
                sp.dma_start(wr[:, :, :], rows(g["L1_xcond_router_W"][0:D, :])).then_inc(ra_ld, 16)
                sp.dma_start(w2[:, :, :], g["L1_xcond_e_w2"].rearrange("e (k p) n -> p (e k) n", p=P)).then_inc(ra_ld, 16)

            load_ra()
            sp.wait_ge(set_pe, 8)
            sp.wait_ge(set_act, 4)
            sp.wait_ge(set_dve, 7)
            for tile, name in ((wproj, "L2_xcond_W_proj"), (wqc, "L2_xcond_W_qc"), (wcp, "L2_xcond_W_cproj"),
                               (wm1, "L2_xcond_W_mlp1"), (wm2, "L2_xcond_W_mlp2"), (wqkv3, "L3_xcond_w_qkv"),
                               (wso, "L3_xcond_w_so"), (wq3, "L3_xcond_w_q"), (wco, "L3_xcond_w_co")):
                sp.dma_start(tile[:, :, :], rows(g[name])).then_inc(rc1_ld, 16)

            sp.sem_inc(out_stored, 1)
            with sp.Fori(0, B) as b:
                xb = g["x"][b, :, :]
                sp.wait_ge(out_stored, b * 64 + 1)
                sp.dma_start(x[:, 0:TB, :], xb[SHIFT:SHIFT + BLK, :].rearrange("(t p) d -> p t d", p=P)).then_inc(x_ld[0], 16)
                sp.dma_start(x[:, TB:T - 1, :], xb[SHIFT + BLK:L - SHIFT, :].rearrange("(t p) d -> p t d", p=P)).then_inc(x_ld[1], 16)
                sp.dma_start(x[0:SHIFT, T - 1, :], xb[L - SHIFT:L, :]).then_inc(x_ld[1], 16)
                sp.dma_start(x[SHIFT:P, T - 1, :], xb[0:SHIFT, :]).then_inc(x_ld[1], 16)
                sp.wait_ge(ring_read, b * N_RING + N_RING)
                sp.wait_ge(pv2_done, b * 32 + 32)
                sp.dma_start(w3a[:, :, :], rows(g["L3_xcond_w_m1"])).then_inc(rc2_ld, 16)
                sp.dma_start(w3b[:, :, :], rows(g["L3_xcond_w_m2"])).then_inc(rc2_ld, 16)
                sp.wait_ge(wo_ready, b * N_UNIT + N_UNIT)
                load_ra()
                ob = out[b, :, :]
                sp.wait_ge(x_final, b * NB + 1)
                sp.dma_start(ob[SHIFT:SHIFT + BLK, :].rearrange("(t p) d -> p t d", p=P), x[:, 0:TB, :]).then_inc(out_stored, 16)
                sp.wait_ge(x_final, b * NB + 2)
                sp.dma_start(ob[SHIFT + BLK:L - SHIFT, :].rearrange("(t p) d -> p t d", p=P), x[:, TB:T - 1, :]).then_inc(out_stored, 16)
                sp.dma_start(ob[L - SHIFT:L, :], x[0:SHIFT, T - 1, :]).then_inc(out_stored, 16)
                sp.dma_start(ob[0:SHIFT, :], x[SHIFT:P, T - 1, :]).then_inc(out_stored, 16)
            sp.wait_ge(out_stored, B * 64 + 1)
            sp.wait_ge(ra_ld, (B + 1) * N_RA)

        @block.tensor
        def _(pe):
            def linear(bank, w, m, src):
                for c in range(KC):
                    ins = pe.matmul(ps[:, bank, :], w[:, c, m * P:(m + 1) * P], src[:, c, :],
                                    start=c == 0, stop=c == KC - 1)
                return ins

            def turn_block(k, src):
                for c in range(KC):
                    for t in range(TB):
                        ins = pe.transpose(ps[:, 4 * k + c, t * P:(t + 1) * P], src[:, TB * k + t, c * P:(c + 1) * P], ident[:, :])
                return ins

            pe.wait_ge(consts_ld, 14 * 16)
            pe.wait_ge(rows_ld, 28 * 16)
            pe.transpose(ps[:, 0, 0:N_COL], s_rows[0:N_COL, :], ident[0:N_COL, 0:N_COL]).then_inc(set_pe, 1)
            pe.wait_ge(set_dve, 1)
            for v in range(3):
                for c in range(KC):
                    ins = pe.transpose(ps[:, 1 + v, c * P:(c + 1) * P], s_xh[:, v, c * P:(c + 1) * P], ident[:, :])
            ins.then_inc(set_pe, 1)
            pe.wait_ge(s_mod_ld, 4 * 16)
            pe.wait_ge(set_act, 1)
            silu = s_silu[:, :].rearrange("p (b c) -> p c b", c=KC)
            n = 0
            for w, chunks in ((s_ss_q, 4), (s_ss_kv, 4), (s_mod, 12), (s_ada, 18)):
                for m in range(chunks):
                    for c in range(KC):
                        ins = pe.matmul(ps[:, 4, n * B:(n + 1) * B], w[:, c, m * P:(m + 1) * P], silu[:, c, :],
                                        start=c == 0, stop=c == KC - 1)
                    n += 1
            ins.then_inc(set_pe, 1)
            pe.wait_ge(s_l1_ld, 13 * 16)
            pe.wait_ge(set_act, 2)
            cond = colT[:, C_COND:C_COND + B * KC].rearrange("p (b c) -> p c b", c=KC)
            for m in range(MC + KC):
                for c in range(KC):
                    w = s_an[:, m // 4, c, m % 4 * P:(m % 4 + 1) * P] if m < MC else s_gan[:, c, (m - MC) * P:(m - MC + 1) * P]
                    ins = pe.matmul(ps[:, 5, m * B:(m + 1) * B], w, cond[:, c, :], start=c == 0, stop=c == KC - 1)
            for b in range(B):
                for c in range(KC):
                    ins = pe.matmul(ps[:, 5, 64 + b * 4:64 + b * 4 + E], s_crep[:, c, b, :], s_ran[:, c, :], start=c == 0, stop=c == KC - 1)
            ins.then_inc(set_pe, 1)
            for i in range(KC):
                for j in range(KC):
                    ins = pe.transpose(ps[:, 6, (j * KC + i) * P:(j * KC + i + 1) * P], s_q1[:, i, j * P:(j + 1) * P], ident[:, :])
            ins.then_inc(set_pe, 1)
            pe.wait_ge(s_kv_ld, 3 * 16)
            pe.wait_ge(set_dve, 3)
            pe.wait_ge(set_act, 3)

            def key(bank, slot, w, m, v):
                for c in range(KC):
                    ins = pe.matmul(ps[:, bank, slot * P:(slot + 1) * P], w[:, c, m * P:(m + 1) * P], s_ctxT[:, v, c, :, 0, :],
                                    start=c == 0, stop=c == KC - 1)
                return ins
            for m in range(KC):
                key(0, m, s_kv0, m, 0)
                key(0, KC + m, s_kvc, m, 1)
                key(1, m, s_kv3, m, 2)
                key(1, KC + m, s_k1, m, 2)
                ins = key(2, m, s_v1, m, 2)
            ins.then_inc(set_pe, 1)
            pe.wait_ge(set_dve, 4)
            for i, (bank, w) in enumerate(((3, s_kv0), (6, s_kvc), (7, s_kv3))):
                for b in range(B):
                    for c in range(KC):
                        ins = pe.matmul(ps[:, bank, b * D:(b + 1) * D], s_ctxT[:, i, c, b, :, :].rearrange("p a s -> p (a s)"),
                                        w[:, c, D:2 * D], start=c == 0, stop=c == KC - 1)
            ins.then_inc(set_pe, 1)
            pe.wait_ge(set_dve, 5)
            for i in range(KC):
                for j in range(KC):
                    ins = pe.matmul(ps[:, 0, i * P:(i + 1) * P], s_wqT[:, j, i * P:(i + 1) * P], s_k1T[:, j, :], start=j == 0, stop=j == KC - 1)
            for b in range(B):
                for c in range(KC):
                    lhsT = s_vT[:, c, b * S:(b + 1) * S]
                    st_, sp_ = c == 0, c == KC - 1
                    pe.matmul(ps[0:S, 0, D + b * 4:D + b * 4 + E], lhsT, s_rev[:, c, :], start=st_, stop=sp_)
            for b in range(B):
                for c in range(KC):
                    lhsT = s_vT[:, c, b * S:(b + 1) * S]
                    pe.matmul(ps[0:S, 1, b * D:(b + 1) * D], lhsT, s_gev[:, c, :], start=c == 0, stop=c == KC - 1)
            pe.wait_ge(set_dve, 6)
            for b in range(B):
                for e in range(E):
                    for c in range(KC):
                        lhsT = s_vT[:, c, b * S:(b + 1) * S]
                        ins = pe.matmul(ps[0:S, 2 + b * E + e, :], lhsT, s_ev[:, e, c, :], start=c == 0, stop=c == KC - 1)
            ins.then_inc(set_pe, 1)

            pe.wait_ge(set_dve, 7)
            pe.wait_ge(rc1_ld, 9 * 16)
            with pe.Fori(0, B) as b:
                def ln(i, k):
                    pe.wait_ge(xhat_ready, b * 2 * N_LN + 2 * i + k + 1)
                    turn_block(k, xhat).then_inc(ln_turned, 1)

                def query(i, k, ln_i, w):
                    pe.wait_ge(hT_ready, b * (2 * N_LN + 2) + ln_i + k + 1)
                    linear(4 * k + 2, w, 0, hT[:, k])
                    linear(4 * k + 3, w, 1, hT[:, k]).then_inc(q_done, 1)

                def residual(i, k, turn, w=None, o_wait=None, src=oT):
                    if not turn:
                        pe.wait_ge(*o_wait)
                        linear(4 * k + 2, w, 0, src[:, k])
                        linear(4 * k + 3, w, 1, src[:, k]).then_inc(y_done, 1)
                    else:
                        pe.wait_ge(yT_ready, b * 2 * N_RES + 2 * i + k + 1)
                        for t in range(TB):
                            for c in range(KC):
                                ins = pe.transpose(ps[:, 4 * k + t // 2, t % 2 * D + c * P:t % 2 * D + (c + 1) * P],
                                                   yT[:, k, c, t * P:(t + 1) * P], ident[:, :])
                        ins.then_inc(y_turned, 1)

                def context_attention(i):
                    u0 = b * N_CA * T + T * i

                    def scores(t):
                        if t % TB == 0:
                            pe.wait_ge(qT_ready, b * 2 * N_Q + 2 * i + t // TB + 1)
                        if t == 0:
                            pe.wait_ge(kblk_ready, b * N_CA + i + 1)
                        if t >= 2:
                            pe.wait_ge(s_read, u0 + t - 1)
                        for c in range(KC):
                            ins = pe.matmul(ps[:, 2 * (t % 2) + c, :], qT[:, t // TB, c, t % TB * P:(t % TB + 1) * P],
                                            kblk[:, c, :, :].rearrange("p h s -> p (h s)"), start=True, stop=True)
                        ins.then_inc(s_ready, 1)

                    def turn(t):
                        pe.wait_ge(p_exp, u0 + t + 1)
                        if t == 0:
                            pe.wait_ge(qT_ready, b * 2 * N_Q + 2 * i + 2)
                        elif t % TB:
                            pe.wait_ge(pT_ready, u0 + t)
                        else:
                            pe.wait_ge(oT_ready, b * 2 * N_CA + 2 * i + t // TB)
                        for j in range(HC):
                            ins = pe.transpose(ps[:, 4 + j // 4, j % 4 * P:(j % 4 + 1) * P], prob[:, t % 2, j * P:(j + 1) * P], ident[:, :])
                        ins.then_inc(p_turned, 1)

                    def values(k):
                        pe.wait_ge(pT_ready, u0 + TB * k + TB)
                        if k:
                            pe.wait_ge(oT_ready, b * 2 * N_CA + 2 * i + k)
                        for c in range(KC):
                            o_bank, sum_bank = ((6, 7), (4, 5))[c]
                            for j in range(4):
                                pe.matmul(ps[32 * j:32 * j + 32, o_bank, :], v_ctx[:, i, 4 * c + j, :], probT[:, 4 * c + j, :], start=True, stop=True)
                            for j in range(4):
                                ins = pe.matmul(ps[32 * j:32 * j + 32, sum_bank, :], ones_ctx[:, :], probT[:, 4 * c + j, :], start=True, stop=True)
                            ins.then_inc(pv_done, 1)

                    scores(0)
                    scores(1)
                    for t in range(T):
                        if t + 2 < T:
                            scores(t + 2)
                        turn(t)
                        if t == TB - 1:
                            values(0)
                    values(1)

                pe.wait_ge(ra_ld, b * N_RA + N_RA)
                pe.wait_ge(begun, b + 1)
                for k in range(NB):
                    ln(0, k)
                for k in range(NB):
                    query(0, k, 0, wq0)
                context_attention(0)
                for k in range(NB):
                    residual(0, k, False, wp0, (oT_ready, b * 2 * N_CA + k + 1))
                for k in range(NB):
                    residual(0, k, True)

                for k in range(NB):
                    ln(1, k)
                for k in range(NB):
                    pe.wait_ge(hT_ready, b * (2 * N_LN + 2) + 2 + k + 1)
                    for t in range(TB):
                        for c in range(KC):
                            ins = pe.matmul(ps[:, 4 * k + 2, t * S:(t + 1) * S], hT[:, k, c, t * P:(t + 1) * P], kw[:, c, :],
                                            start=c == 0, stop=c == KC - 1)
                    ins.then_inc(p1s_done, 1)
                for k in range(NB):
                    pe.wait_ge(p1_ready, b * NB + k + 1)
                    pe.sem_inc(passed, 1)
                    for t in range(TB):
                        ins = pe.transpose(ps[0:S, 4 * k, t * P:(t + 1) * P], p1[:, k, t, :], ident[:, :])
                    ins.then_inc(p1_turned, 1)
                for k in range(NB):
                    pe.wait_ge(p1T_ready, b * NB + k + 1)
                    for t in range(TB):
                        for c in range(KC):
                            pe.matmul(ps[:, 4 * k + 3, t * 4:t * 4 + E], hT[:, k, c, t * P:(t + 1) * P], wr[:, c, :], start=c == 0, stop=False)
                        ins = pe.matmul(ps[:, 4 * k + 3, t * 4:t * 4 + E], p1T[:, k, t * P:(t + 1) * P], vw[:, MC * P + D:MC * P + D + E], start=False, stop=True)
                    ins.then_inc(lg_done, 1)
                for k in range(NB):
                    for m in range(KC):
                        for c in range(KC):
                            pe.matmul(ps[:, 4 * k + 1 + m, :], wg1[:, c, m * P:(m + 1) * P], hT[:, k, c, :], start=c == 0, stop=False)
                        ins = pe.matmul(ps[:, 4 * k + 1 + m, :], vw[:, (MC + m) * P:(MC + m + 1) * P], p1T[:, k, :], start=False, stop=True)
                    ins.then_inc(g1_done, 1)
                for k in range(NB):
                    pe.wait_ge(lg_ready, b * NB + k + 1)
                    pe.sem_inc(passed, 1)
                    for t in range(TB):
                        ins = pe.transpose(ps[0:E, 4 * k + 3, t * P:(t + 1) * P], lg[:, k, t, :], ident[:, :])
                    ins.then_inc(lg_turned, 1)
                for k in range(NB):
                    pe.wait_ge(g1_ready, b * NB + k + 1)
                    for m in range(KC):
                        ins = linear(4 * k + 1 + m, wg2, m, g1[k])
                    ins.then_inc(g2_done, 1)
                for k in range(NB):
                    pe.wait_ge(pT_made, b * NB + k + 1)
                    pe.wait_ge(gT_ready, b * NB + k + 1)
                    for e in range(E):
                        ins = pe.matmul(ps[:, 4 * k + e, :], sel3[:, e, :], pT[:, k, :], start=True, stop=True)
                    ins.then_inc(pbc_done, 1)
                n0 = b * 2 * MC
                for k in range(NB):
                    pe.wait_ge(pbc_ready, b * NB + NB)
                    for m in range(KC):
                        pe.matmul(ps[:, 4 + 2 * k + m, :], b2[:, m * P:(m + 1) * P], pT[:, k, :], start=True, stop=False)
                    for m in range(MC + 2):
                        n = k * MC + m
                        if m < MC:
                            if n >= 4:
                                pe.wait_ge(h1_act, n0 + n - 3)
                            bank = n % 4
                            for c in range(KC):
                                pe.matmul(ps[:, bank, :], w1[:, m // 4, c, m % 4 * P:(m % 4 + 1) * P], hT[:, k, c, :], start=c == 0, stop=False)
                            pe.matmul(ps[:, bank, :], vw[:, m * P:(m + 1) * P], p1T[:, k, :], start=False, stop=True).then_inc(h1_done, 1)
                        if m >= 2:
                            pe.wait_ge(h1_ready, n0 + n - 1)
                            for j in range(KC):
                                ins = pe.matmul(ps[:, 4 + 2 * k + j, :], w2[:, m - 2, j * P:(j + 1) * P], ring[:, (n - 2) % 4, :],
                                                start=False, stop=m == MC + 1)
                            ins.then_inc(w2_done, 1)
                for k in range(NB):
                    pe.wait_ge(rT_ready, b * NB + k + 1)
                    for m in range(KC):
                        ins = linear((2, 4)[k] + m, wout, m, rT[k])
                    ins.then_inc(y_done, 1)
                for k in range(NB):
                    residual(1, k, True)

                for k in range(NB):
                    ln(2, k)
                for k in range(NB):
                    pe.wait_ge(hT_ready, b * (2 * N_LN + 2) + 4 + k + 1)
                    for t in range(TB):
                        for c in range(KC):
                            ins = pe.matmul(ps[:, 4 * k + 2 + t // 2, t % 2 * D:(t % 2 + 1) * D], hT[:, k, c, t * P:(t + 1) * P],
                                            wv2[:, c, :], start=c == 0, stop=c == KC - 1)
                    ins.then_inc(v_done, 1)
                pe.wait_ge(v_ready, b * NB + NB)
                pe.wait_ge(v2_clear, b + 1)
                uses = [0]

                def take_bank():
                    n = uses[0]
                    uses[0] += 1
                    if n >= 2:
                        pe.wait_ge(ring_read, b * N_RING + n - 1)
                    return n % 2

                def queries_keys(c):
                    for qk in range(2):
                        for k in range(NB):
                            bank = take_bank()
                            linear(bank, wqk2, qk * KC + c, hT[:, k]).then_inc(ring_ready, 1)

                def spread(gr):
                    for p in (2 * gr, 2 * gr + 1):
                        for qk in range(2):
                            for half in range(2):
                                bank = take_bank()
                                for part in range(2):
                                    ins = pe.matmul(ps[:, bank, :], sel[:, p % 4, 2 * qk + part, :],
                                                    dense[2 * qk + part][:, half * 512:(half + 1) * 512], start=part == 0, stop=part == 1)
                                ins.then_inc(ring_ready, 1)

                def pair(gr, hh):
                    return (2 * gr + hh // 2) % 4, slice(64 * (hh % 2), 64 * (hh % 2) + 64)

                def query_scores(gr, u):
                    hh, t = u // T, u % T
                    p, r = pair(gr, hh)
                    for half in range(2):
                        bank = take_bank()
                        pe.matmul(ps[:, bank, :], qx[r, p, t * P:(t + 1) * P], kx[r, p, half * 512:(half + 1) * 512],
                                  start=True, stop=True).then_inc(ring_ready, 1)

                def turn_maxima(gr):
                    for p in range(2):
                        pe.wait_ge(mt_ready, b * 8 + 2 * gr + p + 1)
                        for half in range(2):
                            bank = take_bank()
                            for t in range(TB):
                                ins = pe.transpose(ps[:, bank, t * P:(t + 1) * P], mt[:, half * TB + t, :], ident[:, :])
                            ins.then_inc(ring_ready, 1)

                def key_scores(gr, u):
                    kc, hh = u // 4, u % 4
                    p, r = pair(gr, hh)
                    n = 32 * gr + u
                    if n >= 2:
                        pe.wait_ge(pt_ready, b * 128 + n - 1)
                    for half in range(2):
                        ins = pe.matmul(ps[:, 2 + 2 * (u % 2) + half, :], kx[r, p, kc * P:(kc + 1) * P], qx[r, p, half * 512:(half + 1) * 512],
                                        start=True, stop=True)
                    ins.then_inc(st_ready, 1)

                def weigh_values(gr, kc):
                    pe.wait_ge(pt_ready, b * 128 + 32 * gr + 4 * kc + 4)
                    if kc == 0 and gr:
                        pe.wait_ge(acc_read, b * 4 + gr)
                    for half in range(2):
                        for hh in range(4):
                            ins = pe.matmul(ps[32 * hh:32 * hh + 32, 6 + half, :], v2[:, kc, VS * (4 * gr + hh):VS * (4 * gr + hh) + 32],
                                            pt[:, (4 * kc + hh) % 8, half * 512:(half + 1) * 512], start=kc == 0, stop=kc == T - 1)
                    ins.then_inc(pv2_done, 1)

                def finish(gr):
                    pe.wait_ge(acc_read, b * 4 + gr + 1)
                    for half in range(2):
                        bank = take_bank()
                        for t in range(TB):
                            ins = pe.transpose(ps[:, bank, t * P:(t + 1) * P], accS[:, (half * TB + t) * P:(half * TB + t + 1) * P], ident[:, :])
                        ins.then_inc(ring_ready, 1)

                queries_keys(0)
                pe.wait_ge(ring_read, b * N_RING + 4)
                spread(0)
                pe.wait_ge(ring_read, b * N_RING + 12)
                for u in range(32):
                    query_scores(0, u)
                turn_maxima(0)
                for gr in range(4):
                    if gr == 1:
                        queries_keys(1)
                    if gr < 3:
                        pe.wait_ge(ring_read, b * N_RING + uses[0])
                        spread(gr + 1)
                    pe.wait_ge(ring_read, b * N_RING + uses[0])
                    for u in range(32):
                        key_scores(gr, u)
                        if gr < 3:
                            query_scores(gr + 1, u)
                        if u % 4 == 3 and u > 4:
                            weigh_values(gr, u // 4 - 1)
                    weigh_values(gr, T - 1)
                    if gr < 3:
                        turn_maxima(gr + 1)
                    finish(gr)
                assert uses[0] == N_RING

                for k in range(NB):
                    pe.wait_ge(ring_read, b * N_RING + N_RING)
                    turn_block(k, xhat).then_inc(ot_turned, 1)
                for k in range(NB):
                    residual(2, k, False, wproj, (hT_ready, b * (2 * N_LN + 2) + 6 + k + 1), hT)
                for k in range(NB):
                    residual(2, k, True)

                for k in range(NB):
                    ln(3, k)
                for k in range(NB):
                    query(1, k, 8, wqc)
                context_attention(1)
                for k in range(NB):
                    residual(3, k, False, wcp, (oT_ready, b * 2 * N_CA + 2 + k + 1))
                for k in range(NB):
                    residual(3, k, True)

                for k in range(NB):
                    ln(4, k)
                n0 = b * 2 * NC_HID
                for k in range(NB):
                    pe.wait_ge(hT_ready, b * (2 * N_LN + 2) + 10 + k + 1)
                    if k == 0:
                        pe.wait_ge(hT_ready, b * (2 * N_LN + 2) + 10 + 2)
                    for m in range(NC_HID + 2):
                        n = k * NC_HID + m
                        if m < NC_HID:
                            if n >= 4:
                                pe.wait_ge(h2_ready, n0 + n - 3)
                            linear(n % 4, wm1, m, hT[:, k]).then_inc(h2_done, 1)
                        if m >= 2:
                            pe.wait_ge(h2_ready, n0 + n - 1)
                            for j in range(KC):
                                ins = pe.matmul(ps[:, 4 + 2 * k + j, :], wm2[:, m - 2, j * P:(j + 1) * P], ring[:, (n - 2) % 4, :],
                                                start=m == 2, stop=m == NC_HID + 1)
                            ins.then_inc(w22_done, 1)
                for k in range(NB):
                    residual(4, k, True)

                for k in range(NB):
                    ln(5, k)
                for k in range(NB):
                    pe.wait_ge(hT_ready, b * (2 * N_LN + 2) + 12 + k + 1)
                    for m in range(2 * KC):
                        ins = linear(4 * k + m, wqkv3, m, hT[:, k])
                    ins.then_inc(qk3_done, 1)
                for k in range(NB):
                    pe.wait_ge(qk3_ready, b * NB + k + 1)
                    for t in range(TB):
                        for c in range(KC):
                            ins = pe.matmul(ps[:, 4 * k + t // 2, t % 2 * D:(t % 2 + 1) * D], hT[:, k, c, t * P:(t + 1) * P],
                                            wqkv3[:, c, 2 * D:3 * D], start=c == 0, stop=c == KC - 1)
                    ins.then_inc(v3_done, 1)
                u0 = b * N_UNIT

                def window_scores(u):
                    t, c = u // KC, u % KC
                    pe.wait_ge(wk_ready, u0 + u + 1)
                    if u == 0:
                        pe.wait_ge(v3_ready, b * NB + NB)
                        pe.wait_ge(v3_clear, b + 1)
                    if u >= 2:
                        pe.wait_ge(ws_read, u0 + u - 1)
                    for half in range(2):
                        ins = pe.matmul(ps[:, 2 * (u % 2) + half, :], qT[:, t // TB, c, t % TB * P:(t % TB + 1) * P],
                                        wkblk[:, u % 2, 4 * half:4 * half + 4, :].rearrange("p h s -> p (h s)"), start=True, stop=True)
                    ins.then_inc(ws_ready, 1)

                def window_turn(u):
                    pe.wait_ge(wp_exp, u0 + u + 1)
                    if u:
                        pe.wait_ge(wpT_ready, u0 + u)
                    for j in range(HC):
                        ins = pe.transpose(ps[:, 4 + j // 4, j % 4 * P:(j % 4 + 1) * P], prob[:, u % 2, j * P:(j + 1) * P], ident[:, :])
                    ins.then_inc(wp_turned, 1)

                def window_values(u):
                    t, c = u // KC, u % KC
                    pe.wait_ge(wpT_ready, u0 + u + 1)
                    if u >= 2:
                        pe.wait_ge(wo_ready, u0 + u - 1)
                    for part in range(2):
                        for odd in range(2):
                            for j in range(4):
                                h = 2 * j + odd
                                lhsT = v3[:, t, HC * c + h, :] if part == 0 else ones_win[:, odd, :]
                                ins = pe.matmul(ps[32 * j:32 * j + 32, 6 + u % 2, part * P:(part + 1) * P], lhsT, wprobT[:, u % 2, h, :],
                                                start=odd == 0, stop=odd == 1)
                    ins.then_inc(wpv_done, 1)

                window_scores(0)
                window_scores(1)
                window_turn(0)
                for u in range(N_UNIT):
                    if u + 2 < N_UNIT:
                        window_scores(u + 2)
                    window_values(u)
                    if u + 1 < N_UNIT:
                        window_turn(u + 1)
                for k in range(NB):
                    residual(5, k, False, wso, (wo_ready, u0 + N_UNIT))
                for k in range(NB):
                    residual(5, k, True)

                for k in range(NB):
                    ln(6, k)
                for k in range(NB):
                    query(2, k, 14, wq3)
                context_attention(2)
                for k in range(NB):
                    residual(6, k, False, wco, (oT_ready, b * 2 * N_CA + 4 + k + 1))
                for k in range(NB):
                    residual(6, k, True)

                for k in range(NB):
                    ln(7, k)
                pe.wait_ge(rc2_ld, b * 32 + 32)
                n0 = b * 2 * NC_HID
                for k in range(NB):
                    pe.wait_ge(hT_ready, b * (2 * N_LN + 2) + 16 + k + 1)
                    if k == 0:
                        pe.wait_ge(hT_ready, b * (2 * N_LN + 2) + 16 + 2)
                    for m in range(NC_HID + 1):
                        n = k * NC_HID + m
                        if m < NC_HID:
                            if n >= 2:
                                pe.wait_ge(h3_ready, n0 + n - 1)
                            linear(2 * (n % 2), w3a, m, hT[:, k])
                            linear(2 * (n % 2) + 1, w3a, NC_HID + m, hT[:, k]).then_inc(h3_done, 1)
                        if m >= 1:
                            pe.wait_ge(h3_ready, n0 + n)
                            for j in range(KC):
                                ins = pe.matmul(ps[:, 4 + 2 * k + j, :], w3b[:, m - 1, j * P:(j + 1) * P], ring[:, (n - 1) % 4, :],
                                                start=m == 1, stop=m == NC_HID)
                            ins.then_inc(w32_done, 1)
                for k in range(NB):
                    residual(7, k, True)

        @block.scalar
        def _(act):
            def affine(dst, src, scale, bias):
                return act.activation(dst, src, ACT.Identity, bias=bias, scale=scale)

            act.wait_ge(set_dve, 2)
            act.activation(s_silu[:, :], colT[:, C_COND:C_COND + B * KC], ACT.Silu).then_inc(set_act, 1)
            for bb in range(B):
                for c in range(KC):
                    col = C_COND + bb * KC + c
                    ins = act.activation(s_crep[:, c, bb, :], colT[:, col:col + 1].broadcast_to([P, P]), ACT.Copy)
            ins.then_inc(set_act, 1)
            act.wait_ge(set_pe, 2)
            for v in (1, 2):
                for c in range(KC):
                    for dup in range(2):
                        ins = act.activation(s_ctxT[:, v, c, :, dup, :], ps[:, 1 + v, c * P:(c + 1) * P].rearrange("p (b s) -> p b s", b=B), ACT.Copy)
            ins.then_inc(set_act, 1)
            act.wait_ge(set_pe, 8)
            for bb in range(B):
                for e in range(E):
                    act.activation(vw2[:, bb, e * RH:(e + 1) * RH], ps[0:S, 2 + bb * E + e, :], ACT.Copy)
                act.activation(vw2[:, bb, MC * P:MC * P + D], ps[0:S, 1, bb * D:(bb + 1) * D], ACT.Copy)
            act.wait_ge(set_dve, 7)
            for bb in range(B):
                ins = act.activation(vw2[:, bb, MC * P + D:MC * P + D + E], ps[0:S, 0, D + bb * 4:D + bb * 4 + E], ACT.Copy)
            ins.then_inc(set_act, 1)

            with act.Fori(0, B) as b:
                act.wait_ge(begun, b + 1)

                def ln(i, k, cols):
                    act.wait_ge(ln_turned, b * 2 * N_LN + 2 * i + k + 1)
                    for c in range(KC):
                        if cols is None:
                            ins = act.activation(hT[:, k, c, :], ps[:, 4 * k + c, :], ACT.Copy)
                        else:
                            table, scale, bias = cols
                            ins = affine(hT[:, k, c, :], ps[:, 4 * k + c, :], table[:, scale + c:scale + c + 1], table[:, bias + c:bias + c + 1])
                    ins.then_inc(hT_ready, 1)

                def query(i, k, col):
                    act.wait_ge(q_done, b * 2 * N_Q + 2 * i + k + 1)
                    for c in range(KC):
                        ins = affine(qT[:, k, c, :], ps[:, 4 * k + 2 + c, :], 1.0, colT[:, col + c:col + c + 1])
                    ins.then_inc(qT_ready, 1)

                def residual(k, bank, scale, bias):
                    for c in range(KC):
                        ins = affine(yT[:, k, c, :], ps[:, bank + c, :], 1.0 if scale is None else mod[:, scale + c:scale + c + 1],
                                     bias[:, c:c + 1])
                    ins.then_inc(yT_ready, 1)

                def context_attention(i):
                    u0 = b * N_CA * T + T * i

                    def exp(t):
                        act.wait_ge(s_read, u0 + t + 1)
                        act.activation(prob[:, t % 2, :], prob[:, t % 2, :], ACT.Exp, scale=QK_SCALE).then_inc(top_exp if i == 2 else p_exp, 1)

                    def copy(t):
                        act.wait_ge(p_turned, u0 + t + 1)
                        if t == TB:
                            act.wait_ge(pv_done, b * 4 * N_CA + 4 * i + 2)
                        act.activation(probT[:, :, t % TB * P:(t % TB + 1) * P], ps[:, 4:6, :].rearrange("p a (j q) -> p (a j) q", q=P),
                                       ACT.Copy).then_inc(pT_ready, 1)
                    exp(0)
                    for t in range(T):
                        if t + 1 < T:
                            exp(t + 1)
                        copy(t)

                for k in range(NB):
                    ln(0, k, (mod, M_SC_Q, M_SH_Q))
                for k in range(NB):
                    query(0, k, C_BQ0)
                context_attention(0)
                for k in range(NB):
                    act.wait_ge(y_done, b * 12 + k + 1)
                    residual(k, 4 * k + 2, None, colT[:, C_BP0:C_BP0 + KC])

                for k in range(NB):
                    ln(1, k, (colT, C_GAMMA, C_BETA))
                for k in range(NB):
                    act.wait_ge(p1_sub, b * NB + k + 1)
                    act.activation(p1[:, k, :, :], p1[:, k, :, :], ACT.Exp, scale=L1_SCALE).then_inc(p1_exp, 1)
                for k in range(NB):
                    act.wait_ge(p1_turned, b * NB + k + 1)
                    act.activation(p1T[:, k, :], ps[0:S, 4 * k, :], ACT.Copy).then_inc(p1T_ready, 1)
                for k in range(NB):
                    act.wait_ge(lg_sub, b * NB + k + 1)
                    act.activation(lg[:, k, :, :], lg[:, k, :, :], ACT.Exp).then_inc(lg_exp, 1)
                for k in range(NB):
                    act.wait_ge(g1_done, b * NB + k + 1)
                    for m in range(KC):
                        ins = act.activation(g1[k][:, m, :], ps[:, 4 * k + 1 + m, :], ACT.Silu, bias=mod[:, M_HB + MC + m:M_HB + MC + m + 1])
                    ins.then_inc(g1_ready, 1)
                for k in range(NB):
                    act.wait_ge(lg_turned, b * NB + k + 1)
                    act.activation(pT[:, k, :], ps[0:E, 4 * k + 3, :], ACT.Copy).then_inc(pT_made, 1)
                for k in range(NB):
                    act.wait_ge(g2_done, b * NB + k + 1)
                    for m in range(KC):
                        ins = act.activation(gT[:, k, m, :], ps[:, 4 * k + 1 + m, :], ACT.Sigmoid, bias=colT[:, C_GB2 + m:C_GB2 + m + 1])
                    ins.then_inc(gT_ready, 1)
                for k in range(NB):
                    act.wait_ge(pbc_done, b * NB + k + 1)
                    for e in range(E):
                        ins = act.activation(p_bc[:, k, e, :], ps[:, 4 * k + e, :], ACT.Copy)
                    ins.then_inc(pbc_ready, 1)
                n0 = b * NB * MC

                def routed(k):
                    act.wait_ge(w2_done, n0 + k * MC + MC)
                    for c in range(KC):
                        ins = act.activation(rT[k][:, c, :], ps[:, 4 + 2 * k + c, :], ACT.Copy)
                    ins.then_inc(rT_ready, 1)
                for n in range(NB * MC):
                    act.wait_ge(h1_done, n0 + n + 1)
                    if n >= 4:
                        act.wait_ge(w2_done, n0 + n - 3)
                    m = n % MC
                    act.activation(ring[:, n % 4, :], ps[:, n % 4, :], ACT.Silu, bias=mod[:, M_HB + m:M_HB + m + 1]).then_inc(h1_act, 1)
                    if n == MC + 1:
                        routed(0)
                routed(1)

                for k in range(NB):
                    ln(2, k, (mod, M_SC_A, M_SH_A))
                u0 = b * N_RING
                uses = [0]

                def high_parts(c):
                    for qk in range(2):
                        for k in range(NB):
                            act.wait_ge(ring_ready, u0 + uses[0] + 1)
                            col = (C_BQ2, C_BK2)[qk] + c
                            affine(dense[2 * qk][:, k * BLK:(k + 1) * BLK], ps[:, uses[0] % 2, :], 1.0, colT[:, col:col + 1]).then_inc(hi_ready, 1)
                            uses[0] += 1
                high_parts(0)
                uses[0] += 8 + 64 + 4
                for gr in range(4):
                    if gr == 1:
                        high_parts(1)
                    for u in range(32):
                        n = 32 * gr + u
                        act.wait_ge(st_ready, b * 128 + n + 1)
                        if u % 4 == 0 and n >= 8:
                            act.wait_ge(pv2_done, b * 32 + n // 4 - 1)
                        act.activation(pt[:, u % 8, :], ps[:, 2 + 2 * (u % 2):4 + 2 * (u % 2), :].rearrange("p a q -> p (a q)"),
                                       ACT.Exp, scale=QK_SCALE).then_inc(pt_ready, 1)
                    if gr < 3:
                        uses[0] += 8 + 64 + 4
                    act.wait_ge(pv2_done, b * 32 + 8 * gr + 8)
                    if gr:
                        act.wait_ge(ring_read, u0 + finished)
                    act.activation(accS[:, :], ps[:, 6:8, :].rearrange("p a q -> p (a q)"), ACT.Copy).then_inc(acc_read, 1)
                    uses[0] += 2
                    finished = uses[0]
                for k in range(NB):
                    act.wait_ge(ot_turned, b * NB + k + 1)
                    for c in range(KC):
                        ins = act.activation(hT[:, k, c, :], ps[:, 4 * k + c, :], ACT.Copy)
                    ins.then_inc(hT_ready, 1)
                for k in range(NB):
                    act.wait_ge(y_done, b * 12 + 4 + k + 1)
                    residual(k, 4 * k + 2, M_G_A, mod[:, M_BG:M_BG + KC])

                for k in range(NB):
                    ln(3, k, None)
                for k in range(NB):
                    query(1, k, C_BQC)
                context_attention(1)
                for k in range(NB):
                    act.wait_ge(y_done, b * 12 + 6 + k + 1)
                    residual(k, 4 * k + 2, None, colT[:, C_BCP:C_BCP + KC])

                for k in range(NB):
                    ln(4, k, (mod, M_SC_M, M_SH_M))
                n0 = b * NB * NC_HID

                def mlp_out(done, k, scale, bias):
                    act.wait_ge(done, n0 + k * NC_HID + NC_HID)
                    residual(k, 4 + 2 * k, scale, bias)
                for n in range(NB * NC_HID):
                    act.wait_ge(h2_done, n0 + n + 1)
                    if n >= 4:
                        act.wait_ge(w22_done, n0 + n - 3)
                    m = n % NC_HID
                    act.activation(ring[:, n % 4, :], ps[:, n % 4, :], ACT.Gelu_apprx_tanh, bias=colT[:, C_BM1 + m:C_BM1 + m + 1]).then_inc(h2_ready, 1)
                    if n == NC_HID + 1:
                        mlp_out(w22_done, 0, M_G_M, mod[:, M_BG + 2:M_BG + 2 + KC])
                mlp_out(w22_done, 1, M_G_M, mod[:, M_BG + 2:M_BG + 2 + KC])

                for k in range(NB):
                    ln(5, k, (mod, M3_SC_SA, M3_SH_SA))
                for k in range(NB):
                    act.wait_ge(qk3_done, b * NB + k + 1)
                    for m in range(KC):
                        affine(qT[:, k, m, :], ps[:, 4 * k + m, :], 1.0, colT[:, C_BQ3 + m:C_BQ3 + m + 1])
                    for m in range(KC):
                        ins = affine(kT3[:, k, m, :], ps[:, 4 * k + KC + m, :], 1.0, colT[:, C_BK3 + m:C_BK3 + m + 1])
                    ins.then_inc(qk3_ready, 1)
                u0 = b * N_UNIT

                def window_exp(u):
                    act.wait_ge(ws_read, u0 + u + 1)
                    act.activation(prob[:, u % 2, :], prob[:, u % 2, :], ACT.Exp, scale=QK_SCALE).then_inc(wp_exp, 1)

                def window_copy(u):
                    act.wait_ge(wp_turned, u0 + u + 1)
                    if u >= 2:
                        act.wait_ge(wpv_done, u0 + u - 1)
                    act.activation(wprobT[:, u % 2, :, :], ps[:, 4:6, :].rearrange("p a (j q) -> p (a j) q", q=P), ACT.Copy).then_inc(wpT_ready, 1)
                window_exp(0)
                window_exp(1)
                window_copy(0)
                for u in range(N_UNIT):
                    if u + 2 < N_UNIT:
                        window_exp(u + 2)
                    if u + 1 < N_UNIT:
                        window_copy(u + 1)
                for k in range(NB):
                    act.wait_ge(y_done, b * 12 + 8 + k + 1)
                    residual(k, 4 * k + 2, M3_G_SA, mod[:, M_BG + 4:M_BG + 4 + KC])

                for k in range(NB):
                    ln(6, k, (mod, M3_SC_CA, M3_SH_CA))
                for k in range(NB):
                    query(2, k, C_BQ3C)
                context_attention(2)
                for k in range(NB):
                    act.wait_ge(y_done, b * 12 + 10 + k + 1)
                    residual(k, 4 * k + 2, M3_G_CA, mod[:, M_BG + 6:M_BG + 6 + KC])

                for k in range(NB):
                    ln(7, k, (mod, M3_SC_ML, M3_SH_ML))
                for n in range(NB * NC_HID):
                    act.wait_ge(h3_done, n0 + n + 1)
                    if n >= 4:
                        act.wait_ge(w32_done, n0 + n - 3)
                    m = n % NC_HID
                    act.activation(ring[:, n % 4, :], ps[:, 2 * (n % 2), :], ACT.Silu, bias=colT[:, C_BM13 + m:C_BM13 + m + 1]).then_inc(h3_act, 1)
                    if n == NC_HID + 1:
                        mlp_out(w32_done, 0, M3_G_ML, mod[:, M_BG + 8:M_BG + 8 + KC])
                mlp_out(w32_done, 1, M3_G_ML, mod[:, M_BG + 8:M_BG + 8 + KC])

        @block.vector
        def _(dve):
            steps = [0]

            def link(ins):
                steps[0] += 1
                ins.then_inc(dve_step, 1)
                dve.wait_ge(dve_step, steps[0])

            dve.wait_ge(ctx_ld, 16)
            link(dve.bn_stats(s_st[:, 0:6], s_ctx[:, :]))
            link(dve.bn_aggr(s_st[:, 6:8], s_st[:, 0:6]))
            dve.tensor_scalar(s_st[:, 8:9], s_st[:, 7:8], EPS5, None, ALU.add)
            dve.tensor_scalar(s_st[:, 9:10], s_st[:, 7:8], EPS6, None, ALU.add).then_inc(ctx_var, 1)
            dve.wait_ge(ctx_rstd, 1)
            for v in range(2):
                dve.tensor_scalar(s_xh[:, v, :], s_ctx[:, :], s_st[:, 6:7], s_st[:, 10 + v:11 + v], ALU.subtract, ALU.mult)
            dve.tensor_copy(s_xh[:, 2, :], s_ctx[:, :]).then_inc(set_dve, 1)
            dve.wait_ge(set_pe, 1)
            dve.tensor_copy(colT[:, :], ps[:, 0, 0:N_COL]).then_inc(set_dve, 1)
            dve.wait_ge(consts_ld, 14 * 16)
            dve.tensor_copy(sel[:, :, :, :], s_sel[:, :, :, :])
            link(dve.memset(v_ctx2[:, :, :, :, :], 0.0))
            dve.wait_ge(set_dve, 2)
            dve.wait_ge(set_pe, 3)
            link(dve.tensor_tensor(mod2[:, :, 0:N_MOD], ps[:, 4, 0:N_MOD * B].rearrange("p (n b) -> p b n", b=B),
                                   colT[:, 0:N_MOD].unsqueeze(1).broadcast_to([P, B, N_MOD]), ALU.add))
            for m in SCALES:
                ins = dve.tensor_scalar(mod2[:, :, m:m + KC], mod2[:, :, m:m + KC], 1.0, None, ALU.add)
            for i, m in enumerate(GATED):
                o = M_BG + KC * i
                ins = dve.tensor_tensor(mod2[:, :, o:o + KC], mod2[:, :, m:m + KC],
                                        colT[:, o:o + KC].unsqueeze(1).broadcast_to([P, B, KC]), ALU.mult)
            link(ins)
            dve.wait_ge(set_pe, 2)
            for c in range(KC):
                for b in range(B):
                    for dup in range(2):
                        ins = dve.tensor_scalar(s_ctxT[:, 0, c, b, dup, :], ps[:, 1, c * P + b * S:c * P + (b + 1) * S],
                                                mod2[:, b, M_SC_KV + c:M_SC_KV + c + 1], mod2[:, b, M_SH_KV + c:M_SH_KV + c + 1], ALU.mult, ALU.add)
            ins.then_inc(set_dve, 1)
            dve.wait_ge(set_pe, 4)
            dve.tensor_tensor(mod2[:, :, M_HB:N_MC], ps[:, 5, 0:(N_MC - M_HB) * B].rearrange("p (n b) -> p b n", b=B),
                              colT[:, M_HB:N_MC].unsqueeze(1).broadcast_to([P, B, N_MC - M_HB]), ALU.add)
            for b in range(B):
                dve.tensor_tensor(rc2[:, b, :], ps[:, 5, 64 + 4 * b:64 + 4 * b + E], rb[:, :], ALU.add)
            dve.wait_ge(set_pe, 5)
            dve.tensor_copy(s_wqT[:, :, :].rearrange("p j i -> p (j i)"), ps[:, 6, :]).then_inc(set_dve, 1)
            dve.wait_ge(set_pe, 6)
            for m in range(KC):
                for i, (bank, slot, col) in enumerate(((0, m, C_BK0), (0, KC + m, C_BKC), (1, m, C_BK3C))):
                    dve.tensor_scalar(kT2[:, i, m, :, :], ps[:, bank, slot * P:(slot + 1) * P].rearrange("p (b s) -> p b s", b=B),
                                      colT[:, col + m:col + m + 1], None, ALU.add)
                dve.tensor_copy(s_k1T[:, m, :], ps[:, 1, (KC + m) * P:(KC + m + 1) * P])
                ins = dve.tensor_copy(s_vT[:, m, :], ps[:, 2, m * P:(m + 1) * P])
            ins.then_inc(set_dve, 1)
            dve.wait_ge(set_pe, 7)
            for i, bank in enumerate((3, 6, 7)):
                for b in range(B):
                    for odd in range(2):
                        r = slice(S * odd, S * odd + S)
                        ins = dve.tensor_tensor(v_ctx2[r, b, i, :, HD * odd:HD * odd + HD],
                                                ps[r, bank, b * D:(b + 1) * D].rearrange("p (j c) -> p j c", c=2 * HD)[:, :, HD * odd:HD * odd + HD],
                                                s_vb[r, i, :].rearrange("p (j c) -> p j c", c=2 * HD)[:, :, HD * odd:HD * odd + HD], ALU.add)
            ins.then_inc(set_dve, 1)
            dve.wait_ge(set_pe, 8)
            dve.tensor_copy(kw2[:, :, :, :].rearrange("p i b s -> p i (b s)"), ps[:, 0, 0:KC * P].rearrange("p (i n) -> p i n", i=KC)).then_inc(set_dve, 1)
            dve.wait_ge(set_dve, 7)
            dve.wait_ge(set_act, 4)
            dve.wait_ge(dve_step, steps[0])

            with dve.Fori(0, B) as b:
                dve.sem_clear(dve_step)
                steps[0] = 0
                dve.tensor_copy(mod[:, :], mod2[:, b, :])
                dve.tensor_copy(v_ctx[:, :, :, :], v_ctx2[:, b, :, :, :])
                dve.tensor_copy(kT[:, :, :, :], kT2[:, :, :, b, :])
                dve.tensor_copy(kw[:, :, :], kw2[:, :, b, :])
                dve.tensor_copy(rc[:, :], rc2[:, b, :])
                dve.tensor_copy(vw[:, :], vw2[:, b, :]).then_inc(begun, 1)
                dve.wait_ge(begun, b + 1)

                def statistics(i, k):
                    for t in range(TB):
                        ins = dve.bn_stats(st[:, k, t, :], x[:, TB * k + t, :])
                    link(ins)
                    for t in range(TB):
                        ins = dve.bn_aggr(mv[:, k, t, :], st[:, k, t, :])
                    link(ins)
                    dve.tensor_scalar(ve[:, k, :], mv[:, k, :, 1], EPS5 if i < 2 else EPS6, None, ALU.add).then_inc(ve_ready, 1)

                def normalise(i, k):
                    dve.wait_ge(rstd_ready, b * 2 * N_LN + 2 * i + k + 1)
                    for t in range(TB):
                        ins = dve.tensor_scalar(xhat[:, TB * k + t, :], x[:, TB * k + t, :], mv[:, k, t, 0:1], rstd[:, k, t:t + 1], ALU.subtract, ALU.mult)
                    ins.then_inc(xhat_ready, 1)

                def residual(i, k):
                    dve.wait_ge(y_turned, b * 2 * N_RES + 2 * i + k + 1)
                    return dve.tensor_tensor(x[:, TB * k:TB * (k + 1), :].rearrange("p t d -> p (t d)"),
                                             x[:, TB * k:TB * (k + 1), :].rearrange("p t d -> p (t d)"),
                                             ps[:, 4 * k:4 * k + 2, :].rearrange("p a n -> p (a n)"), ALU.add)

                def residual_norm(i):
                    link(residual(i, 0))
                    statistics(i + 1, 0)
                    link(residual(i, 1))
                    normalise(i + 1, 0)
                    statistics(i + 1, 1)
                    normalise(i + 1, 1)

                def build_keys(i):
                    for c in range(KC):
                        ins = dve.tensor_tensor(kblk[:, c, :, :], kT[:, i, c, :].unsqueeze(1).broadcast_to([P, HC, S]),
                                                head_mask[:, :].unsqueeze(2).broadcast_to([P, HC, S]), ALU.mult)
                    ins.then_inc(kblk_ready, 1)

                def context_attention(i):
                    u0 = b * N_CA * T + T * i

                    def heads(t):
                        return ps[:, 2 * (t % 2):2 * (t % 2) + 2, :].rearrange("p a (h s) -> p (a h) s", s=S)

                    def take_top(t):
                        tk = taken[:, t % 2, :].rearrange("p (h s) -> p h s", s=S)
                        sc = heads(t)
                        for h in range(H):
                            ins = dve.max(m8[:, t % 2, h, 0:8], sc[:, h, :])
                        link(ins)
                        for h in range(H):
                            ins = dve.match_replace(tk[:, h, :], m8[:, t % 2, h, 0:8], sc[:, h, :], LOWEST)
                        link(ins)
                        for h in range(H):
                            ins = dve.max(m8[:, t % 2, h, 8:16], tk[:, h, :])
                        link(ins)
                        for h in range(H):
                            ins = dve.match_replace(tk[:, h, :], m8[:, t % 2, h, 8:16], tk[:, h, :], LOWEST)
                        link(ins)

                    def centre(t):
                        dve.wait_ge(s_ready, u0 + t + 1)
                        if i == 2:
                            dve.sem_inc(passed, 1)
                            take_top(t)
                            top = m8[:, t % 2, :, 0]
                        else:
                            link(dve.tensor_reduce(mx[:, t % 2, :], heads(t), X, ALU.max))
                            top = mx[:, t % 2, :]
                        if t >= 2:
                            dve.wait_ge(p_turned, u0 + t - 1)
                        dve.tensor_tensor(prob[:, t % 2, :].rearrange("p (h s) -> p h s", s=S), heads(t),
                                          top.unsqueeze(2).broadcast_to([P, H, S]), ALU.subtract).then_inc(s_read, 1)

                    def mask(t):
                        dve.wait_ge(top_exp, b * T + t + 1)
                        dve.scalar_tensor_tensor(prob[:, t % 2, :], taken[:, t % 2, :], LOWEST, prob[:, t % 2, :], ALU.is_equal, ALU.mult).then_inc(p_exp, 1)

                    def divide(k):
                        for c in range(KC):
                            o_bank, sum_bank = ((6, 7), (4, 5))[c]
                            dve.wait_ge(pv_done, b * 4 * N_CA + 4 * i + 2 * k + c + 1)
                            link(dve.reciprocal(rs[:, :], ps[:, sum_bank, :]))
                            ins = dve.tensor_tensor(oT[:, k, c, :], ps[:, o_bank, :], rs[:, :], ALU.mult)
                            if c == 0:
                                link(ins)
                        ins.then_inc(oT_ready, 1)

                    centre(0)
                    for t in range(1, T):
                        if t == TB + 2:
                            divide(0)
                        centre(t)
                        if i == 2:
                            mask(t - 1)
                    if i == 2:
                        mask(T - 1)
                    divide(1)

                dve.wait_ge(x_ld[0], b * 16 + 16)
                statistics(0, 0)
                dve.wait_ge(x_ld[1], b * 48 + 48)
                normalise(0, 0)
                statistics(0, 1)
                normalise(0, 1)
                build_keys(0)
                context_attention(0)
                residual_norm(0)

                for k in range(NB):
                    dve.wait_ge(p1s_done, b * NB + k + 1)
                    sc = ps[:, 4 * k + 2, 0:TB * S].rearrange("p (t s) -> p t s", s=S)
                    link(dve.tensor_reduce(r1m[:, k, :], sc, X, ALU.max))
                    dve.tensor_tensor(p1[:, k, :, :], sc, r1m[:, k, :].unsqueeze(2).broadcast_to([P, TB, S]), ALU.subtract).then_inc(p1_sub, 1)
                for k in range(NB):
                    dve.wait_ge(p1_exp, b * NB + k + 1)
                    link(dve.tensor_reduce(r1m[:, k, :], p1[:, k, :, :], X, ALU.add))
                    link(dve.reciprocal(r1m[:, k, :], r1m[:, k, :]))
                    dve.tensor_tensor(p1[:, k, :, :], p1[:, k, :, :], r1m[:, k, :].unsqueeze(2).broadcast_to([P, TB, S]), ALU.mult).then_inc(p1_ready, 1)
                for k in range(NB):
                    dve.wait_ge(lg_done, b * NB + k + 1)
                    link(dve.tensor_tensor(lg[:, k, :, :], ps[:, 4 * k + 3, 0:TB * 4].rearrange("p (t e) -> p t e", e=4)[:, :, 0:E],
                                           rc[:, :].unsqueeze(1).broadcast_to([P, TB, E]), ALU.add))
                    link(dve.tensor_reduce(rm[:, k, :], lg[:, k, :, :], X, ALU.max))
                    dve.tensor_tensor(lg[:, k, :, :], lg[:, k, :, :], rm[:, k, :].unsqueeze(2).broadcast_to([P, TB, E]), ALU.subtract).then_inc(lg_sub, 1)
                for k in range(NB):
                    dve.wait_ge(lg_exp, b * NB + k + 1)
                    link(dve.tensor_reduce(rm[:, k, :], lg[:, k, :, :], X, ALU.add))
                    link(dve.reciprocal(rm[:, k, :], rm[:, k, :]))
                    dve.tensor_tensor(lg[:, k, :, :], lg[:, k, :, :], rm[:, k, :].unsqueeze(2).broadcast_to([P, TB, E]), ALU.mult).then_inc(lg_ready, 1)
                dve.wait_ge(pbc_ready, b * NB + NB)
                n0 = b * NB * MC
                for n in range(NB * MC):
                    dve.wait_ge(h1_act, n0 + n + 1)
                    dve.tensor_tensor(ring[:, n % 4, :], ring[:, n % 4, :], p_bc[:, n // MC, n % MC // 4, :], ALU.mult).then_inc(h1_ready, 1)
                for k in range(NB):
                    dve.wait_ge(y_done, b * 12 + 2 + k + 1)
                    for m in range(KC):
                        ins = dve.scalar_tensor_tensor(yT[:, k, m, :], ps[:, (2, 4)[k] + m, :], colT[:, C_OUTB + m:C_OUTB + m + 1], gT[:, k, m, :], ALU.add, ALU.mult)
                    ins.then_inc(yT_ready, 1)
                residual_norm(1)

                for k in range(NB):
                    dve.wait_ge(v_done, b * NB + k + 1)
                    for j in range(2):
                        t = TB * k + 2 * j
                        ins = dve.tensor_tensor(v2[:, t:t + 2, 0:H * VS].rearrange("p t (h d) -> p t h d", d=VS)[:, :, :, 0:HD], ps[:, 4 * k + 2 + j, :].rearrange("p (t h d) -> p t h d", t=2, d=HD),
                                                vb2[:, :].rearrange("p (h d) -> p h d", d=HD).unsqueeze(1).broadcast_to([P, 2, H, HD]), ALU.add)
                    ins.then_inc(v_ready, 1)
                u0 = b * N_RING
                uses = [0]

                def bank():
                    n = uses[0]
                    uses[0] += 1
                    dve.wait_ge(ring_ready, u0 + n + 1)
                    return ps[:, n % 2, :]

                def low_parts(c, h0):
                    for qk in range(2):
                        for k in range(NB):
                            dve.wait_ge(hi_ready, b * 8 + h0 + 2 * qk + k + 1)
                            col = (C_BQ2, C_BK2)[qk] + c
                            cols = slice(k * BLK, (k + 1) * BLK)
                            dve.scalar_tensor_tensor(dense[2 * qk + 1][:, cols], bank(), colT[:, col:col + 1], dense[2 * qk][:, cols].bitcast(F32),
                                                     ALU.add, ALU.subtract).then_inc(ring_read, 1)

                def spread(gr):
                    for p in (2 * gr, 2 * gr + 1):
                        for half in range(2):
                            dve.tensor_copy(qx[:, p % 4, half * 512:(half + 1) * 512], bank()).then_inc(ring_read, 1)
                        for half in range(2):
                            dve.tensor_scalar(kx[:, p % 4, half * 512:(half + 1) * 512], bank(), k_aug[:, 0:1], None, ALU.add).then_inc(ring_read, 1)

                def query_maximum(u):
                    hh, t = u // T, u % T
                    for half in range(2):
                        dve.tensor_reduce(mxp[:, hh, t, half:half + 1], bank(), X, ALU.max).then_inc(ring_read, 1)

                def turn_maxima(gr):
                    dve.wait_ge(ring_read, u0 + uses[0])
                    link(dve.tensor_tensor(mm[:, :, :], mxp[:, :, :, 0], mxp[:, :, :, 1], ALU.max))
                    link(dve.tensor_copy(mh[:, :, :], mm[:, :, :]))
                    link(dve.tensor_tensor(ml[:, :, :], mm[:, :, :], mh[:, :, :].bitcast(F32), ALU.subtract))
                    for p in range(2):
                        cols = mt[:, :, :].rearrange("p t (e c) -> p e t c", e=2)
                        dve.tensor_copy(cols[:, :, :, 48], mh[:, 2 * p:2 * p + 2, :].bitcast(F32))
                        dve.tensor_copy(cols[:, :, :, 49], ml[:, 2 * p:2 * p + 2, :]).then_inc(mt_ready, 1)
                        for half in range(2):
                            q = qx[:, (2 * gr + p) % 4, half * 512:(half + 1) * 512]
                            dve.tensor_tensor(q, bank(), q.bitcast(F32), ALU.add).then_inc(ring_read, 1)

                def finish(gr):
                    for half in range(2):
                        acc = bank().rearrange("p (t h c) -> p t h c", t=TB, h=4)
                        link(dve.reciprocal(fr[:, half, :, :], acc[:, :, :, HD]))
                        dve.tensor_tensor(xhat[:, half * TB:(half + 1) * TB, 4 * HD * gr:4 * HD * (gr + 1)].rearrange("p t (h d) -> p t h d", d=HD),
                                          acc[:, :, :, 0:HD], fr[:, half, :, :].unsqueeze(3).broadcast_to([P, TB, 4, HD]), ALU.mult).then_inc(ring_read, 1)

                low_parts(0, 0)
                spread(0)
                dve.wait_ge(mt_clear, b + 1)
                for u in range(32):
                    query_maximum(u)
                turn_maxima(0)
                for gr in range(4):
                    if gr == 1:
                        low_parts(1, 4)
                    if gr < 3:
                        spread(gr + 1)
                        for u in range(32):
                            query_maximum(u)
                        turn_maxima(gr + 1)
                    finish(gr)
                assert uses[0] == N_RING
                residual_norm(2)

                build_keys(1)
                context_attention(1)
                residual_norm(3)
                residual_norm(4)

                for k in range(NB):
                    dve.wait_ge(v3_done, b * NB + k + 1)
                    for j in range(2):
                        t = TB * k + 2 * j
                        for odd in range(2):
                            o = HD * odd
                            ins = dve.tensor_tensor(
                                v3[:, t:t + 2, :, :].rearrange("p t (j o) d -> p t j o d", o=2)[:, :, :, odd, o:o + HD],
                                ps[:, 4 * k + j, :].rearrange("p (t j d) -> p t j d", t=2, d=2 * HD)[:, :, :, o:o + HD],
                                vb3[:, :].rearrange("p (j d) -> p j d", d=2 * HD)[:, :, o:o + HD].unsqueeze(1).broadcast_to([P, 2, H // 2, HD]), ALU.add)
                    ins.then_inc(v3_ready, 1)
                w0 = b * N_UNIT

                def window_centre(u):
                    dve.wait_ge(ws_ready, w0 + u + 1)
                    sc = ps[:, 2 * (u % 2):2 * (u % 2) + 2, :].rearrange("p a (h s) -> p (a h) s", s=P)
                    link(dve.tensor_reduce(mx[:, u % 2, 0:HC], sc, X, ALU.max))
                    if u >= 2:
                        dve.wait_ge(wp_turned, w0 + u - 1)
                    dve.tensor_tensor(prob[:, u % 2, :].rearrange("p (h s) -> p h s", s=P), sc,
                                      mx[:, u % 2, 0:HC].unsqueeze(2).broadcast_to([P, HC, P]), ALU.subtract).then_inc(ws_read, 1)

                def window_divide(u):
                    t, c = u // KC, u % KC
                    dve.wait_ge(wpv_done, w0 + u + 1)
                    r = rs[:, u % 2 * P:(u % 2 + 1) * P]
                    link(dve.reciprocal(r, ps[:, 6 + u % 2, P:2 * P]))
                    dve.tensor_tensor(oT[:, t // TB, c, t % TB * P:(t % TB + 1) * P], ps[:, 6 + u % 2, 0:P], r, ALU.mult).then_inc(wo_ready, 1)
                window_centre(0)
                window_centre(1)
                for u in range(N_UNIT):
                    if u + 2 < N_UNIT:
                        window_centre(u + 2)
                    window_divide(u)
                residual_norm(5)

                build_keys(2)
                context_attention(2)
                residual_norm(6)

                n0 = b * NB * NC_HID
                for n in range(NB * NC_HID):
                    m = n % NC_HID
                    dve.wait_ge(h3_act, n0 + n + 1)
                    dve.scalar_tensor_tensor(ring[:, n % 4, :], ps[:, 2 * (n % 2) + 1, :], colT[:, C_BM13 + NC_HID + m:C_BM13 + NC_HID + m + 1],
                                             ring[:, n % 4, :], ALU.add, ALU.mult).then_inc(h3_ready, 1)
                for k in range(NB):
                    residual(7, k).then_inc(x_final, 1)
                dve.wait_ge(x_final, b * NB + NB)

        @block.gpsimd
        def _(pool):
            pool.memset(minus_half[:, :], -0.5).then_inc(set_pool, 1)
            pool.wait_ge(set_pool, 1)
            pool.wait_ge(ctx_var, 1)
            pool.tensor_tensor(s_st[:, 10:12], s_st[:, 8:10], minus_half[:, 0:2], ALU.pow).then_inc(ctx_rstd, 1)
            with pool.Fori(0, B) as b:
                def ln(i):
                    for k in range(NB):
                        pool.wait_ge(ve_ready, b * 2 * N_LN + 2 * i + k + 1)
                        pool.tensor_tensor(rstd[:, k, :], ve[:, k, :], minus_half[:, :], ALU.pow).then_inc(rstd_ready, 1)

                ln(0)
                ln(1)
                pool.wait_ge(y_done, b * 12 + 2)
                pool.sem_inc(passed, 1)
                pool.memset(mt[:, :, :], 0.0).then_inc(mt_clear, 1)
                ln(2)
                pool.wait_ge(y_turned, b * 2 * N_RES + 4)
                pool.sem_inc(passed, 1)
                pool.memset(v2[:, :, H * VS:], 0.0)
                pool.memset(v2[:, :, 0:H * VS].rearrange("p t (h d) -> p t h d", d=VS)[:, :, :, HD:VS], 1.0).then_inc(v2_clear, 1)
                pool.wait_ge(pv2_done, b * 32 + 32)
                pool.sem_inc(passed, 1)
                pairs = v3[:, :, :, :].rearrange("p t (j o) d -> p (t j) o d", o=2)
                pool.memset(pairs[:, :, 0, HD:2 * HD], 0.0)
                pool.memset(pairs[:, :, 1, 0:HD], 0.0).then_inc(v3_clear, 1)
                ln(3)
                ln(4)
                ln(5)
                u0 = b * N_UNIT
                for u in range(N_UNIT):
                    t, c = u // KC, u % KC
                    if u % N_UNIT in (0, N_UNIT // 2):
                        pool.wait_ge(qk3_ready, b * NB + t // TB + 1)
                    if u >= 2:
                        pool.wait_ge(ws_ready, u0 + u - 1)
                    pool.tensor_tensor(wkblk[:, u % 2, :, :], kT3[:, t // TB, c, t % TB * P:(t % TB + 1) * P].unsqueeze(1).broadcast_to([P, HC, P]),
                                       head_mask[:, :].unsqueeze(2).broadcast_to([P, HC, P]), ALU.mult).then_inc(wk_ready, 1)
                ln(6)
                ln(7)


def constants():
    row = np.arange(P)
    head_mask = (row[:, None] // HD == np.arange(HC)).astype(np.float32)
    ones_ctx = (row[:, None] // S == np.arange(2 * HD) // HD).astype(np.float32)
    ones_win = np.zeros((P, 2, 2 * HD), np.float32)
    ones_win[:, 0, :HD] = 1
    ones_win[:, 1, HD:] = 1
    sel = np.zeros((P, 4, 4, P), np.float32)
    d = np.arange(HD)
    for pp in range(4):
        for e in range(2):
            r = 32 * pp + HD * e + d
            for part, places in enumerate(((0, 2), (1,), (0, 1), (2,))):
                for place in places:
                    sel[r, pp, part, 64 * e + HD * place + d] = 1
    k_aug = np.zeros((P, 1), np.float32)
    k_aug[[48, 49, 64 + 48, 64 + 49]] = -1
    sel3 = np.zeros((E, E, P), np.float32)
    sel3[np.arange(E), np.arange(E)] = 1
    return {"c_ident": np.eye(P, dtype=np.float32), "c_head_mask": head_mask, "c_ones_ctx": ones_ctx,
            "c_ones_win": ones_win, "c_sel": sel, "c_k_aug": k_aug, "c_sel3": sel3}


def kernel(**inputs):
    import concourse.bacc as bacc
    from concourse.bass_utils import run_bass_kernel_spmd

    arrays = {n: np.ascontiguousarray(np.asarray(a)) for n, a in inputs.items()}
    arrays.update(constants())
    nc = bacc.Bacc("TRN2", target_bir_lowering=False, num_devices=1)
    handles = {n: nc.dram_tensor(f"in_{n}_dram", a.shape, mybir.dt.from_np(a.dtype), kind="ExternalInput") for n, a in arrays.items()}
    out = nc.dram_tensor("out_0_dram", (B, L, D), F32, kind="ExternalOutput")
    build(nc, out.ap(), {n: h.ap() for n, h in handles.items()})
    if not nc.is_finalized():
        nc.finalize()
    result = run_bass_kernel_spmd(nc, [{f"in_{n}_dram": a for n, a in arrays.items()}], core_ids=[0])
    return np.asarray(result.results[0]["out_0_dram"])
```

```python
from contextlib import ExitStack

import numpy as np
import concourse.bass as bass
import concourse.mybir as mybir

F32 = mybir.dt.float32
F32R = mybir.dt.float32r
ALU = mybir.AluOpType
ACT = mybir.ActivationFunctionType
X = mybir.AxisListType.X

P = 128
D = 256
KC = D // P
B = 2
L = 1024
T = L // P
NB = 2
TB = T // NB
BLK = TB * P
H = 16
HD = D // H
HC = P // HD
S = 64
SHIFT = 64
E = 3
RH = 512
MC = E * RH // P
HID = 1024
NC_HID = HID // P
TOPK = 16
VS = HD + 1
QK_SCALE = float(HD) ** -0.5
L1_SCALE = float(D) ** -0.5
EPS5, EPS6 = 1e-5, 1e-6
LOWEST = -3.4028234663852886e38

M_SC_Q, M_SH_Q, M_SC_KV, M_SH_KV = 0, 2, 4, 6
M_SH_A, M_SC_A, M_G_A, M_SH_M, M_SC_M, M_G_M = 8, 10, 12, 14, 16, 18
M3_SH_SA, M3_SC_SA, M3_G_SA, M3_SH_CA, M3_SC_CA, M3_G_CA, M3_SH_ML, M3_SC_ML, M3_G_ML = range(20, 38, 2)
N_MOD = 38
M_BG = 38
GATED = (M_G_A, M_G_M, M3_G_SA, M3_G_CA, M3_G_ML)
SCALES = (M_SC_Q, M_SC_KV, M_SC_A, M_SC_M, M3_SC_SA, M3_SC_CA, M3_SC_ML)
M_HB = 48
N_MC = 62
C_BQ0, C_BP0, C_BK0, C_GAMMA, C_BETA, C_GB2, C_OUTB = range(62, 76, 2)
C_BQ2, C_BK2, C_BQC, C_BKC, C_BCP, C_BM1 = 76, 78, 80, 82, 84, 86
C_BQ3, C_BK3, C_BQ3C, C_BK3C, C_BM13 = 94, 96, 98, 100, 102
C_COND = 118
N_COL = 122

N_LN, N_Q, N_RES, N_CA = 8, 3, 8, 3
NP = H // 2
N_SCORE = 2 * KC + H * T + NP + NP
N_SPREAD = 2 * NP
N_RING = N_SCORE + N_SPREAD
UNITS = H * T
LEAD = 20
N_RA = 12 * 16
N_UNIT = T * KC


def build(nc, out, g):
    es = ExitStack()
    with es:
        base = (nc.sbuf_base + 63) // 64 * 64
        top = [base]

        def at(name, shape, dt, offset):
            return nc.alloc_sbuf_tensor_at(name, shape, dt, offset=offset)

        def keep(name, shape, dt=F32):
            size = int(np.prod(shape[1:])) * 4
            o = top[0]
            top[0] = o + (size + 31) // 32 * 32
            return at(name, shape, dt, o)

        def region(size):
            o = top[0]
            top[0] += size
            return o

        def sem(name):
            return es.enter_context(nc.semaphore(name))

        ident = keep("ident", [P, P])
        head_mask = keep("head_mask", [P, HC])
        ones_ctx = keep("ones_ctx", [P, 32])
        ones_win = keep("ones_win", [P, 2, 32])
        sel = keep("sel", [P, 4, 4, P], F32R)
        k_aug = keep("k_aug", [P, 1])
        minus_half = keep("minus_half", [P, TB])
        sel3 = keep("sel3", [E, E, P])
        b2 = keep("b2", [E, D])
        vb2 = keep("vb2", [P, D])
        vb3 = keep("vb3", [P, D])
        rb = keep("rb", [P, E])
        colT = keep("colT", [P, N_COL])
        mod2 = keep("mod2", [P, B, N_MC])
        kT2 = keep("kT2", [P, 3, KC, B, S])
        v_ctx2 = keep("v_ctx2", [P, B, 3, HC, 32])
        kw2 = keep("kw2", [P, KC, B, S])
        N_VW = E * RH + D + E
        vw2 = keep("vw2", [S, B, N_VW])
        rc2 = keep("rc2", [P, B, E])
        mod = keep("mod", [P, N_MC])
        v_ctx = keep("v_ctx", [P, 3, HC, 32])
        kw = keep("kw", [P, KC, S])
        kT = keep("kT", [P, 3, KC, S])
        rc = keep("rc", [P, E])
        x = keep("x", [P, T, D])
        s_sel = at("s_sel", [P, 4, 4, P], F32, top[0])
        hT = keep("hT", [P, NB, KC, BLK])
        st = keep("st", [P, NB, TB, 6])
        mv = keep("mv", [P, NB, TB, 2])
        ve = keep("ve", [P, NB, TB])
        rstd = keep("rstd", [P, NB, TB])
        mx = keep("mx", [P, 2, H])
        mm = keep("mm", [P, 2, T])
        mh = keep("mh", [P, 2, T], F32R)
        fr = keep("fr", [P, 2, TB, 4])
        r1m = keep("r1m", [P, NB, TB])
        lg = keep("lg", [P, NB, TB, E])
        rm = keep("rm", [P, NB, TB])

        RA = region(40 * 1024 + 64)
        RC1 = region(34 * 1024)
        RC2 = region(24 * 1024)
        RF = region(48 * 1024)
        assert top[0] <= nc.sbuf_usable_end, (top[0], nc.sbuf_usable_end)
        K1 = 1024

        def weights(start, items):
            made, o = [], start
            for name, shape in items:
                made.append(at(name, shape, F32, o))
                o += (int(np.prod(shape[1:])) * 4 + 31) // 32 * 32
            return made, o

        (wq0, wp0, w1, wg1, wr, w2, wg2, wout, wv2, wqk2), e0 = weights(RA, [
            ("wq0", [P, KC, D]), ("wp0", [P, KC, D]), ("w1", [P, E, KC, RH]), ("wg1", [P, KC, D]),
            ("wr", [P, KC, E]), ("w2", [P, MC, D]), ("wg2", [P, KC, D]), ("wout", [P, KC, D]),
            ("wv2", [P, KC, D]), ("wqk2", [P, KC, 2 * D])])
        assert e0 <= RC1
        (wproj, wqc, wcp, wm1, wm2, wqkv3, wso, wq3, wco), e1 = weights(RC1, [
            ("wproj", [P, KC, D]), ("wqc", [P, KC, D]), ("wcp", [P, KC, D]), ("wm1", [P, KC, HID]),
            ("wm2", [P, NC_HID, D]), ("wqkv3", [P, KC, 3 * D]), ("wso", [P, KC, D]), ("wq3", [P, KC, D]),
            ("wco", [P, KC, D])])
        assert e1 <= RC2
        (w3a, w3b), e2 = weights(RC2, [("w3a", [P, KC, 2 * HID]), ("w3b", [P, NC_HID, D])])
        assert e2 <= RF

        (s_ss_q, s_ss_kv, s_mod, s_ada, s_kv0, s_q1, s_k1, s_v1, s_ev, s_an, s_gev, s_gan, s_rev, s_ran, s_kvc, s_kv3,
         s_rows, s_ctx, s_xh, s_ctxT, s_k1T, s_wqT, s_vT, s_crep, s_vb, s_silu, s_st), e3 = weights(RC1, [
             ("s_ss_q", [P, KC, 2 * D]), ("s_ss_kv", [P, KC, 2 * D]), ("s_mod", [P, KC, 6 * D]),
             ("s_ada", [P, KC, 9 * D]), ("s_kv0", [P, KC, 2 * D]), ("s_q1", [P, KC, D]), ("s_k1", [P, KC, D]),
             ("s_v1", [P, KC, D]), ("s_ev", [P, E, KC, RH]), ("s_an", [P, E, KC, RH]), ("s_gev", [P, KC, D]),
             ("s_gan", [P, KC, D]), ("s_rev", [P, KC, E]), ("s_ran", [P, KC, E]), ("s_kvc", [P, KC, 2 * D]),
             ("s_kv3", [P, KC, 2 * D]), ("s_rows", [P, P]), ("s_ctx", [P, D]), ("s_xh", [P, 3, D]),
             ("s_ctxT", [P, 3, KC, B, 2, S]), ("s_k1T", [P, KC, B * S]), ("s_wqT", [P, KC, D]),
             ("s_vT", [P, KC, B * S]), ("s_crep", [P, KC, B, P]), ("s_vb", [P, 3, D]), ("s_silu", [P, B * KC]),
             ("s_st", [P, 16])])
        assert e3 <= top[0], (e3, top[0])

        xhat = at("xhat", [P, T, D], F32, RF)
        yT = at("yT", [P, NB, KC, BLK], F32, RF)
        taken = at("taken", [P, 2, H * S], F32, RF)
        qT = at("qT", [P, NB, KC, BLK], F32, RF + 8 * K1)
        oT = at("oT", [P, NB, KC, BLK], F32, RF + 8 * K1)
        ring = at("ring", [P, 4, BLK], F32, RF + 16 * K1)
        kblk = at("kblk", [P, KC, HC, S], F32, RF + 16 * K1)
        rs = at("rs", [P, BLK], F32, RF + 20 * K1)
        m8 = at("m8", [P, 2, H, TOPK], F32, RF + 22 * K1)
        prob = at("prob", [P, 2, 1024], F32, RF + 24 * K1)
        probT = at("probT", [P, 2, HC, P], F32, RF + 32 * K1)
        vx = at("vx", [P, HC, 64], F32, RF + 40 * K1)
        o_tok = at("o_tok", [P, 2, D], F32, RF + 42 * K1)
        wprobT = at("wprobT", [P, 2, HC, P], F32, RF + 32 * K1)
        wkblk = at("wkblk", [P, 2, HC, P], F32, RF + 40 * K1)
        vw = at("vw", [S, N_VW], F32, RC2)
        p1T = at("p1T", [S, NB, BLK], F32, RC2 + 8 * K1)
        gT = at("gT", [P, NB, KC, BLK], F32, RC2 + 12 * K1)
        g1 = [at("g1_0", [P, KC, BLK], F32, RC2 + 20 * K1), at("g1_1", [P, KC, BLK], F32, RF + 44 * K1)]
        p1 = at("p1", [P, NB, TB, S], F32, RF + 24 * K1)
        pT = at("pT", [E, NB, BLK], F32, RF + 26 * K1)
        p_bc = at("p_bc", [P, NB, E, BLK], F32, RF + 32 * K1)
        rT = [at("rT_0", [P, KC, BLK], F32, RF + 44 * K1), at("rT_1", [P, KC, BLK], F32, RC2 + 20 * K1)]
        qx = at("qx", [P, 4, L], F32R, RA)
        kx = at("kx", [P, 4, L], F32R, RA + 16 * K1)
        dense = [at(n, [P, L], F32R, o) for n, o in (("q_hi", RC2 + 8 * K1), ("q_lo", RA + 32 * K1),
                                                     ("k_hi", RC2), ("k_lo", RC2 + 4 * K1))]
        v2 = at("v2", [P, T, H * VS + HD], F32, RC2 + 12 * K1)
        pt = at("pt", [P, 8, L], F32, RF + 16 * K1)
        accS = at("accS", [P, 2, BLK], F32, RF + 8 * K1)
        mt = at("mt", [P, T, P], F32, RF + 12 * K1)
        v3 = at("v3", [P, T, H, 32], F32, RA)
        kT3 = at("kT3", [P, NB, KC, BLK], F32, RA + 16 * K1)

        ps = es.enter_context(nc.psum_tensor("ps", [P, 8, 512], F32))

        consts_ld, rows_ld, ctx_ld = sem("consts_ld"), sem("rows_ld"), sem("ctx_ld")
        s_mod_ld, s_kv_ld, s_l1_ld, rc1_ld = sem("s_mod_ld"), sem("s_kv_ld"), sem("s_l1_ld"), sem("rc1_ld")
        ra_ld, rc2_ld, out_stored = sem("ra_ld"), sem("rc2_ld"), sem("out_stored")
        x_ld = [sem("x_ld0"), sem("x_ld1")]
        set_pe, set_act, set_dve, set_pool = sem("set_pe"), sem("set_act"), sem("set_dve"), sem("set_pool")
        dve_step, ctx_var, ctx_rstd = sem("dve_step"), sem("ctx_var"), sem("ctx_rstd")
        begun = sem("begun")
        ve_ready, rstd_ready, xhat_ready = sem("ve_ready"), sem("rstd_ready"), sem("xhat_ready")
        ln_turned, hT_ready = sem("ln_turned"), sem("hT_ready")
        q_done, qT_ready = sem("q_done"), sem("qT_ready")
        kblk_ready, s_ready, s_read, p_exp, p_turned, pT_ready = (sem(n) for n in (
            "kblk_ready", "s_ready", "s_read", "p_exp", "p_turned", "pT_ready"))
        top_exp = sem("top_exp")
        pv_done, o_ready, o_turned, oT_ready = sem("pv_done"), sem("o_ready"), sem("o_turned"), sem("oT_ready")
        y_done, yT_ready, y_turned, x_final = sem("y_done"), sem("yT_ready"), sem("y_turned"), sem("x_final")
        p1s_done, p1_sub, p1_exp, p1_ready, p1_turned, p1T_ready = (sem(n) for n in (
            "p1s_done", "p1_sub", "p1_exp", "p1_ready", "p1_turned", "p1T_ready"))
        lg_done, lg_sub, lg_exp, lg_ready, lg_turned, pT_made = (sem(n) for n in (
            "lg_done", "lg_sub", "lg_exp", "lg_ready", "lg_turned", "pT_made"))
        g1_done, g1_ready, g2_done, gT_ready, pbc_done, pbc_ready = (sem(n) for n in (
            "g1_done", "g1_ready", "g2_done", "gT_ready", "pbc_done", "pbc_ready"))
        mt_clear, ot_turned, passed = sem("mt_clear"), sem("ot_turned"), sem("passed")
        h1_done, h1_act, h1_ready, w2_done, rT_ready = (sem(n) for n in (
            "h1_done", "h1_act", "h1_ready", "w2_done", "rT_ready"))
        h2_done, h2_ready, w22_done = sem("h2_done"), sem("h2_ready"), sem("w22_done")
        h3_done, h3_act, h3_ready, w32_done = sem("h3_done"), sem("h3_act"), sem("h3_ready"), sem("w32_done")
        v_done, v_ready, v2_clear = sem("v_done"), sem("v_ready"), sem("v2_clear")
        ring_ready, ring_read, spread_read, hi_ready = (sem(n) for n in ("ring_ready", "ring_read", "spread_read", "hi_ready"))
        st_ready, pt_ready, pv2_done, acc_read, mt_ready = (sem(n) for n in (
            "st_ready", "pt_ready", "pv2_done", "acc_read", "mt_ready"))
        qk3_done, qk3_ready, v3_done, v3_ready, v3_clear = (sem(n) for n in (
            "qk3_done", "qk3_ready", "v3_done", "v3_ready", "v3_clear"))
        wk_ready, ws_ready, ws_read, wp_exp, wp_turned, wpT_ready, wpv_done, wo_ready = (sem(n) for n in (
            "wk_ready", "ws_ready", "ws_read", "wp_exp", "wp_turned", "wpT_ready", "wpv_done", "wo_ready"))

        block = es.enter_context(nc.Block())

        def rows(a):
            return a.rearrange("(k p) n -> p k n", p=P)

        @block.sync
        def _(sp):
            sp.dma_start(ident[:, :], g["c_ident"]).then_inc(consts_ld, 16)
            sp.dma_start(head_mask[:, :], g["c_head_mask"]).then_inc(consts_ld, 16)
            sp.dma_start(ones_ctx[:, :], g["c_ones_ctx"]).then_inc(consts_ld, 16)
            sp.dma_start(ones_win[:, :, :], g["c_ones_win"]).then_inc(consts_ld, 16)
            sp.dma_start(s_sel[:, :, :, :], g["c_sel"]).then_inc(consts_ld, 16)
            sp.dma_start(k_aug[:, :], g["c_k_aug"]).then_inc(consts_ld, 16)
            sp.dma_start(sel3[:, :, :], g["c_sel3"]).then_inc(consts_ld, 16)
            r = 0
            for name in ("L0_xcond_bss_q", "L0_xcond_bss_kv", "L2_xcond_b_mod", "L3_xcond_b_ada", "L2_xcond_b_proj",
                         "L2_xcond_b_mlp2", "L3_xcond_b_so", "L3_xcond_b_co", "L3_xcond_b_m2", "L1_xcond_e_b1",
                         "L1_xcond_gate_b1", "L0_xcond_bq", "L0_xcond_bp", "L0_xcond_bkv", "L1_xcond_ln_gamma",
                         "L1_xcond_ln_beta", "L1_xcond_gate_b2", "L1_xcond_out_b", "L2_xcond_b_qkv", "L2_xcond_b_qc",
                         "L2_xcond_b_kvc", "L2_xcond_b_cproj", "L2_xcond_b_mlp1", "L3_xcond_b_qkv", "L3_xcond_b_q",
                         "L3_xcond_b_kv", "L3_xcond_b_m1", "cond_1024"):
                a = g[name]
                if len(a.shape) == 2:
                    a = a.rearrange("e n -> (e n)")
                n = a.shape[0] // P
                if name in ("L0_xcond_bkv", "L2_xcond_b_kvc", "L3_xcond_b_kv"):
                    n = KC
                if name in ("L2_xcond_b_qkv", "L3_xcond_b_qkv"):
                    n = 2 * KC
                sp.dma_start(s_rows[r:r + n, :], a[0:n * P].rearrange("(n p) -> n p", p=P)).then_inc(rows_ld, 16)
                r += n
            assert r == N_COL
            sp.dma_start(s_ctx[:, :], g["ctx_1024"].rearrange("b s d -> (b s) d")).then_inc(ctx_ld, 16)
            for tile, name, a, z in ((vb2, "L2_xcond_b_qkv", 2 * D, 3 * D), (vb3, "L3_xcond_b_qkv", 2 * D, 3 * D),
                                     (rb, "L1_xcond_router_b", 0, E)):
                sp.dma_start(tile[:, :], g[name][a:z].unsqueeze(0).broadcast_to([P, z - a])).then_inc(consts_ld, 16)
            for i, name in enumerate(("L0_xcond_bkv", "L2_xcond_b_kvc", "L3_xcond_b_kv")):
                sp.dma_start(s_vb[:, i, :], g[name][D:2 * D].unsqueeze(0).broadcast_to([P, D])).then_inc(consts_ld, 16)
            sp.dma_start(b2[:, :], g["L1_xcond_e_b2"]).then_inc(consts_ld, 16)
            for tile, name in ((s_ss_q, "L0_xcond_Wss_q"), (s_ss_kv, "L0_xcond_Wss_kv"), (s_mod, "L2_xcond_W_mod"),
                               (s_ada, "L3_xcond_w_ada")):
                sp.dma_start(tile[:, :, :], rows(g[name])).then_inc(s_mod_ld, 16)
            for tile, name in ((s_kv0, "L0_xcond_Wkv"), (s_kvc, "L2_xcond_W_kvc"), (s_kv3, "L3_xcond_w_kv")):
                sp.dma_start(tile[:, :, :], rows(g[name])).then_inc(s_kv_ld, 16)
            for tile, name in ((s_q1, "L1_xcond_Wq"), (s_k1, "L1_xcond_Wk"), (s_v1, "L1_xcond_Wv")):
                sp.dma_start(tile[:, :, :], rows(g[name])).then_inc(s_l1_ld, 16)
            for e in range(E):
                sp.dma_start(s_ev[:, e, :, :], rows(g["L1_xcond_e_w1"][e, D:2 * D, :])).then_inc(s_l1_ld, 16)
                sp.dma_start(s_an[:, e, :, :], rows(g["L1_xcond_e_w1"][e, 2 * D:3 * D, :])).then_inc(s_l1_ld, 16)
            for tile, name, part in ((s_gev, "L1_xcond_gate_w1", 1), (s_gan, "L1_xcond_gate_w1", 2),
                                     (s_rev, "L1_xcond_router_W", 1), (s_ran, "L1_xcond_router_W", 2)):
                sp.dma_start(tile[:, :, :], rows(g[name][part * D:(part + 1) * D, :])).then_inc(s_l1_ld, 16)

            def load_ra():
                for tile, name in ((wq0, "L0_xcond_Wq"), (wp0, "L0_xcond_Wp"), (wg2, "L1_xcond_gate_w2"),
                                   (wout, "L1_xcond_out_w")):
                    sp.dma_start(tile[:, :, :], rows(g[name])).then_inc(ra_ld, 16)
                sp.dma_start(wqk2[:, :, :], rows(g["L2_xcond_W_qkv"][:, 0:2 * D])).then_inc(ra_ld, 16)
                sp.dma_start(wv2[:, :, :], rows(g["L2_xcond_W_qkv"][:, 2 * D:3 * D])).then_inc(ra_ld, 16)
                for e in range(E):
                    sp.dma_start(w1[:, e, :, :], rows(g["L1_xcond_e_w1"][e, 0:D, :])).then_inc(ra_ld, 16)
                sp.dma_start(wg1[:, :, :], rows(g["L1_xcond_gate_w1"][0:D, :])).then_inc(ra_ld, 16)
                sp.dma_start(wr[:, :, :], rows(g["L1_xcond_router_W"][0:D, :])).then_inc(ra_ld, 16)
                sp.dma_start(w2[:, :, :], g["L1_xcond_e_w2"].rearrange("e (k p) n -> p (e k) n", p=P)).then_inc(ra_ld, 16)

            load_ra()
            sp.wait_ge(set_pe, 8)
            sp.wait_ge(set_act, 4)
            sp.wait_ge(set_dve, 7)
            for tile, name in ((wproj, "L2_xcond_W_proj"), (wqc, "L2_xcond_W_qc"), (wcp, "L2_xcond_W_cproj"),
                               (wm1, "L2_xcond_W_mlp1"), (wm2, "L2_xcond_W_mlp2"), (wqkv3, "L3_xcond_w_qkv"),
                               (wso, "L3_xcond_w_so"), (wq3, "L3_xcond_w_q"), (wco, "L3_xcond_w_co")):
                sp.dma_start(tile[:, :, :], rows(g[name])).then_inc(rc1_ld, 16)

            sp.sem_inc(out_stored, 1)
            with sp.Fori(0, B) as b:
                xb = g["x"][b, :, :]
                sp.wait_ge(out_stored, b * 64 + 1)
                sp.dma_start(x[:, 0:TB, :], xb[SHIFT:SHIFT + BLK, :].rearrange("(t p) d -> p t d", p=P)).then_inc(x_ld[0], 16)
                sp.dma_start(x[:, TB:T - 1, :], xb[SHIFT + BLK:L - SHIFT, :].rearrange("(t p) d -> p t d", p=P)).then_inc(x_ld[1], 16)
                sp.dma_start(x[0:SHIFT, T - 1, :], xb[L - SHIFT:L, :]).then_inc(x_ld[1], 16)
                sp.dma_start(x[SHIFT:P, T - 1, :], xb[0:SHIFT, :]).then_inc(x_ld[1], 16)
                sp.wait_ge(ring_read, b * N_SCORE + N_SCORE)
                sp.wait_ge(pv2_done, b * T * NP + T * NP)
                sp.dma_start(w3a[:, :, :], rows(g["L3_xcond_w_m1"])).then_inc(rc2_ld, 16)
                sp.dma_start(w3b[:, :, :], rows(g["L3_xcond_w_m2"])).then_inc(rc2_ld, 16)
                sp.wait_ge(wo_ready, b * N_UNIT + N_UNIT)
                load_ra()
                ob = out[b, :, :]
                sp.wait_ge(x_final, b * NB + 1)
                sp.dma_start(ob[SHIFT:SHIFT + BLK, :].rearrange("(t p) d -> p t d", p=P), x[:, 0:TB, :]).then_inc(out_stored, 16)
                sp.wait_ge(x_final, b * NB + 2)
                sp.dma_start(ob[SHIFT + BLK:L - SHIFT, :].rearrange("(t p) d -> p t d", p=P), x[:, TB:T - 1, :]).then_inc(out_stored, 16)
                sp.dma_start(ob[L - SHIFT:L, :], x[0:SHIFT, T - 1, :]).then_inc(out_stored, 16)
                sp.dma_start(ob[0:SHIFT, :], x[SHIFT:P, T - 1, :]).then_inc(out_stored, 16)
            sp.wait_ge(out_stored, B * 64 + 1)
            sp.wait_ge(ra_ld, (B + 1) * N_RA)

        @block.tensor
        def _(pe):
            def linear(bank, w, m, src):
                for c in range(KC):
                    ins = pe.matmul(ps[:, bank, :], w[:, c, m * P:(m + 1) * P], src[:, c, :],
                                    start=c == 0, stop=c == KC - 1)
                return ins

            def turn_block(k, src):
                for c in range(KC):
                    for t in range(TB):
                        ins = pe.transpose(ps[:, 4 * k + c, t * P:(t + 1) * P], src[:, TB * k + t, c * P:(c + 1) * P], ident[:, :])
                return ins

            pe.wait_ge(consts_ld, 14 * 16)
            pe.wait_ge(rows_ld, 28 * 16)
            pe.transpose(ps[:, 0, 0:N_COL], s_rows[0:N_COL, :], ident[0:N_COL, 0:N_COL]).then_inc(set_pe, 1)
            pe.wait_ge(set_dve, 1)
            for v in range(3):
                for c in range(KC):
                    ins = pe.transpose(ps[:, 1 + v, c * P:(c + 1) * P], s_xh[:, v, c * P:(c + 1) * P], ident[:, :])
            ins.then_inc(set_pe, 1)
            pe.wait_ge(s_mod_ld, 4 * 16)
            pe.wait_ge(set_act, 1)
            silu = s_silu[:, :].rearrange("p (b c) -> p c b", c=KC)
            n = 0
            for w, chunks in ((s_ss_q, 4), (s_ss_kv, 4), (s_mod, 12), (s_ada, 18)):
                for m in range(chunks):
                    for c in range(KC):
                        ins = pe.matmul(ps[:, 4, n * B:(n + 1) * B], w[:, c, m * P:(m + 1) * P], silu[:, c, :],
                                        start=c == 0, stop=c == KC - 1)
                    n += 1
            ins.then_inc(set_pe, 1)
            pe.wait_ge(s_l1_ld, 13 * 16)
            pe.wait_ge(set_act, 2)
            cond = colT[:, C_COND:C_COND + B * KC].rearrange("p (b c) -> p c b", c=KC)
            for m in range(MC + KC):
                for c in range(KC):
                    w = s_an[:, m // 4, c, m % 4 * P:(m % 4 + 1) * P] if m < MC else s_gan[:, c, (m - MC) * P:(m - MC + 1) * P]
                    ins = pe.matmul(ps[:, 5, m * B:(m + 1) * B], w, cond[:, c, :], start=c == 0, stop=c == KC - 1)
            for b in range(B):
                for c in range(KC):
                    ins = pe.matmul(ps[:, 5, 64 + b * 4:64 + b * 4 + E], s_crep[:, c, b, :], s_ran[:, c, :], start=c == 0, stop=c == KC - 1)
            ins.then_inc(set_pe, 1)
            for i in range(KC):
                for j in range(KC):
                    ins = pe.transpose(ps[:, 6, (j * KC + i) * P:(j * KC + i + 1) * P], s_q1[:, i, j * P:(j + 1) * P], ident[:, :])
            ins.then_inc(set_pe, 1)
            pe.wait_ge(s_kv_ld, 3 * 16)
            pe.wait_ge(set_dve, 3)
            pe.wait_ge(set_act, 3)

            def key(bank, slot, w, m, v):
                for c in range(KC):
                    ins = pe.matmul(ps[:, bank, slot * P:(slot + 1) * P], w[:, c, m * P:(m + 1) * P], s_ctxT[:, v, c, :, 0, :],
                                    start=c == 0, stop=c == KC - 1)
                return ins
            for m in range(KC):
                key(0, m, s_kv0, m, 0)
                key(0, KC + m, s_kvc, m, 1)
                key(1, m, s_kv3, m, 2)
                key(1, KC + m, s_k1, m, 2)
                ins = key(2, m, s_v1, m, 2)
            ins.then_inc(set_pe, 1)
            pe.wait_ge(set_dve, 4)
            for i, (bank, w) in enumerate(((3, s_kv0), (6, s_kvc), (7, s_kv3))):
                for b in range(B):
                    for c in range(KC):
                        ins = pe.matmul(ps[:, bank, b * D:(b + 1) * D], s_ctxT[:, i, c, b, :, :].rearrange("p a s -> p (a s)"),
                                        w[:, c, D:2 * D], start=c == 0, stop=c == KC - 1)
            ins.then_inc(set_pe, 1)
            pe.wait_ge(set_dve, 5)
            for i in range(KC):
                for j in range(KC):
                    ins = pe.matmul(ps[:, 0, i * P:(i + 1) * P], s_wqT[:, j, i * P:(i + 1) * P], s_k1T[:, j, :], start=j == 0, stop=j == KC - 1)
            for b in range(B):
                for c in range(KC):
                    lhsT = s_vT[:, c, b * S:(b + 1) * S]
                    st_, sp_ = c == 0, c == KC - 1
                    pe.matmul(ps[0:S, 0, D + b * 4:D + b * 4 + E], lhsT, s_rev[:, c, :], start=st_, stop=sp_)
            for b in range(B):
                for c in range(KC):
                    lhsT = s_vT[:, c, b * S:(b + 1) * S]
                    pe.matmul(ps[0:S, 1, b * D:(b + 1) * D], lhsT, s_gev[:, c, :], start=c == 0, stop=c == KC - 1)
            pe.wait_ge(set_dve, 6)
            for b in range(B):
                for e in range(E):
                    for c in range(KC):
                        lhsT = s_vT[:, c, b * S:(b + 1) * S]
                        ins = pe.matmul(ps[0:S, 2 + b * E + e, :], lhsT, s_ev[:, e, c, :], start=c == 0, stop=c == KC - 1)
            ins.then_inc(set_pe, 1)

            pe.wait_ge(set_dve, 7)
            pe.wait_ge(rc1_ld, 9 * 16)
            with pe.Fori(0, B) as b:
                def ln(i, k):
                    pe.wait_ge(xhat_ready, b * 2 * N_LN + 2 * i + k + 1)
                    turn_block(k, xhat).then_inc(ln_turned, 1)

                def query(i, k, ln_i, w):
                    pe.wait_ge(hT_ready, b * (2 * N_LN + 2) + ln_i + k + 1)
                    linear(4 * k + 2, w, 0, hT[:, k])
                    linear(4 * k + 3, w, 1, hT[:, k]).then_inc(q_done, 1)

                def residual(i, k, turn, w=None, o_wait=None, src=oT):
                    if not turn:
                        pe.wait_ge(*o_wait)
                        linear(4 * k + 2, w, 0, src[:, k])
                        linear(4 * k + 3, w, 1, src[:, k]).then_inc(y_done, 1)
                    else:
                        pe.wait_ge(yT_ready, b * 2 * N_RES + 2 * i + k + 1)
                        for t in range(TB):
                            for c in range(KC):
                                ins = pe.transpose(ps[:, 4 * k + t // 2, t % 2 * D + c * P:t % 2 * D + (c + 1) * P],
                                                   yT[:, k, c, t * P:(t + 1) * P], ident[:, :])
                        ins.then_inc(y_turned, 1)

                def context_attention(i):
                    u0 = b * N_CA * T + T * i

                    def scores(t):
                        if t % TB == 0:
                            pe.wait_ge(qT_ready, b * 2 * N_Q + 2 * i + t // TB + 1)
                        if t == 0:
                            pe.wait_ge(kblk_ready, b * N_CA + i + 1)
                        if t >= 2:
                            pe.wait_ge(s_read, u0 + t - 1)
                        for c in range(KC):
                            ins = pe.matmul(ps[:, 2 * (t % 2) + c, :], qT[:, t // TB, c, t % TB * P:(t % TB + 1) * P],
                                            kblk[:, c, :, :].rearrange("p h s -> p (h s)"), start=True, stop=True)
                        ins.then_inc(s_ready, 1)

                    def turn(t):
                        pe.wait_ge(p_exp, u0 + t + 1)
                        if t:
                            pe.wait_ge(pT_ready, u0 + t)
                        for j in range(HC):
                            ins = pe.transpose(ps[:, 4 + j // 4, j % 4 * P:(j % 4 + 1) * P], prob[:, t % 2, j * P:(j + 1) * P], ident[:, :])
                        ins.then_inc(p_turned, 1)

                    def values(t):
                        pe.wait_ge(pT_ready, u0 + t + 1)
                        if t == 0:
                            pe.wait_ge(qT_ready, b * 2 * N_Q + 2 * i + 2)
                        else:
                            pe.wait_ge(o_ready, u0 + t)
                        for j in range(HC):
                            ins = pe.matmul(ps[:, 6, 64 * j:64 * (j + 1)], probT[:, t % 2, j, :], vx[:, j, :], start=True, stop=True)
                        ins.then_inc(pv_done, 1)

                    def turn_outputs(t):
                        pe.wait_ge(o_ready, u0 + t + 1)
                        if t:
                            pe.wait_ge(oT_ready, u0 + t)
                        for c in range(KC):
                            ins = pe.transpose(ps[:, 7, t % 2 * D + c * P:t % 2 * D + (c + 1) * P], o_tok[:, t % 2, c * P:(c + 1) * P], ident[:, :])
                        ins.then_inc(o_turned, 1)

                    scores(0)
                    scores(1)
                    for t in range(T + 2):
                        if t + 2 < T:
                            scores(t + 2)
                        if t < T:
                            turn(t)
                        if 1 <= t <= T:
                            values(t - 1)
                        if t >= 2:
                            turn_outputs(t - 2)

                pe.wait_ge(ra_ld, b * N_RA + N_RA)
                pe.wait_ge(begun, b + 1)
                for k in range(NB):
                    ln(0, k)
                for k in range(NB):
                    query(0, k, 0, wq0)
                context_attention(0)
                for k in range(NB):
                    residual(0, k, False, wp0, (oT_ready, b * N_CA * T + TB * k + TB))
                for k in range(NB):
                    residual(0, k, True)

                for k in range(NB):
                    ln(1, k)
                for k in range(NB):
                    pe.wait_ge(hT_ready, b * (2 * N_LN + 2) + 2 + k + 1)
                    for t in range(TB):
                        for c in range(KC):
                            ins = pe.matmul(ps[:, 4 * k + 2, t * S:(t + 1) * S], hT[:, k, c, t * P:(t + 1) * P], kw[:, c, :],
                                            start=c == 0, stop=c == KC - 1)
                    ins.then_inc(p1s_done, 1)
                for k in range(NB):
                    pe.wait_ge(p1_ready, b * NB + k + 1)
                    pe.sem_inc(passed, 1)
                    for t in range(TB):
                        ins = pe.transpose(ps[0:S, 4 * k, t * P:(t + 1) * P], p1[:, k, t, :], ident[:, :])
                    ins.then_inc(p1_turned, 1)
                for k in range(NB):
                    pe.wait_ge(p1T_ready, b * NB + k + 1)
                    for t in range(TB):
                        for c in range(KC):
                            pe.matmul(ps[:, 4 * k + 3, t * 4:t * 4 + E], hT[:, k, c, t * P:(t + 1) * P], wr[:, c, :], start=c == 0, stop=False)
                        ins = pe.matmul(ps[:, 4 * k + 3, t * 4:t * 4 + E], p1T[:, k, t * P:(t + 1) * P], vw[:, MC * P + D:MC * P + D + E], start=False, stop=True)
                    ins.then_inc(lg_done, 1)
                for k in range(NB):
                    for m in range(KC):
                        for c in range(KC):
                            pe.matmul(ps[:, 4 * k + 1 + m, :], wg1[:, c, m * P:(m + 1) * P], hT[:, k, c, :], start=c == 0, stop=False)
                        ins = pe.matmul(ps[:, 4 * k + 1 + m, :], vw[:, (MC + m) * P:(MC + m + 1) * P], p1T[:, k, :], start=False, stop=True)
                    ins.then_inc(g1_done, 1)
                for k in range(NB):
                    pe.wait_ge(lg_ready, b * NB + k + 1)
                    pe.sem_inc(passed, 1)
                    for t in range(TB):
                        ins = pe.transpose(ps[0:E, 4 * k + 3, t * P:(t + 1) * P], lg[:, k, t, :], ident[:, :])
                    ins.then_inc(lg_turned, 1)
                for k in range(NB):
                    pe.wait_ge(g1_ready, b * NB + k + 1)
                    for m in range(KC):
                        ins = linear(4 * k + 1 + m, wg2, m, g1[k])
                    ins.then_inc(g2_done, 1)
                for k in range(NB):
                    pe.wait_ge(pT_made, b * NB + k + 1)
                    pe.wait_ge(gT_ready, b * NB + k + 1)
                    for e in range(E):
                        ins = pe.matmul(ps[:, 4 * k + e, :], sel3[:, e, :], pT[:, k, :], start=True, stop=True)
                    ins.then_inc(pbc_done, 1)
                n0 = b * 2 * MC
                for k in range(NB):
                    pe.wait_ge(pbc_ready, b * NB + NB)
                    for m in range(KC):
                        pe.matmul(ps[:, 4 + 2 * k + m, :], b2[:, m * P:(m + 1) * P], pT[:, k, :], start=True, stop=False)
                    for m in range(MC + 2):
                        n = k * MC + m
                        if m < MC:
                            if n >= 4:
                                pe.wait_ge(h1_act, n0 + n - 3)
                            bank = n % 4
                            for c in range(KC):
                                pe.matmul(ps[:, bank, :], w1[:, m // 4, c, m % 4 * P:(m % 4 + 1) * P], hT[:, k, c, :], start=c == 0, stop=False)
                            pe.matmul(ps[:, bank, :], vw[:, m * P:(m + 1) * P], p1T[:, k, :], start=False, stop=True).then_inc(h1_done, 1)
                        if m >= 2:
                            pe.wait_ge(h1_ready, n0 + n - 1)
                            for j in range(KC):
                                ins = pe.matmul(ps[:, 4 + 2 * k + j, :], w2[:, m - 2, j * P:(j + 1) * P], ring[:, (n - 2) % 4, :],
                                                start=False, stop=m == MC + 1)
                            ins.then_inc(w2_done, 1)
                for k in range(NB):
                    pe.wait_ge(rT_ready, b * NB + k + 1)
                    for m in range(KC):
                        ins = linear((2, 4)[k] + m, wout, m, rT[k])
                    ins.then_inc(y_done, 1)
                for k in range(NB):
                    residual(1, k, True)

                for k in range(NB):
                    ln(2, k)
                for k in range(NB):
                    pe.wait_ge(hT_ready, b * (2 * N_LN + 2) + 4 + k + 1)
                    for t in range(TB):
                        for c in range(KC):
                            ins = pe.matmul(ps[:, 4 * k + 2 + t // 2, t % 2 * D:(t % 2 + 1) * D], hT[:, k, c, t * P:(t + 1) * P],
                                            wv2[:, c, :], start=c == 0, stop=c == KC - 1)
                    ins.then_inc(v_done, 1)
                pe.wait_ge(v_ready, b * NB + NB)
                pe.wait_ge(v2_clear, b + 1)
                uses, read_by = [0, 0], [None, None]

                def take(sem, n):
                    place = uses[0] % 2
                    uses[0] += 1
                    if read_by[place]:
                        pe.wait_ge(*read_by[place])
                    read_by[place] = sem, n
                    return 2 * place

                def take_dve():
                    uses[1] += 1
                    return take(ring_read, b * N_SCORE + uses[1])

                def take_act():
                    return take(spread_read, b * N_SPREAD + uses[0] - uses[1] + 1)

                def queries_keys(c, qk):
                    bank = take_dve()
                    for k in range(NB):
                        ins = linear(bank + k, wqk2, qk * KC + c, hT[:, k])
                    ins.then_inc(ring_ready, 1)

                def spread(p, qk):
                    bank = take_act()
                    for half in range(2):
                        for part in range(2):
                            ins = pe.matmul(ps[:, bank + half, :], sel[:, p % 4, 2 * qk + part, :],
                                            dense[2 * qk + part][:, half * 512:(half + 1) * 512], start=part == 0, stop=part == 1)
                    ins.then_inc(ring_ready, 1)

                def query_scores(p, u):
                    e, t = u // T, u % T
                    r = slice(64 * e, 64 * e + 64)
                    bank = take_dve()
                    for half in range(2):
                        ins = pe.matmul(ps[:, bank + half, :], qx[r, p % 4, t * P:(t + 1) * P], kx[r, p % 4, half * 512:(half + 1) * 512],
                                        start=True, stop=True)
                    ins.then_inc(ring_ready, 1)

                def turn_maxima(p):
                    bank = take_dve()
                    pe.wait_ge(mt_ready, b * NP + p + 1)
                    for t in range(T):
                        ins = pe.transpose(ps[:, bank + t // TB, t % TB * P:(t % TB + 1) * P], mt[:, t, :], ident[:, :])
                    ins.then_inc(ring_ready, 1)

                def key_scores(p, u, half):
                    kc, e = u // 2, u % 2
                    r = slice(64 * e, 64 * e + 64)
                    n = 2 * (2 * T * p + u) + half
                    if n >= 3:
                        pe.wait_ge(pt_ready, b * 4 * T * NP + n - 2)
                    pe.matmul(ps[:, 4 + n % 3, :], kx[r, p % 4, kc * P:(kc + 1) * P], qx[r, p % 4, half * 512:(half + 1) * 512],
                              start=True, stop=True).then_inc(st_ready, 1)

                def weigh_values(w):
                    p, kc = w // T, w % T
                    pe.wait_ge(pt_ready, b * 4 * T * NP + 4 * w + 4)
                    if kc == 0 and p >= 1:
                        pe.wait_ge(acc_read, b * NP + p)
                    for e in range(2):
                        for half in range(2):
                            o = 32 * (2 * e + half)
                            ins = pe.matmul(ps[o:o + 32, 7, :], v2[:, kc, VS * (2 * p + e):VS * (2 * p + e) + 32],
                                            pt[:, (2 * kc + e) % 8, half * 512:(half + 1) * 512], start=kc == 0, stop=kc == T - 1)
                    ins.then_inc(pv2_done, 1)

                def finish(p):
                    bank = take_dve()
                    pe.wait_ge(acc_read, b * NP + p + 1)
                    for j in range(TB):
                        ins = pe.transpose(ps[:, bank, j * P:(j + 1) * P], accS[:, p % 2, j * P:(j + 1) * P], ident[:, :])
                    ins.then_inc(ring_ready, 1)

                for qk in range(2):
                    queries_keys(0, qk)
                pe.wait_ge(ring_read, b * N_SCORE + 2)
                for qk in range(2):
                    spread(0, qk)
                with_maximum = []
                for n in range(-LEAD, UNITS):
                    (p, u), m = divmod(n, 2 * T), n + LEAD
                    if n >= 0:
                        if u == 0:
                            pe.wait_ge(ring_read, b * N_SCORE + with_maximum[p])
                        key_scores(p, u, 0)
                    if m < UNITS:
                        if m % (2 * T) == 0:
                            pe.wait_ge(spread_read, b * N_SPREAD + 2 * (m // (2 * T)) + 2)
                        query_scores(m // (2 * T), m % (2 * T))
                    if n >= 0:
                        key_scores(p, u, 1)
                    if n >= 3 and n % 2:
                        weigh_values((n - 3) // 2)
                    q, at_m = divmod(m, 2 * T)
                    if at_m == 2 and 1 <= q <= NP:
                        turn_maxima(q - 1)
                        with_maximum.append(uses[1])
                    if at_m in (7, 9) and q + 1 < NP:
                        if q + 1 == NP // 2 and at_m == 7:
                            pe.wait_ge(ring_read, b * N_SCORE + second)
                        spread(q + 1, (at_m - 7) // 2)
                    if q + 1 == NP // 2 - 1 and at_m in (11, 13):
                        queries_keys(1, (at_m - 11) // 2)
                        second = uses[1]
                    if u == 5 and p >= 1:
                        finish(p - 1)
                weigh_values(T * NP - 1)
                finish(NP - 1)
                assert uses == [N_RING, N_SCORE]

                for k in range(NB):
                    pe.wait_ge(ring_read, b * N_SCORE + N_SCORE)
                    turn_block(k, xhat).then_inc(ot_turned, 1)
                for k in range(NB):
                    residual(2, k, False, wproj, (hT_ready, b * (2 * N_LN + 2) + 6 + k + 1), hT)
                for k in range(NB):
                    residual(2, k, True)

                for k in range(NB):
                    ln(3, k)
                for k in range(NB):
                    query(1, k, 8, wqc)
                context_attention(1)
                for k in range(NB):
                    residual(3, k, False, wcp, (oT_ready, b * N_CA * T + T + TB * k + TB))
                for k in range(NB):
                    residual(3, k, True)

                for k in range(NB):
                    ln(4, k)
                n0 = b * 2 * NC_HID
                for k in range(NB):
                    pe.wait_ge(hT_ready, b * (2 * N_LN + 2) + 10 + k + 1)
                    if k == 0:
                        pe.wait_ge(hT_ready, b * (2 * N_LN + 2) + 10 + 2)
                    for m in range(NC_HID + 2):
                        n = k * NC_HID + m
                        if m < NC_HID:
                            if n >= 4:
                                pe.wait_ge(h2_ready, n0 + n - 3)
                            linear(n % 4, wm1, m, hT[:, k]).then_inc(h2_done, 1)
                        if m >= 2:
                            pe.wait_ge(h2_ready, n0 + n - 1)
                            for j in range(KC):
                                ins = pe.matmul(ps[:, 4 + 2 * k + j, :], wm2[:, m - 2, j * P:(j + 1) * P], ring[:, (n - 2) % 4, :],
                                                start=m == 2, stop=m == NC_HID + 1)
                            ins.then_inc(w22_done, 1)
                for k in range(NB):
                    residual(4, k, True)

                for k in range(NB):
                    ln(5, k)
                for k in range(NB):
                    pe.wait_ge(hT_ready, b * (2 * N_LN + 2) + 12 + k + 1)
                    for m in range(2 * KC):
                        ins = linear(4 * k + m, wqkv3, m, hT[:, k])
                    ins.then_inc(qk3_done, 1)
                for k in range(NB):
                    pe.wait_ge(qk3_ready, b * NB + k + 1)
                    for t in range(TB):
                        for c in range(KC):
                            ins = pe.matmul(ps[:, 4 * k + t // 2, t % 2 * D:(t % 2 + 1) * D], hT[:, k, c, t * P:(t + 1) * P],
                                            wqkv3[:, c, 2 * D:3 * D], start=c == 0, stop=c == KC - 1)
                    ins.then_inc(v3_done, 1)
                u0 = b * N_UNIT

                def window_scores(u):
                    t, c = u // KC, u % KC
                    pe.wait_ge(wk_ready, u0 + u + 1)
                    if u == 0:
                        pe.wait_ge(v3_ready, b * NB + NB)
                        pe.wait_ge(v3_clear, b + 1)
                    if u >= 2:
                        pe.wait_ge(ws_read, u0 + u - 1)
                    for half in range(2):
                        ins = pe.matmul(ps[:, 2 * (u % 2) + half, :], qT[:, t // TB, c, t % TB * P:(t % TB + 1) * P],
                                        wkblk[:, u % 2, 4 * half:4 * half + 4, :].rearrange("p h s -> p (h s)"), start=True, stop=True)
                    ins.then_inc(ws_ready, 1)

                def window_turn(u):
                    pe.wait_ge(wp_exp, u0 + u + 1)
                    if u:
                        pe.wait_ge(wpT_ready, u0 + u)
                    for j in range(HC):
                        ins = pe.transpose(ps[:, 4 + j // 4, j % 4 * P:(j % 4 + 1) * P], prob[:, u % 2, j * P:(j + 1) * P], ident[:, :])
                    ins.then_inc(wp_turned, 1)

                def window_values(u):
                    t, c = u // KC, u % KC
                    pe.wait_ge(wpT_ready, u0 + u + 1)
                    if u >= 2:
                        pe.wait_ge(wo_ready, u0 + u - 1)
                    for part in range(2):
                        for odd in range(2):
                            for j in range(4):
                                h = 2 * j + odd
                                lhsT = v3[:, t, HC * c + h, :] if part == 0 else ones_win[:, odd, :]
                                ins = pe.matmul(ps[32 * j:32 * j + 32, 6 + u % 2, part * P:(part + 1) * P], lhsT, wprobT[:, u % 2, h, :],
                                                start=odd == 0, stop=odd == 1)
                    ins.then_inc(wpv_done, 1)

                window_scores(0)
                window_scores(1)
                window_turn(0)
                for u in range(N_UNIT):
                    if u + 2 < N_UNIT:
                        window_scores(u + 2)
                    window_values(u)
                    if u + 1 < N_UNIT:
                        window_turn(u + 1)
                for k in range(NB):
                    residual(5, k, False, wso, (wo_ready, u0 + N_UNIT))
                for k in range(NB):
                    residual(5, k, True)

                for k in range(NB):
                    ln(6, k)
                for k in range(NB):
                    query(2, k, 14, wq3)
                context_attention(2)
                for k in range(NB):
                    residual(6, k, False, wco, (oT_ready, b * N_CA * T + 2 * T + TB * k + TB))
                for k in range(NB):
                    residual(6, k, True)

                for k in range(NB):
                    ln(7, k)
                pe.wait_ge(rc2_ld, b * 32 + 32)
                n0 = b * 2 * NC_HID
                for k in range(NB):
                    pe.wait_ge(hT_ready, b * (2 * N_LN + 2) + 16 + k + 1)
                    if k == 0:
                        pe.wait_ge(hT_ready, b * (2 * N_LN + 2) + 16 + 2)
                    for m in range(NC_HID + 1):
                        n = k * NC_HID + m
                        if m < NC_HID:
                            if n >= 2:
                                pe.wait_ge(h3_ready, n0 + n - 1)
                            linear(2 * (n % 2), w3a, m, hT[:, k])
                            linear(2 * (n % 2) + 1, w3a, NC_HID + m, hT[:, k]).then_inc(h3_done, 1)
                        if m >= 1:
                            pe.wait_ge(h3_ready, n0 + n)
                            for j in range(KC):
                                ins = pe.matmul(ps[:, 4 + 2 * k + j, :], w3b[:, m - 1, j * P:(j + 1) * P], ring[:, (n - 1) % 4, :],
                                                start=m == 1, stop=m == NC_HID)
                            ins.then_inc(w32_done, 1)
                for k in range(NB):
                    residual(7, k, True)

        @block.scalar
        def _(act):
            def affine(dst, src, scale, bias):
                return act.activation(dst, src, ACT.Identity, bias=bias, scale=scale)

            act.wait_ge(set_dve, 2)
            act.activation(s_silu[:, :], colT[:, C_COND:C_COND + B * KC], ACT.Silu).then_inc(set_act, 1)
            for bb in range(B):
                for c in range(KC):
                    col = C_COND + bb * KC + c
                    ins = act.activation(s_crep[:, c, bb, :], colT[:, col:col + 1].broadcast_to([P, P]), ACT.Copy)
            ins.then_inc(set_act, 1)
            act.wait_ge(set_pe, 2)
            for v in (1, 2):
                for c in range(KC):
                    for dup in range(2):
                        ins = act.activation(s_ctxT[:, v, c, :, dup, :], ps[:, 1 + v, c * P:(c + 1) * P].rearrange("p (b s) -> p b s", b=B), ACT.Copy)
            ins.then_inc(set_act, 1)
            act.wait_ge(set_pe, 8)
            for bb in range(B):
                for e in range(E):
                    act.activation(vw2[:, bb, e * RH:(e + 1) * RH], ps[0:S, 2 + bb * E + e, :], ACT.Copy)
                act.activation(vw2[:, bb, MC * P:MC * P + D], ps[0:S, 1, bb * D:(bb + 1) * D], ACT.Copy)
            act.wait_ge(set_dve, 7)
            for bb in range(B):
                ins = act.activation(vw2[:, bb, MC * P + D:MC * P + D + E], ps[0:S, 0, D + bb * 4:D + bb * 4 + E], ACT.Copy)
            ins.then_inc(set_act, 1)

            with act.Fori(0, B) as b:
                act.wait_ge(begun, b + 1)

                def ln(i, k, cols):
                    act.wait_ge(ln_turned, b * 2 * N_LN + 2 * i + k + 1)
                    for c in range(KC):
                        if cols is None:
                            ins = act.activation(hT[:, k, c, :], ps[:, 4 * k + c, :], ACT.Copy)
                        else:
                            table, scale, bias = cols
                            ins = affine(hT[:, k, c, :], ps[:, 4 * k + c, :], table[:, scale + c:scale + c + 1], table[:, bias + c:bias + c + 1])
                    ins.then_inc(hT_ready, 1)

                def query(i, k, col):
                    act.wait_ge(q_done, b * 2 * N_Q + 2 * i + k + 1)
                    for c in range(KC):
                        ins = affine(qT[:, k, c, :], ps[:, 4 * k + 2 + c, :], 1.0, colT[:, col + c:col + c + 1])
                    ins.then_inc(qT_ready, 1)

                def residual(k, bank, scale, bias):
                    for c in range(KC):
                        ins = affine(yT[:, k, c, :], ps[:, bank + c, :], 1.0 if scale is None else mod[:, scale + c:scale + c + 1],
                                     bias[:, c:c + 1])
                    ins.then_inc(yT_ready, 1)

                def context_attention(i):
                    u0 = b * N_CA * T + T * i

                    def exp(t):
                        act.wait_ge(s_read, u0 + t + 1)
                        act.activation(prob[:, t % 2, :], prob[:, t % 2, :], ACT.Exp, scale=QK_SCALE).then_inc(top_exp if i == 2 else p_exp, 1)

                    def copy(t):
                        act.wait_ge(p_turned, u0 + t + 1)
                        if t >= 2:
                            act.wait_ge(pv_done, u0 + t - 1)
                        act.activation(probT[:, t % 2, :, :], ps[:, 4:6, :].rearrange("p a (j q) -> p (a j) q", q=P), ACT.Copy).then_inc(pT_ready, 1)

                    def outputs(t):
                        act.wait_ge(o_turned, u0 + t + 1)
                        act.activation(oT[:, t // TB, :, t % TB * P:(t % TB + 1) * P], ps[:, 7, t % 2 * D:(t % 2 + 1) * D].rearrange("p (c q) -> p c q", c=KC),
                                       ACT.Copy).then_inc(oT_ready, 1)
                    exp(0)
                    for t in range(T + 2):
                        if t + 1 < T:
                            exp(t + 1)
                        if t < T:
                            copy(t)
                        if t >= 2:
                            outputs(t - 2)

                for k in range(NB):
                    ln(0, k, (mod, M_SC_Q, M_SH_Q))
                for k in range(NB):
                    query(0, k, C_BQ0)
                context_attention(0)
                for k in range(NB):
                    act.wait_ge(y_done, b * 12 + k + 1)
                    residual(k, 4 * k + 2, None, colT[:, C_BP0:C_BP0 + KC])

                for k in range(NB):
                    ln(1, k, (colT, C_GAMMA, C_BETA))
                for k in range(NB):
                    act.wait_ge(p1_sub, b * NB + k + 1)
                    act.activation(p1[:, k, :, :], p1[:, k, :, :], ACT.Exp, scale=L1_SCALE).then_inc(p1_exp, 1)
                for k in range(NB):
                    act.wait_ge(p1_turned, b * NB + k + 1)
                    act.activation(p1T[:, k, :], ps[0:S, 4 * k, :], ACT.Copy).then_inc(p1T_ready, 1)
                for k in range(NB):
                    act.wait_ge(lg_sub, b * NB + k + 1)
                    act.activation(lg[:, k, :, :], lg[:, k, :, :], ACT.Exp).then_inc(lg_exp, 1)
                for k in range(NB):
                    act.wait_ge(g1_done, b * NB + k + 1)
                    for m in range(KC):
                        ins = act.activation(g1[k][:, m, :], ps[:, 4 * k + 1 + m, :], ACT.Silu, bias=mod[:, M_HB + MC + m:M_HB + MC + m + 1])
                    ins.then_inc(g1_ready, 1)
                for k in range(NB):
                    act.wait_ge(lg_turned, b * NB + k + 1)
                    act.activation(pT[:, k, :], ps[0:E, 4 * k + 3, :], ACT.Copy).then_inc(pT_made, 1)
                for k in range(NB):
                    act.wait_ge(g2_done, b * NB + k + 1)
                    for m in range(KC):
                        ins = act.activation(gT[:, k, m, :], ps[:, 4 * k + 1 + m, :], ACT.Sigmoid, bias=colT[:, C_GB2 + m:C_GB2 + m + 1])
                    ins.then_inc(gT_ready, 1)
                for k in range(NB):
                    act.wait_ge(pbc_done, b * NB + k + 1)
                    for e in range(E):
                        ins = act.activation(p_bc[:, k, e, :], ps[:, 4 * k + e, :], ACT.Copy)
                    ins.then_inc(pbc_ready, 1)
                n0 = b * NB * MC

                def routed(k):
                    act.wait_ge(w2_done, n0 + k * MC + MC)
                    for c in range(KC):
                        ins = act.activation(rT[k][:, c, :], ps[:, 4 + 2 * k + c, :], ACT.Copy)
                    ins.then_inc(rT_ready, 1)
                for n in range(NB * MC):
                    act.wait_ge(h1_done, n0 + n + 1)
                    if n >= 4:
                        act.wait_ge(w2_done, n0 + n - 3)
                    m = n % MC
                    act.activation(ring[:, n % 4, :], ps[:, n % 4, :], ACT.Silu, bias=mod[:, M_HB + m:M_HB + m + 1]).then_inc(h1_act, 1)
                    if n == MC + 1:
                        routed(0)
                routed(1)

                for k in range(NB):
                    ln(2, k, (mod, M_SC_A, M_SH_A))
                u0 = b * N_RING
                uses = [0]

                def place():
                    n = uses[0]
                    uses[0] += 1
                    act.wait_ge(ring_ready, u0 + n + 1)
                    return ps[:, 2 * (n % 2):2 * (n % 2) + 2, :].rearrange("p a q -> p (a q)")

                def high_parts(c, qk):
                    col = (C_BQ2, C_BK2)[qk] + c
                    affine(dense[2 * qk][:, :], place(), 1.0, colT[:, col:col + 1]).then_inc(hi_ready, 1)

                def spread(p, qk):
                    if qk == 0:
                        act.activation(qx[:, p % 4, :], place(), ACT.Copy).then_inc(spread_read, 1)
                    else:
                        affine(kx[:, p % 4, :], place(), 1.0, k_aug[:, 0:1]).then_inc(spread_read, 1)

                def probabilities(p, u):
                    for half in range(2):
                        n = 2 * (2 * T * p + u) + half
                        act.wait_ge(st_ready, b * 4 * T * NP + n + 1)
                        if u % 2 == 0 and half == 0 and n >= 16:
                            act.wait_ge(pv2_done, b * T * NP + n // 4 - 3)
                        act.activation(pt[:, u % 8, half * 512:(half + 1) * 512], ps[:, 4 + n % 3, :], ACT.Exp, scale=QK_SCALE).then_inc(pt_ready, 1)

                def outputs(p):
                    act.wait_ge(pv2_done, b * T * NP + T * p + T)
                    if p >= 2:
                        act.wait_ge(ring_ready, u0 + turned[p - 2])
                    act.activation(accS[:, p % 2, :], ps[:, 7, :], ACT.Copy).then_inc(acc_read, 1)

                for qk in range(2):
                    high_parts(0, qk)
                for qk in range(2):
                    spread(0, qk)
                turned = []
                for n in range(-LEAD, UNITS):
                    (p, u), m = divmod(n, 2 * T), n + LEAD
                    if n >= 0:
                        probabilities(p, u)
                    if m < UNITS:
                        uses[0] += 1
                    if u == 2 and p >= 1:
                        outputs(p - 1)
                    q, at_m = divmod(m, 2 * T)
                    if at_m == 2 and 1 <= q <= NP:
                        uses[0] += 1
                    if at_m in (7, 9) and q + 1 < NP:
                        spread(q + 1, (at_m - 7) // 2)
                    if q + 1 == NP // 2 - 1 and at_m in (11, 13):
                        high_parts(1, (at_m - 11) // 2)
                    if u == 5 and p >= 1:
                        uses[0] += 1
                        turned.append(uses[0])
                outputs(NP - 1)
                for k in range(NB):
                    act.wait_ge(ot_turned, b * NB + k + 1)
                    for c in range(KC):
                        ins = act.activation(hT[:, k, c, :], ps[:, 4 * k + c, :], ACT.Copy)
                    ins.then_inc(hT_ready, 1)
                for k in range(NB):
                    act.wait_ge(y_done, b * 12 + 4 + k + 1)
                    residual(k, 4 * k + 2, M_G_A, mod[:, M_BG:M_BG + KC])

                for k in range(NB):
                    ln(3, k, None)
                for k in range(NB):
                    query(1, k, C_BQC)
                context_attention(1)
                for k in range(NB):
                    act.wait_ge(y_done, b * 12 + 6 + k + 1)
                    residual(k, 4 * k + 2, None, colT[:, C_BCP:C_BCP + KC])

                for k in range(NB):
                    ln(4, k, (mod, M_SC_M, M_SH_M))
                n0 = b * NB * NC_HID

                def mlp_out(done, k, scale, bias):
                    act.wait_ge(done, n0 + k * NC_HID + NC_HID)
                    residual(k, 4 + 2 * k, scale, bias)
                for n in range(NB * NC_HID):
                    act.wait_ge(h2_done, n0 + n + 1)
                    if n >= 4:
                        act.wait_ge(w22_done, n0 + n - 3)
                    m = n % NC_HID
                    act.activation(ring[:, n % 4, :], ps[:, n % 4, :], ACT.Gelu_apprx_tanh, bias=colT[:, C_BM1 + m:C_BM1 + m + 1]).then_inc(h2_ready, 1)
                    if n == NC_HID + 1:
                        mlp_out(w22_done, 0, M_G_M, mod[:, M_BG + 2:M_BG + 2 + KC])
                mlp_out(w22_done, 1, M_G_M, mod[:, M_BG + 2:M_BG + 2 + KC])

                for k in range(NB):
                    ln(5, k, (mod, M3_SC_SA, M3_SH_SA))
                for k in range(NB):
                    act.wait_ge(qk3_done, b * NB + k + 1)
                    for m in range(KC):
                        affine(qT[:, k, m, :], ps[:, 4 * k + m, :], 1.0, colT[:, C_BQ3 + m:C_BQ3 + m + 1])
                    for m in range(KC):
                        ins = affine(kT3[:, k, m, :], ps[:, 4 * k + KC + m, :], 1.0, colT[:, C_BK3 + m:C_BK3 + m + 1])
                    ins.then_inc(qk3_ready, 1)
                u0 = b * N_UNIT

                def window_exp(u):
                    act.wait_ge(ws_read, u0 + u + 1)
                    act.activation(prob[:, u % 2, :], prob[:, u % 2, :], ACT.Exp, scale=QK_SCALE).then_inc(wp_exp, 1)

                def window_copy(u):
                    act.wait_ge(wp_turned, u0 + u + 1)
                    if u >= 2:
                        act.wait_ge(wpv_done, u0 + u - 1)
                    act.activation(wprobT[:, u % 2, :, :], ps[:, 4:6, :].rearrange("p a (j q) -> p (a j) q", q=P), ACT.Copy).then_inc(wpT_ready, 1)
                window_exp(0)
                window_exp(1)
                window_copy(0)
                for u in range(N_UNIT):
                    if u + 2 < N_UNIT:
                        window_exp(u + 2)
                    if u + 1 < N_UNIT:
                        window_copy(u + 1)
                for k in range(NB):
                    act.wait_ge(y_done, b * 12 + 8 + k + 1)
                    residual(k, 4 * k + 2, M3_G_SA, mod[:, M_BG + 4:M_BG + 4 + KC])

                for k in range(NB):
                    ln(6, k, (mod, M3_SC_CA, M3_SH_CA))
                for k in range(NB):
                    query(2, k, C_BQ3C)
                context_attention(2)
                for k in range(NB):
                    act.wait_ge(y_done, b * 12 + 10 + k + 1)
                    residual(k, 4 * k + 2, M3_G_CA, mod[:, M_BG + 6:M_BG + 6 + KC])

                for k in range(NB):
                    ln(7, k, (mod, M3_SC_ML, M3_SH_ML))
                for n in range(NB * NC_HID):
                    act.wait_ge(h3_done, n0 + n + 1)
                    if n >= 4:
                        act.wait_ge(w32_done, n0 + n - 3)
                    m = n % NC_HID
                    act.activation(ring[:, n % 4, :], ps[:, 2 * (n % 2), :], ACT.Silu, bias=colT[:, C_BM13 + m:C_BM13 + m + 1]).then_inc(h3_act, 1)
                    if n == NC_HID + 1:
                        mlp_out(w32_done, 0, M3_G_ML, mod[:, M_BG + 8:M_BG + 8 + KC])
                mlp_out(w32_done, 1, M3_G_ML, mod[:, M_BG + 8:M_BG + 8 + KC])

        @block.vector
        def _(dve):
            steps = [0]

            def link(ins):
                steps[0] += 1
                ins.then_inc(dve_step, 1)
                dve.wait_ge(dve_step, steps[0])

            dve.wait_ge(ctx_ld, 16)
            link(dve.bn_stats(s_st[:, 0:6], s_ctx[:, :]))
            link(dve.bn_aggr(s_st[:, 6:8], s_st[:, 0:6]))
            dve.tensor_scalar(s_st[:, 8:9], s_st[:, 7:8], EPS5, None, ALU.add)
            dve.tensor_scalar(s_st[:, 9:10], s_st[:, 7:8], EPS6, None, ALU.add).then_inc(ctx_var, 1)
            dve.wait_ge(ctx_rstd, 1)
            for v in range(2):
                dve.tensor_scalar(s_xh[:, v, :], s_ctx[:, :], s_st[:, 6:7], s_st[:, 10 + v:11 + v], ALU.subtract, ALU.mult)
            dve.tensor_copy(s_xh[:, 2, :], s_ctx[:, :]).then_inc(set_dve, 1)
            dve.wait_ge(set_pe, 1)
            dve.tensor_copy(colT[:, :], ps[:, 0, 0:N_COL]).then_inc(set_dve, 1)
            dve.wait_ge(consts_ld, 14 * 16)
            dve.tensor_copy(sel[:, :, :, :], s_sel[:, :, :, :])
            link(dve.memset(v_ctx2[:, :, :, :, :], 0.0))
            dve.wait_ge(set_dve, 2)
            dve.wait_ge(set_pe, 3)
            link(dve.tensor_tensor(mod2[:, :, 0:N_MOD], ps[:, 4, 0:N_MOD * B].rearrange("p (n b) -> p b n", b=B),
                                   colT[:, 0:N_MOD].unsqueeze(1).broadcast_to([P, B, N_MOD]), ALU.add))
            for m in SCALES:
                ins = dve.tensor_scalar(mod2[:, :, m:m + KC], mod2[:, :, m:m + KC], 1.0, None, ALU.add)
            for i, m in enumerate(GATED):
                o = M_BG + KC * i
                ins = dve.tensor_tensor(mod2[:, :, o:o + KC], mod2[:, :, m:m + KC],
                                        colT[:, o:o + KC].unsqueeze(1).broadcast_to([P, B, KC]), ALU.mult)
            link(ins)
            dve.wait_ge(set_pe, 2)
            for c in range(KC):
                for b in range(B):
                    for dup in range(2):
                        ins = dve.tensor_scalar(s_ctxT[:, 0, c, b, dup, :], ps[:, 1, c * P + b * S:c * P + (b + 1) * S],
                                                mod2[:, b, M_SC_KV + c:M_SC_KV + c + 1], mod2[:, b, M_SH_KV + c:M_SH_KV + c + 1], ALU.mult, ALU.add)
            ins.then_inc(set_dve, 1)
            dve.wait_ge(set_pe, 4)
            dve.tensor_tensor(mod2[:, :, M_HB:N_MC], ps[:, 5, 0:(N_MC - M_HB) * B].rearrange("p (n b) -> p b n", b=B),
                              colT[:, M_HB:N_MC].unsqueeze(1).broadcast_to([P, B, N_MC - M_HB]), ALU.add)
            for b in range(B):
                dve.tensor_tensor(rc2[:, b, :], ps[:, 5, 64 + 4 * b:64 + 4 * b + E], rb[:, :], ALU.add)
            dve.wait_ge(set_pe, 5)
            dve.tensor_copy(s_wqT[:, :, :].rearrange("p j i -> p (j i)"), ps[:, 6, :]).then_inc(set_dve, 1)
            dve.wait_ge(set_pe, 6)
            for m in range(KC):
                for i, (bank, slot, col) in enumerate(((0, m, C_BK0), (0, KC + m, C_BKC), (1, m, C_BK3C))):
                    dve.tensor_scalar(kT2[:, i, m, :, :], ps[:, bank, slot * P:(slot + 1) * P].rearrange("p (b s) -> p b s", b=B),
                                      colT[:, col + m:col + m + 1], None, ALU.add)
                dve.tensor_copy(s_k1T[:, m, :], ps[:, 1, (KC + m) * P:(KC + m + 1) * P])
                ins = dve.tensor_copy(s_vT[:, m, :], ps[:, 2, m * P:(m + 1) * P])
            ins.then_inc(set_dve, 1)
            dve.wait_ge(set_pe, 7)
            for i, bank in enumerate((3, 6, 7)):
                for b in range(B):
                    for odd in range(2):
                        r = slice(S * odd, S * odd + S)
                        ins = dve.tensor_tensor(v_ctx2[r, b, i, :, HD * odd:HD * odd + HD],
                                                ps[r, bank, b * D:(b + 1) * D].rearrange("p (j c) -> p j c", c=2 * HD)[:, :, HD * odd:HD * odd + HD],
                                                s_vb[r, i, :].rearrange("p (j c) -> p j c", c=2 * HD)[:, :, HD * odd:HD * odd + HD], ALU.add)
            ins.then_inc(set_dve, 1)
            dve.wait_ge(set_pe, 8)
            dve.tensor_copy(kw2[:, :, :, :].rearrange("p i b s -> p i (b s)"), ps[:, 0, 0:KC * P].rearrange("p (i n) -> p i n", i=KC)).then_inc(set_dve, 1)
            dve.wait_ge(set_dve, 7)
            dve.wait_ge(set_act, 4)
            dve.wait_ge(dve_step, steps[0])

            with dve.Fori(0, B) as b:
                dve.sem_clear(dve_step)
                steps[0] = 0
                dve.tensor_copy(mod[:, :], mod2[:, b, :])
                dve.tensor_copy(v_ctx[:, :, :, :], v_ctx2[:, b, :, :, :])
                dve.tensor_copy(kT[:, :, :, :], kT2[:, :, :, b, :])
                dve.tensor_copy(kw[:, :, :], kw2[:, :, b, :])
                dve.tensor_copy(rc[:, :], rc2[:, b, :])
                dve.tensor_copy(vw[:, :], vw2[:, b, :]).then_inc(begun, 1)
                dve.wait_ge(begun, b + 1)

                def statistics(i, k):
                    for t in range(TB):
                        ins = dve.bn_stats(st[:, k, t, :], x[:, TB * k + t, :])
                    link(ins)
                    for t in range(TB):
                        ins = dve.bn_aggr(mv[:, k, t, :], st[:, k, t, :])
                    link(ins)
                    dve.tensor_scalar(ve[:, k, :], mv[:, k, :, 1], EPS5 if i < 2 else EPS6, None, ALU.add).then_inc(ve_ready, 1)

                def normalise(i, k):
                    dve.wait_ge(rstd_ready, b * 2 * N_LN + 2 * i + k + 1)
                    for t in range(TB):
                        ins = dve.tensor_scalar(xhat[:, TB * k + t, :], x[:, TB * k + t, :], mv[:, k, t, 0:1], rstd[:, k, t:t + 1], ALU.subtract, ALU.mult)
                    ins.then_inc(xhat_ready, 1)

                def residual(i, k):
                    dve.wait_ge(y_turned, b * 2 * N_RES + 2 * i + k + 1)
                    return dve.tensor_tensor(x[:, TB * k:TB * (k + 1), :].rearrange("p t d -> p (t d)"),
                                             x[:, TB * k:TB * (k + 1), :].rearrange("p t d -> p (t d)"),
                                             ps[:, 4 * k:4 * k + 2, :].rearrange("p a n -> p (a n)"), ALU.add)

                def residual_norm(i):
                    link(residual(i, 0))
                    statistics(i + 1, 0)
                    link(residual(i, 1))
                    normalise(i + 1, 0)
                    statistics(i + 1, 1)
                    normalise(i + 1, 1)

                def build_keys(i):
                    for c in range(KC):
                        dve.tensor_tensor(kblk[:, c, :, :], kT[:, i, c, :].unsqueeze(1).broadcast_to([P, HC, S]),
                                                head_mask[:, :].unsqueeze(2).broadcast_to([P, HC, S]), ALU.mult)
                    dve.tensor_copy(vx[:, :, 0:2 * HD], v_ctx[:, i, :, :])
                    dve.tensor_copy(vx[:, :, 2 * HD:], ones_ctx[:, :].unsqueeze(1).broadcast_to([P, HC, 64 - 2 * HD])).then_inc(kblk_ready, 1)

                def context_attention(i):
                    u0 = b * N_CA * T + T * i

                    def heads(t):
                        return ps[:, 2 * (t % 2):2 * (t % 2) + 2, :].rearrange("p a (h s) -> p (a h) s", s=S)

                    def take_top(t):
                        tk = taken[:, t % 2, :].rearrange("p (h s) -> p h s", s=S)
                        sc = heads(t)
                        for h in range(H):
                            ins = dve.max(m8[:, t % 2, h, 0:8], sc[:, h, :])
                        link(ins)
                        for h in range(H):
                            ins = dve.match_replace(tk[:, h, :], m8[:, t % 2, h, 0:8], sc[:, h, :], LOWEST)
                        link(ins)
                        for h in range(H):
                            ins = dve.max(m8[:, t % 2, h, 8:16], tk[:, h, :])
                        link(ins)
                        for h in range(H):
                            ins = dve.match_replace(tk[:, h, :], m8[:, t % 2, h, 8:16], tk[:, h, :], LOWEST)
                        link(ins)

                    def centre(t):
                        dve.wait_ge(s_ready, u0 + t + 1)
                        if i == 2:
                            dve.sem_inc(passed, 1)
                            take_top(t)
                            top = m8[:, t % 2, :, 0]
                        else:
                            link(dve.tensor_reduce(mx[:, t % 2, :], heads(t), X, ALU.max))
                            top = mx[:, t % 2, :]
                        if t >= 2:
                            dve.wait_ge(p_turned, u0 + t - 1)
                        dve.tensor_tensor(prob[:, t % 2, :].rearrange("p (h s) -> p h s", s=S), heads(t),
                                          top.unsqueeze(2).broadcast_to([P, H, S]), ALU.subtract).then_inc(s_read, 1)

                    def mask(t):
                        dve.wait_ge(top_exp, b * T + t + 1)
                        dve.scalar_tensor_tensor(prob[:, t % 2, :], taken[:, t % 2, :], LOWEST, prob[:, t % 2, :], ALU.is_equal, ALU.mult).then_inc(p_exp, 1)

                    def divide(t):
                        dve.wait_ge(pv_done, u0 + t + 1)
                        o = ps[:, 6, :].rearrange("p (j c) -> p j c", j=HC)
                        r = rs[:, t % 2 * H:(t % 2 + 1) * H].rearrange("p (j a) -> p j a", a=2)
                        link(dve.reciprocal(r, o[:, :, 2 * HD:2 * HD + 2]))
                        if t >= 2:
                            dve.wait_ge(o_turned, u0 + t - 1)
                        dve.tensor_tensor(o_tok[:, t % 2, :].rearrange("p (j a d) -> p j a d", j=HC, a=2), o[:, :, 0:2 * HD].rearrange("p j (a d) -> p j a d", a=2),
                                          r.unsqueeze(3).broadcast_to([P, HC, 2, HD]), ALU.mult).then_inc(o_ready, 1)

                    centre(0)
                    centre(1)
                    if i == 2:
                        mask(0)
                    for t in range(T + 1):
                        if t + 2 < T:
                            centre(t + 2)
                        if i == 2 and t + 1 < T:
                            mask(t + 1)
                        if t >= 1:
                            divide(t - 1)

                dve.wait_ge(x_ld[0], b * 16 + 16)
                statistics(0, 0)
                dve.wait_ge(x_ld[1], b * 48 + 48)
                normalise(0, 0)
                statistics(0, 1)
                normalise(0, 1)
                build_keys(0)
                context_attention(0)
                residual_norm(0)

                for k in range(NB):
                    dve.wait_ge(p1s_done, b * NB + k + 1)
                    sc = ps[:, 4 * k + 2, 0:TB * S].rearrange("p (t s) -> p t s", s=S)
                    link(dve.tensor_reduce(r1m[:, k, :], sc, X, ALU.max))
                    dve.tensor_tensor(p1[:, k, :, :], sc, r1m[:, k, :].unsqueeze(2).broadcast_to([P, TB, S]), ALU.subtract).then_inc(p1_sub, 1)
                for k in range(NB):
                    dve.wait_ge(p1_exp, b * NB + k + 1)
                    link(dve.tensor_reduce(r1m[:, k, :], p1[:, k, :, :], X, ALU.add))
                    link(dve.reciprocal(r1m[:, k, :], r1m[:, k, :]))
                    dve.tensor_tensor(p1[:, k, :, :], p1[:, k, :, :], r1m[:, k, :].unsqueeze(2).broadcast_to([P, TB, S]), ALU.mult).then_inc(p1_ready, 1)
                for k in range(NB):
                    dve.wait_ge(lg_done, b * NB + k + 1)
                    link(dve.tensor_tensor(lg[:, k, :, :], ps[:, 4 * k + 3, 0:TB * 4].rearrange("p (t e) -> p t e", e=4)[:, :, 0:E],
                                           rc[:, :].unsqueeze(1).broadcast_to([P, TB, E]), ALU.add))
                    link(dve.tensor_reduce(rm[:, k, :], lg[:, k, :, :], X, ALU.max))
                    dve.tensor_tensor(lg[:, k, :, :], lg[:, k, :, :], rm[:, k, :].unsqueeze(2).broadcast_to([P, TB, E]), ALU.subtract).then_inc(lg_sub, 1)
                for k in range(NB):
                    dve.wait_ge(lg_exp, b * NB + k + 1)
                    link(dve.tensor_reduce(rm[:, k, :], lg[:, k, :, :], X, ALU.add))
                    link(dve.reciprocal(rm[:, k, :], rm[:, k, :]))
                    dve.tensor_tensor(lg[:, k, :, :], lg[:, k, :, :], rm[:, k, :].unsqueeze(2).broadcast_to([P, TB, E]), ALU.mult).then_inc(lg_ready, 1)
                dve.wait_ge(pbc_ready, b * NB + NB)
                n0 = b * NB * MC
                for n in range(NB * MC):
                    dve.wait_ge(h1_act, n0 + n + 1)
                    dve.tensor_tensor(ring[:, n % 4, :], ring[:, n % 4, :], p_bc[:, n // MC, n % MC // 4, :], ALU.mult).then_inc(h1_ready, 1)
                for k in range(NB):
                    dve.wait_ge(y_done, b * 12 + 2 + k + 1)
                    for m in range(KC):
                        ins = dve.scalar_tensor_tensor(yT[:, k, m, :], ps[:, (2, 4)[k] + m, :], colT[:, C_OUTB + m:C_OUTB + m + 1], gT[:, k, m, :], ALU.add, ALU.mult)
                    ins.then_inc(yT_ready, 1)
                residual_norm(1)

                for k in range(NB):
                    dve.wait_ge(v_done, b * NB + k + 1)
                    for j in range(2):
                        t = TB * k + 2 * j
                        ins = dve.tensor_tensor(v2[:, t:t + 2, 0:H * VS].rearrange("p t (h d) -> p t h d", d=VS)[:, :, :, 0:HD], ps[:, 4 * k + 2 + j, :].rearrange("p (t h d) -> p t h d", t=2, d=HD),
                                                vb2[:, :].rearrange("p (h d) -> p h d", d=HD).unsqueeze(1).broadcast_to([P, 2, H, HD]), ALU.add)
                    ins.then_inc(v_ready, 1)
                u0 = b * N_RING
                uses = [0]

                def place():
                    n = uses[0]
                    uses[0] += 1
                    dve.wait_ge(ring_ready, u0 + n + 1)
                    return ps[:, 2 * (n % 2):2 * (n % 2) + 2, :].rearrange("p a q -> p (a q)")

                def low_parts(c, qk):
                    dve.wait_ge(hi_ready, b * 2 * KC + 2 * c + qk + 1)
                    col = (C_BQ2, C_BK2)[qk] + c
                    dve.scalar_tensor_tensor(dense[2 * qk + 1][:, :], place(), colT[:, col:col + 1], dense[2 * qk][:, :].bitcast(F32),
                                             ALU.add, ALU.subtract).then_inc(ring_read, 1)

                def query_maximum(u):
                    e, t = u // T, u % T
                    return dve.tensor_reduce(mm[:, e, t:t + 1], place(), X, ALU.max).then_inc(ring_read, 1)

                def maxima(p):
                    dve.wait_ge(ring_read, b * N_SCORE + reads())
                    link(dve.tensor_copy(mh[:, :, :], mm[:, :, :]))
                    cols = mt[:, :, :].rearrange("p t (e c) -> p e t c", e=2)
                    dve.tensor_copy(cols[:, :, :, 48], mh[:, :, :].bitcast(F32))
                    dve.tensor_tensor(cols[:, :, :, 49], mm[:, :, :], mh[:, :, :].bitcast(F32), ALU.subtract).then_inc(mt_ready, 1)
                    dve.wait_ge(mt_ready, b * NP + p + 1)

                def add_maxima(p):
                    dve.tensor_tensor(qx[:, p % 4, :], place(), qx[:, p % 4, :].bitcast(F32), ALU.add).then_inc(ring_read, 1)

                def finish(p):
                    acc = place()[:, 0:BLK].rearrange("p (j e h c) -> p j e h c", j=TB, e=2, h=2)
                    link(dve.reciprocal(fr[:, p % 2, :, :].rearrange("p j (e h) -> p j e h", h=2), acc[:, :, :, :, HD]))
                    for half in range(2):
                        ins = dve.tensor_tensor(xhat[:, half * TB:(half + 1) * TB, 2 * HD * p:2 * HD * (p + 1)].rearrange("p t (e d) -> p t e d", d=HD),
                                                acc[:, :, :, half, 0:HD],
                                                fr[:, p % 2, :, :].rearrange("p j (e h) -> p j e h", h=2)[:, :, :, half].unsqueeze(3).broadcast_to([P, TB, 2, HD]), ALU.mult)
                    ins.then_inc(ring_read, 1)

                spreads = [0]

                def reads():
                    return uses[0] - spreads[0]

                for qk in range(2):
                    low_parts(0, qk)
                uses[0] += 2
                spreads[0] += 2
                dve.wait_ge(mt_clear, b + 1)
                for n in range(-LEAD, UNITS):
                    (p, u), m = divmod(n, 2 * T), n + LEAD
                    q, at_m = divmod(m, 2 * T)
                    if m < UNITS:
                        query_maximum(at_m)
                    if at_m == 2 and 1 <= q <= NP:
                        add_maxima(q - 1)
                    if at_m in (7, 9) and q + 1 < NP:
                        uses[0] += 1
                        spreads[0] += 1
                    if q + 1 == NP // 2 - 1 and at_m in (11, 13):
                        low_parts(1, (at_m - 11) // 2)
                    if u == 5 and p >= 1:
                        finish(p - 1)
                    if m < UNITS and at_m == 2 * T - 1:
                        maxima(q)
                finish(NP - 1)
                assert uses[0] == N_RING and reads() == N_SCORE
                residual_norm(2)

                build_keys(1)
                context_attention(1)
                residual_norm(3)
                residual_norm(4)

                for k in range(NB):
                    dve.wait_ge(v3_done, b * NB + k + 1)
                    for j in range(2):
                        t = TB * k + 2 * j
                        for odd in range(2):
                            o = HD * odd
                            ins = dve.tensor_tensor(
                                v3[:, t:t + 2, :, :].rearrange("p t (j o) d -> p t j o d", o=2)[:, :, :, odd, o:o + HD],
                                ps[:, 4 * k + j, :].rearrange("p (t j d) -> p t j d", t=2, d=2 * HD)[:, :, :, o:o + HD],
                                vb3[:, :].rearrange("p (j d) -> p j d", d=2 * HD)[:, :, o:o + HD].unsqueeze(1).broadcast_to([P, 2, H // 2, HD]), ALU.add)
                    ins.then_inc(v3_ready, 1)
                w0 = b * N_UNIT

                def window_centre(u):
                    dve.wait_ge(ws_ready, w0 + u + 1)
                    sc = ps[:, 2 * (u % 2):2 * (u % 2) + 2, :].rearrange("p a (h s) -> p (a h) s", s=P)
                    link(dve.tensor_reduce(mx[:, u % 2, 0:HC], sc, X, ALU.max))
                    if u >= 2:
                        dve.wait_ge(wp_turned, w0 + u - 1)
                    dve.tensor_tensor(prob[:, u % 2, :].rearrange("p (h s) -> p h s", s=P), sc,
                                      mx[:, u % 2, 0:HC].unsqueeze(2).broadcast_to([P, HC, P]), ALU.subtract).then_inc(ws_read, 1)

                def window_divide(u):
                    t, c = u // KC, u % KC
                    dve.wait_ge(wpv_done, w0 + u + 1)
                    r = rs[:, u % 2 * P:(u % 2 + 1) * P]
                    link(dve.reciprocal(r, ps[:, 6 + u % 2, P:2 * P]))
                    dve.tensor_tensor(oT[:, t // TB, c, t % TB * P:(t % TB + 1) * P], ps[:, 6 + u % 2, 0:P], r, ALU.mult).then_inc(wo_ready, 1)
                window_centre(0)
                window_centre(1)
                for u in range(N_UNIT):
                    if u + 2 < N_UNIT:
                        window_centre(u + 2)
                    window_divide(u)
                residual_norm(5)

                build_keys(2)
                context_attention(2)
                residual_norm(6)

                n0 = b * NB * NC_HID
                for n in range(NB * NC_HID):
                    m = n % NC_HID
                    dve.wait_ge(h3_act, n0 + n + 1)
                    dve.scalar_tensor_tensor(ring[:, n % 4, :], ps[:, 2 * (n % 2) + 1, :], colT[:, C_BM13 + NC_HID + m:C_BM13 + NC_HID + m + 1],
                                             ring[:, n % 4, :], ALU.add, ALU.mult).then_inc(h3_ready, 1)
                for k in range(NB):
                    residual(7, k).then_inc(x_final, 1)
                dve.wait_ge(x_final, b * NB + NB)

        @block.gpsimd
        def _(pool):
            pool.memset(minus_half[:, :], -0.5).then_inc(set_pool, 1)
            pool.wait_ge(set_pool, 1)
            pool.wait_ge(ctx_var, 1)
            pool.tensor_tensor(s_st[:, 10:12], s_st[:, 8:10], minus_half[:, 0:2], ALU.pow).then_inc(ctx_rstd, 1)
            with pool.Fori(0, B) as b:
                def ln(i):
                    for k in range(NB):
                        pool.wait_ge(ve_ready, b * 2 * N_LN + 2 * i + k + 1)
                        pool.tensor_tensor(rstd[:, k, :], ve[:, k, :], minus_half[:, :], ALU.pow).then_inc(rstd_ready, 1)

                ln(0)
                ln(1)
                pool.wait_ge(y_done, b * 12 + 2)
                pool.sem_inc(passed, 1)
                pool.memset(mt[:, :, :], 0.0).then_inc(mt_clear, 1)
                ln(2)
                pool.wait_ge(y_turned, b * 2 * N_RES + 4)
                pool.sem_inc(passed, 1)
                pool.memset(v2[:, :, H * VS:], 0.0)
                pool.memset(v2[:, :, 0:H * VS].rearrange("p t (h d) -> p t h d", d=VS)[:, :, :, HD:VS], 1.0).then_inc(v2_clear, 1)
                pool.wait_ge(pv2_done, b * T * NP + T * NP)
                pool.sem_inc(passed, 1)
                pairs = v3[:, :, :, :].rearrange("p t (j o) d -> p (t j) o d", o=2)
                pool.memset(pairs[:, :, 0, HD:2 * HD], 0.0)
                pool.memset(pairs[:, :, 1, 0:HD], 0.0).then_inc(v3_clear, 1)
                ln(3)
                ln(4)
                ln(5)
                u0 = b * N_UNIT
                for u in range(N_UNIT):
                    t, c = u // KC, u % KC
                    if u % N_UNIT in (0, N_UNIT // 2):
                        pool.wait_ge(qk3_ready, b * NB + t // TB + 1)
                    if u >= 2:
                        pool.wait_ge(ws_ready, u0 + u - 1)
                    pool.tensor_tensor(wkblk[:, u % 2, :, :], kT3[:, t // TB, c, t % TB * P:(t % TB + 1) * P].unsqueeze(1).broadcast_to([P, HC, P]),
                                       head_mask[:, :].unsqueeze(2).broadcast_to([P, HC, P]), ALU.mult).then_inc(wk_ready, 1)
                ln(6)
                ln(7)


def constants():
    row = np.arange(P)
    head_mask = (row[:, None] // HD == np.arange(HC)).astype(np.float32)
    ones_ctx = (row[:, None] // S == np.arange(64 - 2 * HD)).astype(np.float32)
    ones_win = np.zeros((P, 2, 2 * HD), np.float32)
    ones_win[:, 0, :HD] = 1
    ones_win[:, 1, HD:] = 1
    sel = np.zeros((P, 4, 4, P), np.float32)
    d = np.arange(HD)
    for pp in range(4):
        for e in range(2):
            r = 32 * pp + HD * e + d
            for part, places in enumerate(((0, 2), (1,), (0, 1), (2,))):
                for place in places:
                    sel[r, pp, part, 64 * e + HD * place + d] = 1
    k_aug = np.zeros((P, 1), np.float32)
    k_aug[[48, 49, 64 + 48, 64 + 49]] = -1
    sel3 = np.zeros((E, E, P), np.float32)
    sel3[np.arange(E), np.arange(E)] = 1
    return {"c_ident": np.eye(P, dtype=np.float32), "c_head_mask": head_mask, "c_ones_ctx": ones_ctx,
            "c_ones_win": ones_win, "c_sel": sel, "c_k_aug": k_aug, "c_sel3": sel3}


def kernel(**inputs):
    import concourse.bacc as bacc
    from concourse.bass_utils import run_bass_kernel_spmd

    arrays = {n: np.ascontiguousarray(np.asarray(a)) for n, a in inputs.items()}
    arrays.update(constants())
    nc = bacc.Bacc("TRN2", target_bir_lowering=False, num_devices=1)
    handles = {n: nc.dram_tensor(f"in_{n}_dram", a.shape, mybir.dt.from_np(a.dtype), kind="ExternalInput") for n, a in arrays.items()}
    out = nc.dram_tensor("out_0_dram", (B, L, D), F32, kind="ExternalOutput")
    build(nc, out.ap(), {n: h.ap() for n, h in handles.items()})
    if not nc.is_finalized():
        nc.finalize()
    result = run_bass_kernel_spmd(nc, [{f"in_{n}_dram": a for n, a in arrays.items()}], core_ids=[0])
    return np.asarray(result.results[0]["out_0_dram"])
```

```python
from contextlib import ExitStack

import numpy as np
import concourse.bass as bass
import concourse.mybir as mybir

F32 = mybir.dt.float32
F32R = mybir.dt.float32r
ALU = mybir.AluOpType
ACT = mybir.ActivationFunctionType
X = mybir.AxisListType.X

P = 128
D = 256
KC = D // P
B = 2
L = 1024
T = L // P
NB = 2
TB = T // NB
BLK = TB * P
H = 16
HD = D // H
HC = P // HD
S = 64
SHIFT = 64
E = 3
RH = 512
MC = E * RH // P
HID = 1024
NC_HID = HID // P
TOPK = 16
VS = HD + 1
QK_SCALE = float(HD) ** -0.5
L1_SCALE = float(D) ** -0.5
EPS5, EPS6 = 1e-5, 1e-6
LOWEST = -3.4028234663852886e38

M_SC_Q, M_SH_Q, M_SC_KV, M_SH_KV = 0, 2, 4, 6
M_SH_A, M_SC_A, M_G_A, M_SH_M, M_SC_M, M_G_M = 8, 10, 12, 14, 16, 18
M3_SH_SA, M3_SC_SA, M3_G_SA, M3_SH_CA, M3_SC_CA, M3_G_CA, M3_SH_ML, M3_SC_ML, M3_G_ML = range(20, 38, 2)
N_MOD = 38
M_BG = 38
GATED = (M_G_A, M_G_M, M3_G_SA, M3_G_CA, M3_G_ML)
SCALES = (M_SC_Q, M_SC_KV, M_SC_A, M_SC_M, M3_SC_SA, M3_SC_CA, M3_SC_ML)
M_HB = 48
N_MC = 62
C_BQ0, C_BP0, C_BK0, C_GAMMA, C_BETA, C_GB2, C_OUTB = range(62, 76, 2)
C_BQ2, C_BK2, C_BQC, C_BKC, C_BCP, C_BM1 = 76, 78, 80, 82, 84, 86
C_BQ3, C_BK3, C_BQ3C, C_BK3C, C_BM13 = 94, 96, 98, 100, 102
C_COND = 118
N_COL = 122

N_LN, N_Q, N_RES, N_CA = 8, 3, 8, 3
NP = H // 2
N_SCORE = 2 + H * T + NP + NP
N_SPREAD = 2 * NP
N_RING = N_SCORE + N_SPREAD
UNITS = H * T
LEAD = 20
N_RA = 12 * 16
N_UNIT = T * KC


def build(nc, out, g):
    es = ExitStack()
    with es:
        base = (nc.sbuf_base + 63) // 64 * 64
        top = [base]

        def at(name, shape, dt, offset):
            return nc.alloc_sbuf_tensor_at(name, shape, dt, offset=offset)

        def keep(name, shape, dt=F32):
            size = int(np.prod(shape[1:])) * 4
            o = top[0]
            top[0] = o + (size + 31) // 32 * 32
            return at(name, shape, dt, o)

        def region(size):
            o = top[0]
            top[0] += size
            return o

        def sem(name):
            return es.enter_context(nc.semaphore(name))

        ident = keep("ident", [P, P])
        head_mask = keep("head_mask", [P, HC])
        ones_ctx = keep("ones_ctx", [P, 32])
        ones_win = keep("ones_win", [P, 2, 32])
        sel = keep("sel", [P, 4, 4, P], F32R)
        k_aug = keep("k_aug", [P, 1])
        minus_half = keep("minus_half", [P, TB])
        sel3 = keep("sel3", [E, E, P])
        b2 = keep("b2", [E, D])
        vb2 = keep("vb2", [P, D])
        vb3 = keep("vb3", [P, D])
        rb = keep("rb", [P, E])
        colT = keep("colT", [P, N_COL])
        mod2 = keep("mod2", [P, B, N_MC])
        kT2 = keep("kT2", [P, 3, KC, B, S])
        v_ctx2 = keep("v_ctx2", [P, B, 3, HC, 32])
        kw2 = keep("kw2", [P, KC, B, S])
        N_VW = E * RH + D + E
        vw2 = keep("vw2", [P, B, N_VW])
        rc2 = keep("rc2", [P, B, E])
        mod = keep("mod", [P, N_MC])
        v_ctx = keep("v_ctx", [P, 3, HC, 32])
        kw = keep("kw", [P, KC, S + E])
        kT = keep("kT", [P, 3, KC, S])
        rc = keep("rc", [P, E])
        x = keep("x", [P, T, D])
        s_sel = at("s_sel", [P, 4, 4, P], F32, top[0])
        hT = keep("hT", [P, NB, KC, BLK])
        s_st = at("s_st", [P, 16], F32, top[0])
        st = keep("st", [P, NB, TB, 6])
        mv = keep("mv", [P, NB, TB, 2])
        ve = keep("ve", [P, NB, TB])
        rstd = keep("rstd", [P, NB, TB])
        mx = keep("mx", [P, 2, H])
        mm = keep("mm", [P, 2, T])
        mh = keep("mh", [P, 2, T], F32R)
        fr = keep("fr", [P, 2, TB, 4])
        r1m = keep("r1m", [P, NB, TB])
        lg = keep("lg", [P, NB, TB, E])
        rm = keep("rm", [P, NB, TB])

        RA = region(40 * 1024 + 64)
        RC1 = region(34 * 1024)
        RC2 = region(24 * 1024)
        RF = region(48 * 1024)
        assert top[0] <= nc.sbuf_usable_end, (top[0], nc.sbuf_usable_end)
        K1 = 1024

        def weights(start, items):
            made, o = [], start
            for name, shape in items:
                made.append(at(name, shape, F32, o))
                o += (int(np.prod(shape[1:])) * 4 + 31) // 32 * 32
            return made, o

        (wq0, wp0, w1, wg1, w2, wg2, wout, wv2, wqk2), e0 = weights(RA, [
            ("wq0", [P, KC, D]), ("wp0", [P, KC, D]), ("w1", [P, E, KC, RH]), ("wg1", [P, KC, D]),
            ("w2", [P, MC, D]), ("wg2", [P, KC, D]), ("wout", [P, KC, D]),
            ("wv2", [P, KC, D]), ("wqk2", [P, KC, 2 * D])])
        assert e0 <= RC1
        (wproj, wqc, wcp, wm1, wm2, wqkv3, wso, wq3, wco), e1 = weights(RC1, [
            ("wproj", [P, KC, D]), ("wqc", [P, KC, D]), ("wcp", [P, KC, D]), ("wm1", [P, KC, HID]),
            ("wm2", [P, NC_HID, D]), ("wqkv3", [P, KC, 3 * D]), ("wso", [P, KC, D]), ("wq3", [P, KC, D]),
            ("wco", [P, KC, D])])
        assert e1 <= RC2
        (w3a, w3b), e2 = weights(RC2, [("w3a", [P, KC, 2 * HID]), ("w3b", [P, NC_HID, D])])
        assert e2 <= RF

        (s_mrow01, s_mrow2, s_ss_q, s_ss_kv, s_mod, s_ada, s_kv0, s_q1, s_k1, s_v1, s_ev, s_an, s_gev, s_gan, s_rev, s_ran, s_kvc, s_kv3,
         s_rows, s_ctxT, s_k1T, s_wqT, s_vT, s_crep, s_vb, s_silu, s_cond), e3 = weights(RC1, [
             ("s_mrow01", [P, 2, 512]), ("s_mrow2", [P, 512]), ("s_ss_q", [P, KC, 2 * D]), ("s_ss_kv", [P, KC, 2 * D]), ("s_mod", [P, KC, 6 * D]),
             ("s_ada", [P, KC, 9 * D]), ("s_kv0", [P, KC, 2 * D]), ("s_q1", [P, KC, D]), ("s_k1", [P, KC, D]),
             ("s_v1", [P, KC, D]), ("s_ev", [P, E, KC, RH]), ("s_an", [P, E, KC, RH]), ("s_gev", [P, KC, D]),
             ("s_gan", [P, KC, D]), ("s_rev", [P, KC, E]), ("s_ran", [P, KC, E]), ("s_kvc", [P, KC, 2 * D]),
             ("s_kv3", [P, KC, 2 * D]), ("s_rows", [P, P]),
             ("s_ctxT", [P, 3, KC, B, 2, S]), ("s_k1T", [P, KC, B * S]), ("s_wqT", [P, KC, D]),
             ("s_vT", [P, KC, B, 2, S]), ("s_crep", [P, KC, B, P]), ("s_vb", [P, 3, D]), ("s_silu", [P, KC, 32]), ("s_cond", [P, KC, 32]),
             ])
        assert e3 <= nc.sbuf_usable_end, e3
        s_ctx = at("s_ctx", [P, D], F32, RC1)
        s_xh = at("s_xh", [P, 3, D], F32, RC1 + K1)
        s_mrow = [s_mrow01[:, 0], s_mrow01[:, 1], s_mrow2, s_mrow01[:, 0]]

        xhat = at("xhat", [P, T, D], F32, RF)
        yT = at("yT", [P, NB, KC, BLK], F32, RF)
        qT = at("qT", [P, NB, KC, BLK], F32, RF + 8 * K1)
        oT = at("oT", [P, NB, KC, BLK], F32, RF + 8 * K1)
        ring = at("ring", [P, 4, BLK], F32, RF + 16 * K1)
        kblk = at("kblk", [P, KC, HC, S], F32, RF + 16 * K1)
        rs = at("rs", [P, BLK], F32, RF + 20 * K1)
        m8 = at("m8", [P, 2, H, TOPK], F32, RF + 22 * K1)
        prob = at("prob", [P, 2, 1024], F32, RF + 24 * K1)
        probT = at("probT", [P, 2, HC, P], F32, RF + 32 * K1)
        vx = at("vx", [P, HC, 64], F32, RF + 40 * K1)
        o_tok = at("o_tok", [P, 2, D], F32, RF + 42 * K1)
        wprobT = at("wprobT", [P, 2, HC, P], F32, RF + 32 * K1)
        wkblk = at("wkblk", [P, 2, HC, P], F32, RF + 40 * K1)
        vw = at("vw", [P, N_VW], F32R, RC2)
        p1T = at("p1T", [P, NB, BLK], F32R, RC2 + 8 * K1)
        p1lo = at("p1lo", [S, NB, BLK], F32R, RF + 8 * K1)
        gT = at("gT", [P, NB, KC, BLK], F32, RC2 + 12 * K1)
        g1 = [at("g1_0", [P, KC, BLK], F32, RC2 + 20 * K1), at("g1_1", [P, KC, BLK], F32, RF + 44 * K1)]
        p1 = at("p1", [P, NB, TB, 2, S], F32, RF + 24 * K1)
        pT = at("pT", [E, NB, BLK], F32, RF + 28 * K1)
        p_bc = at("p_bc", [P, NB, E, BLK], F32, RF + 32 * K1)
        rT = [at("rT_0", [P, KC, BLK], F32, RF + 44 * K1), at("rT_1", [P, KC, BLK], F32, RC2 + 20 * K1)]
        qx = at("qx", [P, 4, L], F32R, RA)
        kx = at("kx", [P, 4, L], F32R, RA + 16 * K1)
        dense = [at(n, [P, L], F32R, o) for n, o in (("q_hi", RC2 + 8 * K1), ("q_lo", RA + 32 * K1),
                                                     ("k_hi", RC2), ("k_lo", RC2 + 4 * K1))]
        v2 = at("v2", [P, T, H * VS + HD], F32, RC2 + 12 * K1)
        pt = at("pt", [P, 8, L], F32, RF + 16 * K1)
        full = [hT[:, qk].rearrange("p c q -> p (c q)") for qk in range(2)]
        accS = at("accS", [P, 2, BLK], F32, RF + 8 * K1)
        mt = at("mt", [P, T, P], F32, RF + 12 * K1)
        w1s = at("w1s", [P, 2, KC, HID], F32R, RA)
        w2s = at("w2s", [P, 2, NC_HID, D], F32R, RA + 16 * K1)
        hs = at("hs", [P, NB, 2, KC, BLK], F32R, RF + 24 * K1)
        gelu = at("gelu", [P, 4, BLK], F32, RA + 32 * K1)
        gelus = [at("gelu_hi", [P, 4, BLK], F32R, RF + 16 * K1), at("gelu_lo", [P, 4, BLK], F32R, RF + 40 * K1)]
        gate3 = [at("gate3_0", [P, 4, BLK], F32, RA), at("gate3_1", [P, 4, BLK], F32, RF + 16 * K1)]
        up3 = [at("up3_0", [P, 4, BLK], F32, RA + 8 * K1), at("up3_1", [P, 4, BLK], F32, RF + 24 * K1)]
        taken = at("taken", [P, 2, H * S], F32, RA + 16 * K1)
        prob3 = at("prob3", [P, 3, H * S], F32, RA + 24 * K1)
        v3 = at("v3", [P, T, H, 32], F32, RA)
        kT3 = at("kT3", [P, NB, KC, BLK], F32, RA + 16 * K1)

        ps = es.enter_context(nc.psum_tensor("ps", [P, 8, 512], F32))

        consts_ld, ident_ld, rows_ld, ctx_ld = sem("consts_ld"), sem("ident_ld"), sem("rows_ld"), sem("ctx_ld")
        s_mod_ld, s_kv_ld, s_l1_ld, rc1_ld = sem("s_mod_ld"), sem("s_kv_ld"), sem("s_l1_ld"), sem("rc1_ld")
        ra_ld, rc2_ld, out_stored = sem("ra_ld"), sem("rc2_ld"), [sem("out_stored0"), sem("out_stored1")]
        x_ld = [sem("x_ld0"), sem("x_ld1")]
        set_pe, set_act, set_dve, set_pool = sem("set_pe"), sem("set_act"), sem("set_dve"), sem("set_pool")
        mrow_done, mrow_copied = sem("mrow_done"), sem("mrow_copied")
        dve_step, ctx_var, ctx_rstd = sem("dve_step"), sem("ctx_var"), sem("ctx_rstd")
        begun = sem("begun")
        ve_ready, rstd_ready, xhat_ready = sem("ve_ready"), sem("rstd_ready"), sem("xhat_ready")
        ln_turned, hT_ready = sem("ln_turned"), sem("hT_ready")
        q_done, qT_ready = sem("q_done"), sem("qT_ready")
        kblk_ready, s_ready, s_read, p_exp, p_turned, pT_ready = (sem(n) for n in (
            "kblk_ready", "s_ready", "s_read", "p_exp", "p_turned", "pT_ready"))
        ts_ready, ts_read, top_marked, top_sub, top_exp, top_ready, tp_turned, tpT_ready, tpv_done, to_ready, to_turned, toT_ready = (sem(n) for n in (
            "ts_ready", "ts_read", "top_marked", "top_sub", "top_exp", "top_ready", "tp_turned", "tpT_ready", "tpv_done", "to_ready", "to_turned", "toT_ready"))
        pv_done, o_ready, o_turned, oT_ready = sem("pv_done"), sem("o_ready"), sem("o_turned"), sem("oT_ready")
        y_done, yT_ready, y_turned, x_final = sem("y_done"), sem("yT_ready"), sem("y_turned"), sem("x_final")
        p1s_done, p1_sub, p1_exp, p1_ready, p1_turned, p1T_hi, p1T_ready, vw_hi, vw_ready = (sem(n) for n in (
            "p1s_done", "p1_sub", "p1_exp", "p1_ready", "p1_turned", "p1T_hi", "p1T_ready", "vw_hi", "vw_ready"))
        lg_done, lg_sub, lg_exp, lg_ready, lg_turned, pT_made = (sem(n) for n in (
            "lg_done", "lg_sub", "lg_exp", "lg_ready", "lg_turned", "pT_made"))
        g1_done, g1_ready, g2_done, gT_ready, pbc_done, pbc_ready = (sem(n) for n in (
            "g1_done", "g1_ready", "g2_done", "gT_ready", "pbc_done", "pbc_ready"))
        mt_clear, ot_turned, passed = sem("mt_clear"), sem("ot_turned"), sem("passed")
        h1_done, h1_act, h1_ready, w2_done, rT_ready = (sem(n) for n in (
            "h1_done", "h1_act", "h1_ready", "w2_done", "rT_ready"))
        h2_done, h2_ready, w22_done = sem("h2_done"), sem("h2_ready"), sem("w22_done")
        h3_done, h3_read, h3_ready, w32_done = sem("h3_done"), sem("h3_read"), sem("h3_ready"), sem("w32_done")
        v_done, v_ready, v2_clear = sem("v_done"), sem("v_ready"), sem("v2_clear")
        ring_ready, ring_read, spread_read, hi_ready, lo_ready, full_done, full_ready = (sem(n) for n in (
            "ring_ready", "ring_read", "spread_read", "hi_ready", "lo_ready", "full_done", "full_ready"))
        st_ready, pt_ready, pv2_done, acc_read, mt_ready = (sem(n) for n in (
            "st_ready", "pt_ready", "pv2_done", "acc_read", "mt_ready"))
        w_hi, w_split, hs_lo, h2_lo = sem("w_hi"), sem("w_split"), sem("hs_lo"), sem("h2_lo")
        qk3_done, qk3_ready, v3_done, v3_ready, v3_clear = (sem(n) for n in (
            "qk3_done", "qk3_ready", "v3_done", "v3_ready", "v3_clear"))
        wk_ready, ws_ready, ws_read, wp_exp, wp_turned, wpT_ready, wpv_done, wo_ready = (sem(n) for n in (
            "wk_ready", "ws_ready", "ws_read", "wp_exp", "wp_turned", "wpT_ready", "wpv_done", "wo_ready"))

        block = es.enter_context(nc.Block())

        def rows(a):
            return a.rearrange("(k p) n -> p k n", p=P)

        vectors = ("L0_xcond_bss_q", "L0_xcond_bss_kv", "L2_xcond_b_mod", "L3_xcond_b_ada", "L2_xcond_b_proj",
                   "L2_xcond_b_mlp2", "L3_xcond_b_so", "L3_xcond_b_co", "L3_xcond_b_m2", "L1_xcond_e_b1",
                   "L1_xcond_gate_b1", "L0_xcond_bq", "L0_xcond_bp", "L0_xcond_bkv", "L1_xcond_ln_gamma",
                   "L1_xcond_ln_beta", "L1_xcond_gate_b2", "L1_xcond_out_b", "L2_xcond_b_qkv", "L2_xcond_b_qc",
                   "L2_xcond_b_kvc", "L2_xcond_b_cproj", "L2_xcond_b_mlp1", "L3_xcond_b_qkv", "L3_xcond_b_q",
                   "L3_xcond_b_kv", "L3_xcond_b_m1", "cond_1024")

        def load_rows(eng, first, last):
            r = 0
            for i, name in enumerate(vectors):
                a = g[name]
                if len(a.shape) == 2:
                    a = a.rearrange("e n -> (e n)")
                n = a.shape[0] // P
                if name in ("L0_xcond_bkv", "L2_xcond_b_kvc", "L3_xcond_b_kv"):
                    n = KC
                if name in ("L2_xcond_b_qkv", "L3_xcond_b_qkv"):
                    n = 2 * KC
                if first <= i < last:
                    eng.dma_start(s_rows[r:r + n, :], a[0:n * P].rearrange("(n p) -> n p", p=P)).then_inc(rows_ld, 16)
                r += n
            assert r == N_COL

        @block.sync
        def _(sp):
            sp.dma_start(s_ctx[:, :], g["ctx_1024"].rearrange("b s d -> (b s) d")).then_inc(ctx_ld, 16)
            sp.dma_start(ident[:, :], g["c_ident"]).then_inc(ident_ld, 16)
            load_rows(sp, 0, len(vectors))
            for tile, name in ((s_q1, "L1_xcond_Wq"), (s_k1, "L1_xcond_Wk"), (s_v1, "L1_xcond_Wv")):
                sp.dma_start(tile[:, :, :], rows(g[name])).then_inc(s_l1_ld, 16)
            for e in range(E):
                sp.dma_start(s_ev[:, e, :, :], rows(g["L1_xcond_e_w1"][e, D:2 * D, :])).then_inc(s_l1_ld, 16)
                sp.dma_start(s_an[:, e, :, :], rows(g["L1_xcond_e_w1"][e, 2 * D:3 * D, :])).then_inc(s_l1_ld, 16)
            for tile, name, part in ((s_gev, "L1_xcond_gate_w1", 1), (s_gan, "L1_xcond_gate_w1", 2),
                                     (s_rev, "L1_xcond_router_W", 1), (s_ran, "L1_xcond_router_W", 2)):
                sp.dma_start(tile[:, :, :], rows(g[name][part * D:(part + 1) * D, :])).then_inc(s_l1_ld, 16)

            sp.dma_start(head_mask[:, :], g["c_head_mask"]).then_inc(consts_ld, 16)
            sp.dma_start(ones_ctx[:, :], g["c_ones_ctx"]).then_inc(consts_ld, 16)
            sp.dma_start(ones_win[:, :, :], g["c_ones_win"]).then_inc(consts_ld, 16)
            sp.dma_start(s_sel[:, :, :, :], g["c_sel"]).then_inc(consts_ld, 16)
            sp.dma_start(k_aug[:, :], g["c_k_aug"]).then_inc(consts_ld, 16)
            sp.dma_start(sel3[:, :, :], g["c_sel3"]).then_inc(consts_ld, 16)
            for tile, name, a, z in ((vb2, "L2_xcond_b_qkv", 2 * D, 3 * D), (vb3, "L3_xcond_b_qkv", 2 * D, 3 * D),
                                     (rb, "L1_xcond_router_b", 0, E)):
                sp.dma_start(tile[:, :], g[name][a:z].unsqueeze(0).broadcast_to([P, z - a])).then_inc(consts_ld, 16)
            for i, name in enumerate(("L0_xcond_bkv", "L2_xcond_b_kvc", "L3_xcond_b_kv")):
                sp.dma_start(s_vb[:, i, :], g[name][D:2 * D].unsqueeze(0).broadcast_to([P, D])).then_inc(consts_ld, 16)
            sp.dma_start(b2[:, :], g["L1_xcond_e_b2"]).then_inc(consts_ld, 16)

            def load_ra():
                for tile, name in ((wq0, "L0_xcond_Wq"), (wp0, "L0_xcond_Wp"), (wg2, "L1_xcond_gate_w2"),
                                   (wout, "L1_xcond_out_w")):
                    sp.dma_start(tile[:, :, :], rows(g[name])).then_inc(ra_ld, 16)
                sp.dma_start(wqk2[:, :, :], rows(g["L2_xcond_W_qkv"][:, 0:2 * D])).then_inc(ra_ld, 16)
                sp.dma_start(wv2[:, :, :], rows(g["L2_xcond_W_qkv"][:, 2 * D:3 * D])).then_inc(ra_ld, 16)
                for e in range(E):
                    sp.dma_start(w1[:, e, :, :], rows(g["L1_xcond_e_w1"][e, 0:D, :])).then_inc(ra_ld, 16)
                sp.dma_start(wg1[:, :, :], rows(g["L1_xcond_gate_w1"][0:D, :])).then_inc(ra_ld, 16)
                sp.dma_start(kw[:, :, S:], rows(g["L1_xcond_router_W"][0:D, :])).then_inc(ra_ld, 16)
                sp.dma_start(w2[:, :, :], g["L1_xcond_e_w2"].rearrange("e (k p) n -> p (e k) n", p=P)).then_inc(ra_ld, 16)

            load_ra()
            def load_x0(b):
                sp.dma_start(x[:, 0:TB, :], g["x"][b, SHIFT:SHIFT + BLK, :].rearrange("(t p) d -> p t d", p=P)).then_inc(x_ld[0], 16)

            def sequence(b, more):
                xb = g["x"][b, :, :]
                sp.wait_ge(out_stored[1], b * 48 + 1)
                sp.dma_start(x[:, TB:T - 1, :], xb[SHIFT + BLK:L - SHIFT, :].rearrange("(t p) d -> p t d", p=P)).then_inc(x_ld[1], 16)
                sp.dma_start(x[0:SHIFT, T - 1, :], xb[L - SHIFT:L, :]).then_inc(x_ld[1], 16)
                sp.dma_start(x[SHIFT:P, T - 1, :], xb[0:SHIFT, :]).then_inc(x_ld[1], 16)
                sp.wait_ge(ring_read, b * N_SCORE + N_SCORE)
                sp.wait_ge(pv2_done, b * T * NP + T * NP)
                sp.dma_start(w3a[:, :, :], rows(g["L3_xcond_w_m1"])).then_inc(rc2_ld, 16)
                sp.dma_start(w3b[:, :, :], rows(g["L3_xcond_w_m2"])).then_inc(rc2_ld, 16)
                sp.wait_ge(w32_done, b * NB * NC_HID + NC_HID)
                load_ra()
                ob = out[b, :, :]
                sp.wait_ge(x_final, b * NB + 1)
                sp.dma_start(ob[SHIFT:SHIFT + BLK, :].rearrange("(t p) d -> p t d", p=P), x[:, 0:TB, :]).then_inc(out_stored[0], 16)
                if more:
                    sp.wait_ge(out_stored[0], b * 16 + 16)
                    load_x0(b + 1)
                sp.wait_ge(x_final, b * NB + 2)
                sp.dma_start(ob[SHIFT + BLK:L - SHIFT, :].rearrange("(t p) d -> p t d", p=P), x[:, TB:T - 1, :]).then_inc(out_stored[1], 16)
                sp.dma_start(ob[L - SHIFT:L, :], x[0:SHIFT, T - 1, :]).then_inc(out_stored[1], 16)
                sp.dma_start(ob[0:SHIFT, :], x[SHIFT:P, T - 1, :]).then_inc(out_stored[1], 16)

            sp.sem_inc(out_stored[1], 1)
            load_x0(0)
            with sp.Fori(0, B - 1) as b:
                sequence(b, True)
            sequence(B - 1, False)
            sp.wait_ge(out_stored[0], B * 16)
            sp.wait_ge(out_stored[1], B * 48 + 1)
            sp.wait_ge(ra_ld, (B + 1) * N_RA)

        @block.tensor
        def _(pe):
            def linear(bank, w, m, src):
                for c in range(KC):
                    ins = pe.matmul(ps[:, bank, :], w[:, c, m * P:(m + 1) * P], src[:, c, :],
                                    start=c == 0, stop=c == KC - 1)
                return ins

            def turn_block(k, src, bank=None):
                bank = 4 * k if bank is None else bank
                for c in range(KC):
                    for t in range(TB):
                        ins = pe.transpose(ps[:, bank + c, t * P:(t + 1) * P], src[:, TB * k + t, c * P:(c + 1) * P], ident[:, :])
                return ins

            pe.wait_ge(ident_ld, 16)
            pe.wait_ge(rows_ld, 28 * 16)
            pe.transpose(ps[:, 0, 0:N_COL], s_rows[0:N_COL, :], ident[0:N_COL, 0:N_COL]).then_inc(set_pe, 1)
            pe.wait_ge(set_dve, 1)
            for v in range(3):
                for c in range(KC):
                    ins = pe.transpose(ps[:, 1 + v, c * P:(c + 1) * P], s_xh[:, v, c * P:(c + 1) * P], ident[:, :])
            ins.then_inc(set_pe, 1)
            def as_rows(bank, w512, cond):
                for c in range(KC):
                    for i, w in enumerate(w512):
                        ins = pe.matmul(ps[32 * i:32 * i + 32, bank, 0:w.shape[2]], cond[:, c, :], w[:, c, :], start=c == 0, stop=c == KC - 1)
                ins.then_inc(mrow_done, 1)

            def as_columns(bank, r, w512):
                for q in range(4):
                    n = 32 * sum(w.shape[2] > P * q for w in w512)
                    ins = pe.transpose(ps[:, bank, q * P:q * P + n], s_mrow[r][0:n, q * P:(q + 1) * P], ident[0:n, 0:n])
                return ins

            pe.wait_ge(s_mod_ld, 4 * 16)
            pe.wait_ge(set_act, 1)
            lots = [w[:, :, o:min(o + 512, w.shape[2])] for w in (s_ss_q, s_ss_kv, s_mod, s_ada) for o in range(0, w.shape[2], 512)]
            lots = [lots[0:4], lots[4:8], lots[8:]]
            for r in range(3):
                as_rows(4 + r, lots[r], s_silu)
            for r in range(3):
                pe.wait_ge(mrow_copied, r + 1)
                ins = as_columns(4 + r, r, lots[r])
            ins.then_inc(set_pe, 1)
            pe.wait_ge(s_l1_ld, 13 * 16)
            pe.wait_ge(set_act, 2)
            anchor = [s_an[:, e] for e in range(E)] + [s_gan]
            as_rows(7, anchor, s_cond)
            pe.wait_ge(mrow_copied, 4)
            as_columns(7, 3, anchor)
            for b in range(B):
                for c in range(KC):
                    ins = pe.matmul(ps[:, 7, 480 + b * 4:480 + b * 4 + E], s_crep[:, c, b, :], s_ran[:, c, :], start=c == 0, stop=c == KC - 1)
            ins.then_inc(set_pe, 1)
            pe.wait_ge(set_dve, 3)
            for i in range(KC):
                for j in range(KC):
                    ins = pe.transpose(ps[:, 6, (j * KC + i) * P:(j * KC + i + 1) * P], s_q1[:, i, j * P:(j + 1) * P], ident[:, :])
            ins.then_inc(set_pe, 1)
            pe.wait_ge(s_kv_ld, 3 * 16)
            pe.wait_ge(set_act, 3)

            def key(bank, slot, w, m, v):
                for c in range(KC):
                    ins = pe.matmul(ps[:, bank, slot * P:(slot + 1) * P], w[:, c, m * P:(m + 1) * P], s_ctxT[:, v, c, :, 0, :],
                                    start=c == 0, stop=c == KC - 1)
                return ins
            for m in range(KC):
                key(0, m, s_kv0, m, 0)
                key(0, KC + m, s_kvc, m, 1)
                key(1, m, s_kv3, m, 2)
                key(1, KC + m, s_k1, m, 2)
                ins = key(2, m, s_v1, m, 2)
            ins.then_inc(set_pe, 1)
            pe.wait_ge(set_dve, 4)
            for i, (bank, w) in enumerate(((3, s_kv0), (6, s_kvc), (7, s_kv3))):
                for b in range(B):
                    for c in range(KC):
                        ins = pe.matmul(ps[:, bank, b * D:(b + 1) * D], s_ctxT[:, i, c, b, :, :].rearrange("p a s -> p (a s)"),
                                        w[:, c, D:2 * D], start=c == 0, stop=c == KC - 1)
            ins.then_inc(set_pe, 1)
            pe.wait_ge(set_dve, 5)
            for i in range(KC):
                for j in range(KC):
                    ins = pe.matmul(ps[:, 0, i * P:(i + 1) * P], s_wqT[:, j, i * P:(i + 1) * P], s_k1T[:, j, :], start=j == 0, stop=j == KC - 1)
            for b in range(B):
                for c in range(KC):
                    lhsT = s_vT[:, c, b, :, :].rearrange("p a s -> p (a s)")
                    st_, sp_ = c == 0, c == KC - 1
                    pe.matmul(ps[:, 0, D + b * 4:D + b * 4 + E], lhsT, s_rev[:, c, :], start=st_, stop=sp_)
            for b in range(B):
                for c in range(KC):
                    lhsT = s_vT[:, c, b, :, :].rearrange("p a s -> p (a s)")
                    pe.matmul(ps[:, 1, b * D:(b + 1) * D], lhsT, s_gev[:, c, :], start=c == 0, stop=c == KC - 1)
            pe.wait_ge(set_dve, 6)
            for b in range(B):
                for e in range(E):
                    for c in range(KC):
                        lhsT = s_vT[:, c, b, :, :].rearrange("p a s -> p (a s)")
                        ins = pe.matmul(ps[:, 2 + b * E + e, :], lhsT, s_ev[:, e, c, :], start=c == 0, stop=c == KC - 1)
            ins.then_inc(set_pe, 1)

            pe.wait_ge(set_dve, 7)
            with pe.Fori(0, B) as b:
                def ln(i, k, bank=None):
                    pe.wait_ge(xhat_ready, b * 2 * N_LN + 2 * i + k + 1)
                    turn_block(k, xhat, bank).then_inc(ln_turned, 1)

                def query(i, k, ln_i, w):
                    pe.wait_ge(hT_ready, b * (2 * N_LN + 2) + ln_i + k + 1)
                    linear(4 * k + 2, w, 0, hT[:, k])
                    linear(4 * k + 3, w, 1, hT[:, k]).then_inc(q_done, 1)

                def residual(i, k, turn, w=None, o_wait=None, src=oT, bank=None):
                    if not turn:
                        bank = 4 * k + 2 if bank is None else bank
                        pe.wait_ge(*o_wait)
                        linear(bank, w, 0, src[:, k])
                        linear(bank + 1, w, 1, src[:, k]).then_inc(y_done, 1)
                    else:
                        bank = 4 * k if bank is None else bank
                        pe.wait_ge(yT_ready, b * 2 * N_RES + 2 * i + k + 1)
                        for t in range(TB):
                            for c in range(KC):
                                ins = pe.transpose(ps[:, bank + t // 2, t % 2 * D + c * P:t % 2 * D + (c + 1) * P],
                                                   yT[:, k, c, t * P:(t + 1) * P], ident[:, :])
                        ins.then_inc(y_turned, 1)

                def context_attention(i, norm, col, wq, step, w):
                    u0 = b * 2 * T + T * i

                    def scores(t):
                        if t % TB == 0:
                            pe.wait_ge(qT_ready, b * 2 * N_Q + 2 * i + t // TB + 1)
                        if t == 0:
                            pe.wait_ge(kblk_ready, b * N_CA + i + 1)
                        if t >= 2:
                            pe.wait_ge(s_read, u0 + t - 1)
                        for c in range(KC):
                            ins = pe.matmul(ps[:, 2 * (t % 2) + c, :], qT[:, t // TB, c, t % TB * P:(t % TB + 1) * P],
                                            kblk[:, c, :, :].rearrange("p h s -> p (h s)"), start=True, stop=True)
                        ins.then_inc(s_ready, 1)

                    def turn(t):
                        pe.wait_ge(p_exp, u0 + t + 1)
                        if t:
                            pe.wait_ge(pT_ready, u0 + t)
                        for j in range(HC):
                            ins = pe.transpose(ps[:, 4 + j // 4, j % 4 * P:(j % 4 + 1) * P], prob[:, t % 2, j * P:(j + 1) * P], ident[:, :])
                        ins.then_inc(p_turned, 1)

                    def values(t):
                        pe.wait_ge(pT_ready, u0 + t + 1)
                        if t == 0:
                            pe.wait_ge(qT_ready, b * 2 * N_Q + 2 * i + 2)
                        else:
                            pe.wait_ge(o_ready, u0 + t)
                        for j in range(HC):
                            ins = pe.matmul(ps[:, 6, 64 * j:64 * (j + 1)], probT[:, t % 2, j, :], vx[:, j, :], start=True, stop=True)
                        ins.then_inc(pv_done, 1)

                    def turn_outputs(t):
                        pe.wait_ge(o_ready, u0 + t + 1)
                        if t:
                            pe.wait_ge(oT_ready, u0 + t)
                        for c in range(KC):
                            ins = pe.transpose(ps[:, 7, t % 2 * D + c * P:t % 2 * D + (c + 1) * P], o_tok[:, t % 2, c * P:(c + 1) * P], ident[:, :])
                        ins.then_inc(o_turned, 1)

                    ln(norm, 0)
                    query(i, 0, col, wq)
                    ln(norm, 1)
                    scores(0)
                    scores(1)
                    query(i, 1, col, wq)
                    for t in range(T + 2):
                        if t + 2 < T:
                            scores(t + 2)
                        if t < T:
                            turn(t)
                        if 1 <= t <= T:
                            values(t - 1)
                        if t >= 2:
                            turn_outputs(t - 2)
                        if t == T - 2:
                            pe.wait_ge(s_read, u0 + T - 1)
                            residual(step, 0, False, w, (oT_ready, u0 + TB), bank=0)
                        if t == T - 1:
                            residual(step, 0, True)
                    residual(step, 1, False, w, (oT_ready, u0 + T))
                    ln(step + 1, 0)

                pe.wait_ge(ra_ld, b * N_RA + N_RA)
                pe.wait_ge(begun, b + 1)
                context_attention(0, 0, 0, wq0, 0, wp0)

                def evidence_scores(k):
                    pe.wait_ge(hT_ready, b * (2 * N_LN + 2) + 2 + k + 1)
                    for t in range(TB):
                        for c in range(KC):
                            ins = pe.matmul(ps[:, 4 * k + 3, t * (S + E):(t + 1) * (S + E)], hT[:, k, c, t * P:(t + 1) * P], kw[:, c, :],
                                            start=c == 0, stop=c == KC - 1)
                    ins.then_inc(p1s_done, 1)

                def gate_tokens(k):
                    for m in range(KC):
                        for c in range(KC):
                            pe.matmul(ps[:, 4 * k + 1 + m, :], wg1[:, c, m * P:(m + 1) * P], hT[:, k, c, :], start=c == 0, stop=False)

                def turn_evidence(k):
                    pe.wait_ge(p1_ready, b * NB + k + 1)
                    pe.sem_inc(passed, 1)
                    for t in range(TB):
                        ins = pe.transpose(ps[:, 4 * k, t * P:(t + 1) * P], p1[:, k, t, :, :].rearrange("p a s -> p (a s)"), ident[:, :])
                    ins.then_inc(p1_turned, 1)

                def through_evidence(bank, m, k):
                    pe.matmul(ps[:, bank, :], vw[:, m * P:(m + 1) * P], p1T[:, k, :], start=False, stop=False)
                    return pe.matmul(ps[:, bank, :], vw[0:S, m * P:(m + 1) * P], p1lo[:, k, :], start=False, stop=True)

                def add_evidence(k):
                    pe.wait_ge(p1T_ready, b * NB + k + 1)
                    if k == 0:
                        pe.wait_ge(vw_ready, b + 1)
                    for t in range(TB):
                        rows, cols = slice(t * P, (t + 1) * P), slice(MC * P + D, MC * P + D + E)
                        pe.matmul(ps[:, 4 * k, t * E:(t + 1) * E], p1T[:, k, rows].bitcast(F32), vw[:, cols].bitcast(F32), start=True, stop=False)
                        ins = pe.matmul(ps[:, 4 * k, t * E:(t + 1) * E], p1lo[:, k, rows].bitcast(F32), vw[0:S, cols].bitcast(F32), start=False, stop=True)
                    ins.then_inc(lg_done, 1)
                    for m in range(KC):
                        ins = through_evidence(4 * k + 1 + m, MC + m, k)
                    ins.then_inc(g1_done, 1)

                evidence_scores(0)
                residual(0, 1, True)
                gate_tokens(0)
                ln(1, 1)
                turn_evidence(0)
                evidence_scores(1)
                add_evidence(0)
                gate_tokens(1)
                turn_evidence(1)
                add_evidence(1)
                for k in range(NB):
                    pe.wait_ge(lg_ready, b * NB + k + 1)
                    pe.sem_inc(passed, 1)
                    for t in range(TB):
                        ins = pe.transpose(ps[0:E, 4 * k + 3, t * P:(t + 1) * P], lg[:, k, t, :], ident[:, :])
                    ins.then_inc(lg_turned, 1)
                for k in range(NB):
                    pe.wait_ge(g1_ready, b * NB + k + 1)
                    for m in range(KC):
                        ins = linear(4 * k + 1 + m, wg2, m, g1[k])
                    ins.then_inc(g2_done, 1)
                for k in range(NB):
                    pe.wait_ge(pT_made, b * NB + k + 1)
                    pe.wait_ge(gT_ready, b * NB + k + 1)
                    for e in range(E):
                        ins = pe.matmul(ps[:, 4 * k + e, :], sel3[:, e, :], pT[:, k, :], start=True, stop=True)
                    ins.then_inc(pbc_done, 1)
                n0 = b * 2 * MC

                def routed_out(k):
                    pe.wait_ge(rT_ready, b * NB + k + 1)
                    for m in range(KC):
                        ins = linear(4 + 2 * k + m, wout, m, rT[k])
                    ins.then_inc(y_done, 1)

                for k in range(NB):
                    pe.wait_ge(pbc_ready, b * NB + NB)
                    for m in range(KC):
                        pe.matmul(ps[:, 4 + 2 * k + m, :], b2[:, m * P:(m + 1) * P], pT[:, k, :], start=True, stop=False)
                    for m in range(MC + 2):
                        n = k * MC + m
                        if m < MC:
                            if n >= 4:
                                pe.wait_ge(h1_act, n0 + n - 3)
                            bank = n % 4
                            for c in range(KC):
                                pe.matmul(ps[:, bank, :], w1[:, m // 4, c, m % 4 * P:(m % 4 + 1) * P], hT[:, k, c, :], start=c == 0, stop=False)
                            through_evidence(bank, m, k).then_inc(h1_done, 1)
                        if m >= 2:
                            pe.wait_ge(h1_ready, n0 + n - 1)
                            for j in range(KC):
                                ins = pe.matmul(ps[:, 4 + 2 * k + j, :], w2[:, m - 2, j * P:(j + 1) * P], ring[:, (n - 2) % 4, :],
                                                start=False, stop=m == MC + 1)
                            ins.then_inc(w2_done, 1)
                        if k == 1 and m == 3:
                            routed_out(0)
                        if k == 1 and m == 6:
                            residual(1, 0, True, bank=4)
                        if k == 1 and m == 10:
                            ln(2, 0, bank=4)

                def values(k):
                    pe.wait_ge(hT_ready, b * (2 * N_LN + 2) + 4 + k + 1)
                    for t in range(TB):
                        for c in range(KC):
                            ins = pe.matmul(ps[:, 4 * k + 2 + t // 2, t % 2 * D:(t % 2 + 1) * D], hT[:, k, c, t * P:(t + 1) * P],
                                            wv2[:, c, :], start=c == 0, stop=c == KC - 1)
                    ins.then_inc(v_done, 1)

                values(0)
                routed_out(1)
                linear(0, wqk2, 0, hT[:, 0])
                pe.wait_ge(v_ready, b * NB + 1)
                linear(2, wqk2, KC, hT[:, 0])
                residual(1, 1, True)
                ln(2, 1)
                values(1)
                uses, read_by = [0, 0], [None, None]

                def take(sem, n):
                    place = uses[0] % 2
                    uses[0] += 1
                    if read_by[place]:
                        pe.wait_ge(*read_by[place])
                    read_by[place] = sem, n
                    return 2 * place

                def take_dve():
                    uses[1] += 1
                    return take(ring_read, b * N_SCORE + uses[1])

                def take_act():
                    return take(spread_read, b * N_SPREAD + uses[0] - uses[1] + 1)

                def queries_keys(c, qk, bank, blocks=range(NB)):
                    for k in blocks:
                        ins = linear(bank + k, wqk2, qk * KC + c, hT[:, k])
                    return ins

                def spread(p, qk):
                    bank = take_act()
                    for half in range(2):
                        for part in range(2):
                            ins = pe.matmul(ps[:, bank + half, :], sel[:, p % 4, 2 * qk + part, :],
                                            dense[2 * qk + part][:, half * 512:(half + 1) * 512], start=part == 0, stop=part == 1)
                    ins.then_inc(ring_ready, 1)

                def query_scores(p, u):
                    e, t = 1 - u % 2, u // 2
                    r = slice(64 * e, 64 * e + 64)
                    bank = take_dve()
                    for half in range(2):
                        ins = pe.matmul(ps[:, bank + half, :], qx[r, p % 4, t * P:(t + 1) * P], kx[r, p % 4, half * 512:(half + 1) * 512],
                                        start=True, stop=True)
                    ins.then_inc(ring_ready, 1)

                def turn_maxima(p):
                    bank = take_dve()
                    pe.wait_ge(mt_ready, b * NP + p + 1)
                    for t in range(T):
                        ins = pe.transpose(ps[:, bank + t // TB, t % TB * P:(t % TB + 1) * P], mt[:, t, :], ident[:, :])
                    ins.then_inc(ring_ready, 1)

                def key_scores(p, u, half):
                    kc, e = u // 2, u % 2
                    r = slice(64 * e, 64 * e + 64)
                    n = 2 * (2 * T * p + u) + half
                    if n >= 3:
                        pe.wait_ge(pt_ready, b * 4 * T * NP + n - 2)
                    pe.matmul(ps[:, 4 + n % 3, :], kx[r, p % 4, kc * P:(kc + 1) * P], qx[r, p % 4, half * 512:(half + 1) * 512],
                              start=True, stop=True).then_inc(st_ready, 1)

                def weigh_values(w):
                    p, kc = w // T, w % T
                    pe.wait_ge(pt_ready, b * 4 * T * NP + 4 * w + 4)
                    if kc == 0 and p >= 1:
                        pe.wait_ge(acc_read, b * NP + p)
                    for e in range(2):
                        for half in range(2):
                            o = 32 * (2 * e + half)
                            ins = pe.matmul(ps[o:o + 32, 7, :], v2[:, kc, VS * (2 * p + e):VS * (2 * p + e) + 32],
                                            pt[:, (2 * kc + e) % 8, half * 512:(half + 1) * 512], start=kc == 0, stop=kc == T - 1)
                    ins.then_inc(pv2_done, 1)

                def finish(p):
                    bank = take_dve()
                    pe.wait_ge(acc_read, b * NP + p + 1)
                    for j in range(TB):
                        ins = pe.transpose(ps[:, bank, j * P:(j + 1) * P], accS[:, p % 2, j * P:(j + 1) * P], ident[:, :])
                    ins.then_inc(ring_ready, 1)

                for qk in range(2):
                    queries_keys(0, qk, take_dve(), (1,)).then_inc(ring_ready, 1)
                pe.wait_ge(ring_read, b * N_SCORE + 2)
                for qk in range(2):
                    spread(0, qk)
                with_maximum = []
                for n in range(-LEAD, UNITS):
                    (p, u), m = divmod(n, 2 * T), n + LEAD
                    if n >= 0:
                        if n == 0:
                            pe.wait_ge(full_ready, b + 1)
                        if u == 0:
                            pe.wait_ge(ring_read, b * N_SCORE + with_maximum[p])
                        key_scores(p, u, 0)
                    if m < 2 * NB:
                        qk, k = divmod(m, NB)
                        if m == NB:
                            pe.wait_ge(v_ready, b * NB + NB)
                        ins = queries_keys(1, qk, 4 + 2 * qk, (k,))
                        if m == 2 * NB - 1:
                            ins.then_inc(full_done, 1)
                            pe.wait_ge(v2_clear, b + 1)
                    if m < UNITS:
                        if m % (2 * T) == 0:
                            pe.wait_ge(spread_read, b * N_SPREAD + 2 * (m // (2 * T)) + 2)
                        query_scores(m // (2 * T), m % (2 * T))
                    if n >= 0:
                        key_scores(p, u, 1)
                    if n >= 5 and n % 4 == 1:
                        weigh_values((n - 5) // 2)
                        weigh_values((n - 3) // 2)
                    q, at_m = divmod(m, 2 * T)
                    if at_m == 2 and 1 <= q <= NP:
                        turn_maxima(q - 1)
                        with_maximum.append(uses[1])
                    if at_m in (8, 12) and q + 1 < NP:
                        if q + 1 == NP // 2 and at_m == 8:
                            pe.wait_ge(lo_ready, b * 2 + 2)
                        spread(q + 1, (at_m - 8) // 4)
                    if u == 13 and p >= 1:
                        finish(p - 1)
                weigh_values(T * NP - 2)
                weigh_values(T * NP - 1)
                finish(NP - 1)
                assert uses == [N_RING, N_SCORE]

                for k in range(NB):
                    pe.wait_ge(ring_read, b * N_SCORE + N_SCORE)
                    turn_block(k, xhat).then_inc(ot_turned, 1)
                pe.wait_ge(rc1_ld, 9 * 16)
                for k in range(NB):
                    residual(2, k, False, wproj, (hT_ready, b * (2 * N_LN + 2) + 6 + k + 1), hT)
                for k in range(NB):
                    residual(2, k, True)

                context_attention(1, 3, 8, wqc, 3, wcp)

                TERMS = ((0, 0), (1, 0), (0, 1))
                n0 = b * 2 * NC_HID

                def hidden_features(k, m):
                    for wp, sp in TERMS:
                        if m == 0 and sp == 1:
                            pe.wait_ge(hs_lo, b * NB + k + 1)
                        for c in range(KC):
                            ins = pe.matmul(ps[:, m % 4, :], w1s[:, wp, c, m * P:(m + 1) * P], hs[:, k, sp, c, :],
                                            start=(wp, sp, c) == (0, 0, 0), stop=(sp, c) == (1, KC - 1))
                    ins.then_inc(h2_done, 1)

                def hidden_out(k, m):
                    for j in range(KC):
                        for wp, sp in TERMS:
                            ins = pe.matmul(ps[:, 4 + 2 * k + j, :], w2s[:, wp, m, j * P:(j + 1) * P], gelus[sp][:, m % 4, :],
                                            start=m == 0 and (wp, sp) == (0, 0), stop=m == NC_HID - 1 and sp == 1)
                    ins.then_inc(w22_done, 1)

                pe.wait_ge(w_split, b * 2 + 2)
                for k in range(NB):
                    pe.wait_ge(hT_ready, b * (2 * N_LN + 2) + 10 + k + 1)
                    for m in range(NC_HID + 2):
                        n = k * NC_HID + m
                        if m < NC_HID:
                            if n >= 4:
                                pe.wait_ge(h2_ready, n0 + n - 3)
                            hidden_features(k, m)
                        if m >= 2:
                            pe.wait_ge(h2_lo, n0 + n - 1)
                            hidden_out(k, m - 2)
                        if k == 0 and m == 1:
                            residual(3, 1, True, bank=6)
                        if k == 0 and m == 5:
                            ln(4, 1, bank=6)
                        if k == 1 and m == 4:
                            residual(4, 0, True, bank=4)
                        if k == 1 and m == 7:
                            ln(5, 0, bank=4)

                def window_queries_keys(k):
                    pe.wait_ge(hT_ready, b * (2 * N_LN + 2) + 12 + k + 1)
                    for m in range(2 * KC):
                        ins = linear(4 * k + m, wqkv3, m, hT[:, k])
                    ins.then_inc(qk3_done, 1)

                def window_v(k):
                    pe.wait_ge(qk3_ready, b * NB + k + 1)
                    for t in range(TB):
                        for c in range(KC):
                            ins = pe.matmul(ps[:, 4 * k + t // 2, t % 2 * D:(t % 2 + 1) * D], hT[:, k, c, t * P:(t + 1) * P],
                                            wqkv3[:, c, 2 * D:3 * D], start=c == 0, stop=c == KC - 1)
                    ins.then_inc(v3_done, 1)

                window_queries_keys(0)
                residual(4, 1, True)
                window_v(0)
                ln(5, 1)
                u0 = b * N_UNIT

                def window_scores(u):
                    t, c = u // KC, u % KC
                    pe.wait_ge(wk_ready, u0 + u + 1)
                    if u == 0:
                        pe.wait_ge(v3_ready, b * NB + 1)
                    if u >= 2:
                        pe.wait_ge(ws_read, u0 + u - 1)
                    for half in range(2):
                        ins = pe.matmul(ps[:, 2 * (u % 2) + half, :], qT[:, t // TB, c, t % TB * P:(t % TB + 1) * P],
                                        wkblk[:, u % 2, 4 * half:4 * half + 4, :].rearrange("p h s -> p (h s)"), start=True, stop=True)
                    ins.then_inc(ws_ready, 1)

                def window_turn(u):
                    pe.wait_ge(wp_exp, u0 + u + 1)
                    if u == 0:
                        pe.wait_ge(v3_ready, b * NB + NB)
                        pe.wait_ge(v3_clear, b + 1)
                    else:
                        pe.wait_ge(wpT_ready, u0 + u)
                    for j in range(HC):
                        ins = pe.transpose(ps[:, 4 + j // 4, j % 4 * P:(j % 4 + 1) * P], prob[:, u % 2, j * P:(j + 1) * P], ident[:, :])
                    ins.then_inc(wp_turned, 1)

                def window_values(u):
                    t, c = u // KC, u % KC
                    pe.wait_ge(wpT_ready, u0 + u + 1)
                    if u >= 2:
                        pe.wait_ge(wo_ready, u0 + u - 1)
                    for part in range(2):
                        for odd in range(2):
                            for j in range(4):
                                h = 2 * j + odd
                                lhsT = v3[:, t, HC * c + h, :] if part == 0 else ones_win[:, odd, :]
                                ins = pe.matmul(ps[32 * j:32 * j + 32, 6 + u % 2, part * P:(part + 1) * P], lhsT, wprobT[:, u % 2, h, :],
                                                start=odd == 0, stop=odd == 1)
                    ins.then_inc(wpv_done, 1)

                window_scores(0)
                window_scores(1)
                window_queries_keys(1)
                window_v(1)
                window_turn(0)
                for u in range(N_UNIT):
                    if u + 2 < N_UNIT:
                        window_scores(u + 2)
                    window_values(u)
                    if u + 1 < N_UNIT:
                        window_turn(u + 1)
                    if u == N_UNIT - 2:
                        pe.wait_ge(ws_read, u0 + N_UNIT - 1)
                        residual(5, 0, False, wso, (wo_ready, u0 + N_UNIT // 2), bank=0)
                residual(5, 0, True)
                residual(5, 1, False, wso, (wo_ready, u0 + N_UNIT))

                t0 = b * T

                def top_scores(t):
                    if t % TB == 0:
                        pe.wait_ge(qT_ready, b * 2 * N_Q + 4 + t // TB + 1)
                    if t == 0:
                        pe.wait_ge(kblk_ready, b * N_CA + 3)
                    else:
                        pe.wait_ge(ts_read, t0 + t)
                    for c in range(KC):
                        ins = pe.matmul(ps[:, c, :], qT[:, t // TB, c, t % TB * P:(t % TB + 1) * P],
                                        kblk[:, c, :, :].rearrange("p h s -> p (h s)"), start=True, stop=True)
                    ins.then_inc(ts_ready, 1)

                def top_turn(t):
                    pe.wait_ge(top_ready, t0 + t + 1)
                    if t == 0:
                        pe.wait_ge(qT_ready, b * 2 * N_Q + 6)
                    else:
                        pe.wait_ge(toT_ready, t0 + t)
                    for half in range(2):
                        if half and t:
                            pe.wait_ge(to_ready, t0 + t)
                        for j in range(4):
                            ins = pe.transpose(ps[:, 2 + half, j * P:(j + 1) * P], prob3[:, t % 3, (4 * half + j) * P:(4 * half + j + 1) * P], ident[:, :])
                        ins.then_inc(tp_turned, 1)

                def top_values(t):
                    pe.wait_ge(tpT_ready, t0 * 2 + 2 * t + 2)
                    for j in range(HC):
                        ins = pe.matmul(ps[:, 3, 64 * j:64 * (j + 1)], probT[:, t % 2, j, :], vx[:, j, :], start=True, stop=True)
                    ins.then_inc(tpv_done, 1)

                def top_turn_outputs(t):
                    pe.wait_ge(to_ready, t0 + t + 1)
                    for c in range(KC):
                        ins = pe.transpose(ps[:, 2, c * P:(c + 1) * P], o_tok[:, t % 2, c * P:(c + 1) * P], ident[:, :])
                    ins.then_inc(to_turned, 1)

                n0 = b * NB * NC_HID

                def up(n):
                    k, m = n // NC_HID, n % NC_HID
                    if m == 0:
                        pe.wait_ge(hT_ready, b * (2 * N_LN + 2) + 16 + k + 1)
                    if n == 0:
                        pe.wait_ge(rc2_ld, b * 32 + 32)
                    else:
                        pe.wait_ge(h3_read, n0 + n)
                    linear(4, w3a, m, hT[:, k]).then_inc(h3_done, 1)
                    linear(5, w3a, NC_HID + m, hT[:, k]).then_inc(h3_done, 1)

                def down(n):
                    k, m = n // NC_HID, n % NC_HID
                    pe.wait_ge(h3_ready, n0 + n + 1)
                    for j in range(KC):
                        ins = pe.matmul(ps[:, 6 * (1 - k) + j, :], w3b[:, m, j * P:(j + 1) * P], gate3[k][:, m % 4, :],
                                        start=m == 0, stop=m == NC_HID - 1)
                    ins.then_inc(w32_done, 1)

                ln(6, 0)
                residual(5, 1, True)
                query(2, 0, 14, wq3)
                top_scores(0)
                ln(6, 1)
                query(2, 1, 14, wq3)
                top_scores(1)
                for t in range(TB):
                    top_scores(t + 2)
                    if t:
                        top_turn_outputs(t - 1)
                    top_turn(t)
                    top_values(t)
                top_turn_outputs(3)
                residual(6, 0, False, wco, (toT_ready, t0 + TB), bank=6)
                top_scores(6)
                top_turn(4)
                residual(6, 0, True, bank=6)
                top_values(4)
                top_scores(7)
                ln(7, 0, 6)
                up(0)
                top_turn_outputs(4)
                top_turn(5)
                top_values(5)
                up(1)
                down(0)
                up(2)
                top_turn_outputs(5)
                down(1)
                up(3)
                top_turn(6)
                top_values(6)
                down(2)
                up(4)
                top_turn_outputs(6)
                down(3)
                up(5)
                top_turn(7)
                top_values(7)
                down(4)
                up(6)
                top_turn_outputs(7)
                residual(6, 1, False, wco, (toT_ready, t0 + T), bank=2)
                down(5)
                up(7)
                residual(6, 1, True, bank=2)
                down(6)
                ln(7, 1, 2)
                down(7)
                for n in range(NC_HID, 2 * NC_HID + 2):
                    if n < 2 * NC_HID:
                        up(n)
                    if n == NC_HID + 2:
                        residual(7, 0, True, bank=6)
                    if n >= NC_HID + 2:
                        down(n - 2)
                residual(7, 1, True, bank=0)

        @block.scalar
        def _(act):
            def affine(dst, src, scale, bias):
                return act.activation(dst, src, ACT.Identity, bias=bias, scale=scale)


            for tile, name in ((s_ss_q, "L0_xcond_Wss_q"), (s_ss_kv, "L0_xcond_Wss_kv"), (s_mod, "L2_xcond_W_mod"),
                               (s_ada, "L3_xcond_w_ada")):
                act.dma_start(tile[:, :, :], rows(g[name])).then_inc(s_mod_ld, 16)
            for tile, name in ((s_kv0, "L0_xcond_Wkv"), (s_kvc, "L2_xcond_W_kvc"), (s_kv3, "L3_xcond_w_kv")):
                act.dma_start(tile[:, :, :], rows(g[name])).then_inc(s_kv_ld, 16)


            act.wait_ge(set_dve, 2)
            act.wait_ge(set_pool, 1)
            cond = colT[:, C_COND:C_COND + B * KC].rearrange("p (b c) -> p c b", c=KC)
            act.activation(s_silu[:, :, 0:B], cond, ACT.Silu).then_inc(set_act, 1)
            act.activation(s_cond[:, :, 0:B], cond, ACT.Copy)
            for bb in range(B):
                for c in range(KC):
                    col = C_COND + bb * KC + c
                    ins = act.activation(s_crep[:, c, bb, :], colT[:, col:col + 1].broadcast_to([P, P]), ACT.Copy)
            ins.then_inc(set_act, 1)
            act.wait_ge(set_pe, 2)
            for v in (1, 2):
                for c in range(KC):
                    for dup in range(2):
                        ins = act.activation(s_ctxT[:, v, c, :, dup, :], ps[:, 1 + v, c * P:(c + 1) * P].rearrange("p (b s) -> p b s", b=B), ACT.Copy)
            ins.then_inc(set_act, 1)
            for r, parts in enumerate((((P, 0, 512),), ((P, 0, 512),), ((64, 0, 256), (32, 256, 512)), ((P, 0, 256), (96, 256, 512)))):
                act.wait_ge(mrow_done, r + 1)
                for n, o, z in parts:
                    ins = act.activation(s_mrow[r][0:n, o:z], ps[0:n, 4 + r, o:z], ACT.Copy)
                ins.then_inc(mrow_copied, 1)
            act.wait_ge(set_pe, 8)
            for bb in range(B):
                for e in range(E):
                    act.activation(vw2[:, bb, e * RH:(e + 1) * RH], ps[:, 2 + bb * E + e, :], ACT.Copy)
                act.activation(vw2[:, bb, MC * P:MC * P + D], ps[:, 1, bb * D:(bb + 1) * D], ACT.Copy)
            act.wait_ge(set_dve, 7)
            for bb in range(B):
                ins = act.activation(vw2[:, bb, MC * P + D:MC * P + D + E], ps[:, 0, D + bb * 4:D + bb * 4 + E], ACT.Copy)
            ins.then_inc(set_act, 1)

            act.wait_ge(set_pe, 8)
            act.wait_ge(set_act, 4)
            act.wait_ge(set_dve, 7)
            for tile, name in ((wproj, "L2_xcond_W_proj"), (wqc, "L2_xcond_W_qc"), (wcp, "L2_xcond_W_cproj"),
                               (wm1, "L2_xcond_W_mlp1"), (wm2, "L2_xcond_W_mlp2"), (wqkv3, "L3_xcond_w_qkv"),
                               (wso, "L3_xcond_w_so"), (wq3, "L3_xcond_w_q"), (wco, "L3_xcond_w_co")):
                act.dma_start(tile[:, :, :], rows(g[name])).then_inc(rc1_ld, 16)

            with act.Fori(0, B) as b:
                act.wait_ge(begun, b + 1)

                def ln(i, k, cols, bank=None):
                    bank = 4 * k if bank is None else bank
                    act.wait_ge(ln_turned, b * 2 * N_LN + 2 * i + k + 1)
                    for c in range(KC):
                        if cols is None:
                            ins = act.activation(hT[:, k, c, :], ps[:, bank + c, :], ACT.Copy)
                        else:
                            table, scale, bias = cols
                            ins = affine(hT[:, k, c, :], ps[:, bank + c, :], table[:, scale + c:scale + c + 1], table[:, bias + c:bias + c + 1])
                        if i == 4:
                            ins = affine(hs[:, k, 0, c, :], ps[:, bank + c, :], table[:, scale + c:scale + c + 1], table[:, bias + c:bias + c + 1])
                    ins.then_inc(hT_ready, 1)

                def query(i, k, col):
                    act.wait_ge(q_done, b * 2 * N_Q + 2 * i + k + 1)
                    for c in range(KC):
                        ins = affine(qT[:, k, c, :], ps[:, 4 * k + 2 + c, :], 1.0, colT[:, col + c:col + c + 1])
                    ins.then_inc(qT_ready, 1)

                def residual(k, bank, scale, bias):
                    for c in range(KC):
                        ins = affine(yT[:, k, c, :], ps[:, bank + c, :], 1.0 if scale is None else mod[:, scale + c:scale + c + 1],
                                     bias[:, c:c + 1])
                    ins.then_inc(yT_ready, 1)

                def context_attention(i, norm, norm_cols, col, done, scale, bias, next_ln, cols):
                    u0 = b * 2 * T + T * i

                    def exp(t):
                        act.wait_ge(s_read, u0 + t + 1)
                        act.activation(prob[:, t % 2, :], prob[:, t % 2, :], ACT.Exp, scale=QK_SCALE).then_inc(p_exp, 1)

                    def copy(t):
                        act.wait_ge(p_turned, u0 + t + 1)
                        if t >= 2:
                            act.wait_ge(pv_done, u0 + t - 1)
                        act.activation(probT[:, t % 2, :, :], ps[:, 4:6, :].rearrange("p a (j q) -> p (a j) q", q=P), ACT.Copy).then_inc(pT_ready, 1)

                    def outputs(t):
                        act.wait_ge(o_turned, u0 + t + 1)
                        act.activation(oT[:, t // TB, :, t % TB * P:(t % TB + 1) * P], ps[:, 7, t % 2 * D:(t % 2 + 1) * D].rearrange("p (c q) -> p c q", c=KC),
                                       ACT.Copy).then_inc(oT_ready, 1)
                    ln(norm, 0, norm_cols)
                    query(i, 0, col)
                    ln(norm, 1, norm_cols)
                    exp(0)
                    query(i, 1, col)
                    for t in range(T + 2):
                        if t + 1 < T:
                            exp(t + 1)
                        if t < T:
                            copy(t)
                        if t >= 2:
                            outputs(t - 2)
                        if t == T - 2:
                            act.wait_ge(y_done, b * 12 + done + 1)
                            residual(0, 0, scale, bias)
                    act.wait_ge(y_done, b * 12 + done + 2)
                    residual(1, 6, scale, bias)
                    ln(next_ln, 0, cols)

                context_attention(0, 0, (mod, M_SC_Q, M_SH_Q), C_BQ0, 0, None, colT[:, C_BP0:C_BP0 + KC], 1, (colT, C_GAMMA, C_BETA))

                def evidence_exp(k):
                    act.wait_ge(p1_sub, b * NB + k + 1)
                    act.activation(p1[:, k, :, 0, :], p1[:, k, :, 0, :], ACT.Exp, scale=L1_SCALE).then_inc(p1_exp, 1)

                def evidence_turned(k):
                    act.wait_ge(p1_turned, b * NB + k + 1)
                    act.activation(p1T[:, k, :], ps[:, 4 * k, :], ACT.Copy).then_inc(p1T_hi, 1)

                evidence_exp(0)
                ln(1, 1, (colT, C_GAMMA, C_BETA))
                evidence_turned(0)
                evidence_exp(1)
                evidence_turned(1)
                for k in range(NB):
                    act.wait_ge(lg_sub, b * NB + k + 1)
                    act.activation(lg[:, k, :, :], lg[:, k, :, :], ACT.Exp).then_inc(lg_exp, 1)
                for k in range(NB):
                    act.wait_ge(g1_done, b * NB + k + 1)
                    for m in range(KC):
                        ins = act.activation(g1[k][:, m, :], ps[:, 4 * k + 1 + m, :], ACT.Silu, bias=mod[:, M_HB + MC + m:M_HB + MC + m + 1])
                    ins.then_inc(g1_ready, 1)
                for k in range(NB):
                    act.wait_ge(lg_turned, b * NB + k + 1)
                    act.activation(pT[:, k, :], ps[0:E, 4 * k + 3, :], ACT.Copy).then_inc(pT_made, 1)
                for k in range(NB):
                    act.wait_ge(g2_done, b * NB + k + 1)
                    for m in range(KC):
                        ins = act.activation(gT[:, k, m, :], ps[:, 4 * k + 1 + m, :], ACT.Sigmoid, bias=colT[:, C_GB2 + m:C_GB2 + m + 1])
                    ins.then_inc(gT_ready, 1)
                for k in range(NB):
                    act.wait_ge(pbc_done, b * NB + k + 1)
                    for e in range(E):
                        ins = act.activation(p_bc[:, k, e, :], ps[:, 4 * k + e, :], ACT.Copy)
                    ins.then_inc(pbc_ready, 1)
                n0 = b * NB * MC

                def routed(k):
                    act.wait_ge(w2_done, n0 + k * MC + MC)
                    for c in range(KC):
                        ins = act.activation(rT[k][:, c, :], ps[:, 4 + 2 * k + c, :], ACT.Copy)
                    ins.then_inc(rT_ready, 1)
                for n in range(NB * MC):
                    act.wait_ge(h1_done, n0 + n + 1)
                    if n >= 4:
                        act.wait_ge(w2_done, n0 + n - 3)
                    m = n % MC
                    act.activation(ring[:, n % 4, :], ps[:, n % 4, :], ACT.Silu, bias=mod[:, M_HB + m:M_HB + m + 1]).then_inc(h1_act, 1)
                    if n == MC + 1:
                        routed(0)
                    if n == MC + 10:
                        ln(2, 0, (mod, M_SC_A, M_SH_A), 4)
                routed(1)

                ln(2, 1, (mod, M_SC_A, M_SH_A))
                u0 = b * N_RING
                uses = [0]

                def place():
                    n = uses[0]
                    uses[0] += 1
                    act.wait_ge(ring_ready, u0 + n + 1)
                    return ps[:, 2 * (n % 2):2 * (n % 2) + 2, :].rearrange("p a q -> p (a q)")

                def high_parts(c, qk):
                    if c == 0:
                        affine(dense[2 * qk][:, :], place(), 1.0, colT[:, C_BQ2 + (C_BK2 - C_BQ2) * qk:C_BQ2 + (C_BK2 - C_BQ2) * qk + 1]).then_inc(hi_ready, 1)
                    else:
                        act.activation(dense[2 * qk][:, :], full[qk], ACT.Copy).then_inc(hi_ready, 1)

                def spread(p, qk):
                    if qk == 0:
                        act.activation(qx[:, p % 4, :], place(), ACT.Copy).then_inc(spread_read, 1)
                    else:
                        affine(kx[:, p % 4, :], place(), 1.0, k_aug[:, 0:1]).then_inc(spread_read, 1)

                def probabilities(p, u):
                    for half in range(2):
                        n = 2 * (2 * T * p + u) + half
                        act.wait_ge(st_ready, b * 4 * T * NP + n + 1)
                        if u % 2 == 0 and half == 0 and n >= 16:
                            act.wait_ge(pv2_done, b * T * NP + n // 4 - 3)
                        act.activation(pt[:, u % 8, half * 512:(half + 1) * 512], ps[:, 4 + n % 3, :], ACT.Exp, scale=QK_SCALE).then_inc(pt_ready, 1)

                def outputs(p):
                    act.wait_ge(pv2_done, b * T * NP + T * p + T)
                    if p >= 2:
                        act.wait_ge(ring_ready, u0 + turned[p - 2])
                    act.activation(accS[:, p % 2, :], ps[:, 7, :], ACT.Copy).then_inc(acc_read, 1)

                for qk in range(2):
                    high_parts(0, qk)
                for qk in range(2):
                    spread(0, qk)
                act.wait_ge(full_done, b + 1)
                for qk in range(2):
                    col = (C_BQ2, C_BK2)[qk] + 1
                    ins = affine(full[qk], ps[:, 4 + 2 * qk:6 + 2 * qk, :].rearrange("p a q -> p (a q)"), 1.0, colT[:, col:col + 1])
                ins.then_inc(full_ready, 1)
                turned = []
                for n in range(-LEAD, UNITS):
                    (p, u), m = divmod(n, 2 * T), n + LEAD
                    if n >= 0:
                        probabilities(p, u)
                    if m < UNITS:
                        uses[0] += 1
                    if u == 2 and p >= 1:
                        outputs(p - 1)
                    q, at_m = divmod(m, 2 * T)
                    if at_m == 2 and 1 <= q <= NP:
                        uses[0] += 1
                    if at_m in (8, 12) and q + 1 < NP:
                        spread(q + 1, (at_m - 8) // 4)
                    if q + 1 == NP // 2 - 1 and at_m in (11, 13):
                        if at_m == 11:
                            act.wait_ge(full_ready, b + 1)
                        high_parts(1, (at_m - 11) // 2)
                    if u == 13 and p >= 1:
                        uses[0] += 1
                        turned.append(uses[0])
                outputs(NP - 1)
                for k in range(NB):
                    act.wait_ge(ot_turned, b * NB + k + 1)
                    for c in range(KC):
                        ins = act.activation(hT[:, k, c, :], ps[:, 4 * k + c, :], ACT.Copy)
                    ins.then_inc(hT_ready, 1)
                for k in range(NB):
                    act.wait_ge(y_done, b * 12 + 4 + k + 1)
                    residual(k, 4 * k + 2, M_G_A, mod[:, M_BG:M_BG + KC])

                context_attention(1, 3, None, C_BQC, 6, None, colT[:, C_BCP:C_BCP + KC], 4, (mod, M_SC_M, M_SH_M))

                n0 = b * NB * NC_HID

                def mlp_out(done, k, scale, bias):
                    act.wait_ge(done, n0 + k * NC_HID + NC_HID)
                    residual(k, 4 + 2 * k, scale, bias)
                for n in range(NB * NC_HID):
                    act.wait_ge(h2_done, n0 + n + 1)
                    if n >= 4:
                        act.wait_ge(w22_done, n0 + n - 3)
                    m = n % NC_HID
                    for dst in (gelus[0], gelu):
                        ins = act.activation(dst[:, n % 4, :], ps[:, n % 4, :], ACT.Gelu_apprx_tanh, bias=colT[:, C_BM1 + m:C_BM1 + m + 1])
                    ins.then_inc(h2_ready, 1)
                    if n == 5:
                        ln(4, 1, (mod, M_SC_M, M_SH_M), 6)
                    if n == NC_HID + 1:
                        mlp_out(w22_done, 0, M_G_M, mod[:, M_BG + 2:M_BG + 2 + KC])
                    if n == NC_HID + 7:
                        ln(5, 0, (mod, M3_SC_SA, M3_SH_SA), 4)
                mlp_out(w22_done, 1, M_G_M, mod[:, M_BG + 2:M_BG + 2 + KC])

                def window_queries_keys(k):
                    act.wait_ge(qk3_done, b * NB + k + 1)
                    for m in range(KC):
                        affine(qT[:, k, m, :], ps[:, 4 * k + m, :], 1.0, colT[:, C_BQ3 + m:C_BQ3 + m + 1])
                    for m in range(KC):
                        ins = affine(kT3[:, k, m, :], ps[:, 4 * k + KC + m, :], 1.0, colT[:, C_BK3 + m:C_BK3 + m + 1])
                    ins.then_inc(qk3_ready, 1)

                window_queries_keys(0)
                ln(5, 1, (mod, M3_SC_SA, M3_SH_SA))
                u0 = b * N_UNIT

                def window_exp(u):
                    act.wait_ge(ws_read, u0 + u + 1)
                    act.activation(prob[:, u % 2, :], prob[:, u % 2, :], ACT.Exp, scale=QK_SCALE).then_inc(wp_exp, 1)

                def window_copy(u):
                    act.wait_ge(wp_turned, u0 + u + 1)
                    if u >= 2:
                        act.wait_ge(wpv_done, u0 + u - 1)
                    act.activation(wprobT[:, u % 2, :, :], ps[:, 4:6, :].rearrange("p a (j q) -> p (a j) q", q=P), ACT.Copy).then_inc(wpT_ready, 1)
                window_exp(0)
                window_exp(1)
                window_queries_keys(1)
                window_copy(0)
                for u in range(N_UNIT):
                    if u + 1 < N_UNIT:
                        window_copy(u + 1)
                    if u + 2 < N_UNIT:
                        window_exp(u + 2)
                for k in range(NB):
                    act.wait_ge(y_done, b * 12 + 8 + k + 1)
                    residual(k, 6 * k, M3_G_SA, mod[:, M_BG + 4:M_BG + 4 + KC])

                t0 = b * T

                def top_copy(t):
                    act.wait_ge(ts_ready, t0 + t + 1)
                    if t >= 3:
                        act.wait_ge(tp_turned, 2 * t0 + 2 * t - 4)
                    act.activation(prob3[:, t % 3, :], ps[:, 0:2, :].rearrange("p a n -> p (a n)"), ACT.Copy).then_inc(ts_read, 1)

                def exp(t):
                    act.wait_ge(top_sub, t0 + t + 1)
                    act.activation(prob3[:, t % 3, :], prob3[:, t % 3, :], ACT.Exp, scale=QK_SCALE).then_inc(top_exp, 1)

                def turned(t):
                    for half in range(2):
                        act.wait_ge(tp_turned, 2 * t0 + 2 * t + half + 1)
                        if t >= 2:
                            act.wait_ge(tpv_done, t0 + t - 1)
                        act.activation(probT[:, t % 2, 4 * half:4 * half + 4, :], ps[:, 2 + half, :].rearrange("p (j q) -> p j q", q=P), ACT.Copy).then_inc(tpT_ready, 1)

                def outputs3(t):
                    act.wait_ge(to_turned, t0 + t + 1)
                    act.activation(oT[:, t // TB, :, t % TB * P:(t % TB + 1) * P], ps[:, 2, 0:D].rearrange("p (c q) -> p c q", c=KC), ACT.Copy).then_inc(toT_ready, 1)

                def residual6(k, bank):
                    act.wait_ge(y_done, b * 12 + 10 + k + 1)
                    residual(k, bank, M3_G_CA, mod[:, M_BG + 6:M_BG + 6 + KC])

                def hidden(n):
                    k, m = n // NC_HID, n % NC_HID
                    act.wait_ge(h3_done, 2 * n0 + 2 * n + 1)
                    if m >= 4:
                        act.wait_ge(w32_done, n0 + n - 3)
                    act.activation(gate3[k][:, m % 4, :], ps[:, 4, :], ACT.Silu, bias=colT[:, C_BM13 + m:C_BM13 + m + 1])
                    act.wait_ge(h3_done, 2 * n0 + 2 * n + 2)
                    col = C_BM13 + NC_HID + m
                    affine(up3[k][:, m % 4, :], ps[:, 5, :], 1.0, colT[:, col:col + 1]).then_inc(h3_read, 1)

                def mlp3_out(k):
                    act.wait_ge(w32_done, n0 + k * NC_HID + NC_HID)
                    residual(k, 6 * (1 - k), M3_G_ML, mod[:, M_BG + 8:M_BG + 8 + KC])

                ln(6, 0, (mod, M3_SC_CA, M3_SH_CA))
                query(2, 0, C_BQ3C)
                top_copy(0)
                ln(6, 1, (mod, M3_SC_CA, M3_SH_CA))
                query(2, 1, C_BQ3C)
                top_copy(1)
                top_copy(2)
                exp(0)
                turned(0)
                for t in range(1, TB):
                    exp(t)
                    top_copy(t + 2)
                    outputs3(t - 1)
                    turned(t)
                exp(4)
                outputs3(3)
                residual6(0, 6)
                top_copy(6)
                turned(4)
                exp(5)
                top_copy(7)
                ln(7, 0, (mod, M3_SC_ML, M3_SH_ML), 6)
                hidden(0)
                outputs3(4)
                turned(5)
                exp(6)
                hidden(1)
                hidden(2)
                outputs3(5)
                hidden(3)
                turned(6)
                exp(7)
                hidden(4)
                outputs3(6)
                hidden(5)
                turned(7)
                hidden(6)
                outputs3(7)
                residual6(1, 2)
                hidden(7)
                ln(7, 1, (mod, M3_SC_ML, M3_SH_ML), 2)
                for n in range(NC_HID, 2 * NC_HID):
                    hidden(n)
                    if n == NC_HID:
                        mlp3_out(0)
                mlp3_out(1)

        @block.vector
        def _(dve):
            steps = [0]

            def link(ins):
                steps[0] += 1
                ins.then_inc(dve_step, 1)
                dve.wait_ge(dve_step, steps[0])

            dve.wait_ge(ctx_ld, 16)
            link(dve.bn_stats(s_st[:, 0:6], s_ctx[:, :]))
            link(dve.bn_aggr(s_st[:, 6:8], s_st[:, 0:6]))
            dve.tensor_scalar(s_st[:, 8:9], s_st[:, 7:8], EPS5, None, ALU.add)
            dve.tensor_scalar(s_st[:, 9:10], s_st[:, 7:8], EPS6, None, ALU.add).then_inc(ctx_var, 1)
            dve.wait_ge(ctx_rstd, 1)
            for v in range(2):
                dve.tensor_scalar(s_xh[:, v, :], s_ctx[:, :], s_st[:, 6:7], s_st[:, 10 + v:11 + v], ALU.subtract, ALU.mult)
            dve.tensor_copy(s_xh[:, 2, :], s_ctx[:, :]).then_inc(set_dve, 1)
            dve.wait_ge(set_pe, 1)
            dve.tensor_copy(colT[:, :], ps[:, 0, 0:N_COL]).then_inc(set_dve, 1)
            dve.wait_ge(consts_ld, 13 * 16)
            dve.tensor_copy(sel[:, :, :, :], s_sel[:, :, :, :])
            link(dve.memset(v_ctx2[:, :, :, :, :], 0.0))
            dve.wait_ge(set_dve, 2)
            dve.wait_ge(set_pe, 3)
            def plus_biases(first, bank, lot, lots, chunks):
                n = lots * chunks
                rows = ps[:, bank, :].rearrange("p (q i s) -> p s i q", q=4, i=4)
                return dve.tensor_tensor(mod2[:, :, first:first + n].rearrange("p b (i q) -> p b i q", q=chunks),
                                         rows[:, 0:B, lot:lot + lots, 0:chunks],
                                         colT[:, first:first + n].rearrange("p (i q) -> p i q", q=chunks).unsqueeze(1).broadcast_to([P, B, lots, chunks]), ALU.add)
            plus_biases(0, 4, 0, 4, 4)
            plus_biases(16, 5, 0, 4, 4)
            plus_biases(32, 6, 0, 1, 4)
            link(plus_biases(36, 6, 1, 1, 2))
            for m in SCALES:
                ins = dve.tensor_scalar(mod2[:, :, m:m + KC], mod2[:, :, m:m + KC], 1.0, None, ALU.add)
            for i, m in enumerate(GATED):
                o = M_BG + KC * i
                ins = dve.tensor_tensor(mod2[:, :, o:o + KC], mod2[:, :, m:m + KC],
                                        colT[:, o:o + KC].unsqueeze(1).broadcast_to([P, B, KC]), ALU.mult)
            link(ins)
            dve.wait_ge(set_pe, 2)
            for c in range(KC):
                for b in range(B):
                    for dup in range(2):
                        ins = dve.tensor_scalar(s_ctxT[:, 0, c, b, dup, :], ps[:, 1, c * P + b * S:c * P + (b + 1) * S],
                                                mod2[:, b, M_SC_KV + c:M_SC_KV + c + 1], mod2[:, b, M_SH_KV + c:M_SH_KV + c + 1], ALU.mult, ALU.add)
            ins.then_inc(set_dve, 1)
            dve.wait_ge(set_pe, 4)
            plus_biases(M_HB, 7, 0, E, RH // P)
            plus_biases(M_HB + MC, 7, E, 1, KC)
            for b in range(B):
                dve.tensor_tensor(rc2[:, b, :], ps[:, 7, 480 + 4 * b:480 + 4 * b + E], rb[:, :], ALU.add)
            dve.wait_ge(set_pe, 5)
            dve.tensor_copy(s_wqT[:, :, :].rearrange("p j i -> p (j i)"), ps[:, 6, :]).then_inc(set_dve, 1)
            dve.wait_ge(set_pe, 6)
            for m in range(KC):
                for i, (bank, slot, col) in enumerate(((0, m, C_BK0), (0, KC + m, C_BKC), (1, m, C_BK3C))):
                    dve.tensor_scalar(kT2[:, i, m, :, :], ps[:, bank, slot * P:(slot + 1) * P].rearrange("p (b s) -> p b s", b=B),
                                      colT[:, col + m:col + m + 1], None, ALU.add)
                dve.tensor_copy(s_k1T[:, m, :], ps[:, 1, (KC + m) * P:(KC + m + 1) * P])
                for dup in range(2):
                    ins = dve.tensor_copy(s_vT[:, m, :, dup, :], ps[:, 2, m * P:(m + 1) * P].rearrange("p (b s) -> p b s", b=B))
            ins.then_inc(set_dve, 1)
            dve.wait_ge(set_pe, 7)
            for i, bank in enumerate((3, 6, 7)):
                for b in range(B):
                    for odd in range(2):
                        r = slice(S * odd, S * odd + S)
                        ins = dve.tensor_tensor(v_ctx2[r, b, i, :, HD * odd:HD * odd + HD],
                                                ps[r, bank, b * D:(b + 1) * D].rearrange("p (j c) -> p j c", c=2 * HD)[:, :, HD * odd:HD * odd + HD],
                                                s_vb[r, i, :].rearrange("p (j c) -> p j c", c=2 * HD)[:, :, HD * odd:HD * odd + HD], ALU.add)
            ins.then_inc(set_dve, 1)
            dve.wait_ge(set_pe, 8)
            dve.tensor_copy(kw2[:, :, :, :].rearrange("p i b s -> p i (b s)"), ps[:, 0, 0:KC * P].rearrange("p (i n) -> p i n", i=KC)).then_inc(set_dve, 1)
            dve.wait_ge(set_dve, 7)
            dve.wait_ge(dve_step, steps[0])

            with dve.Fori(0, B) as b:
                dve.sem_clear(dve_step)
                steps[0] = 0
                def statistics(i, k):
                    for t in range(TB):
                        ins = dve.bn_stats(st[:, k, t, :], x[:, TB * k + t, :])
                    link(ins)
                    for t in range(TB):
                        ins = dve.bn_aggr(mv[:, k, t, :], st[:, k, t, :])
                    link(ins)
                    dve.tensor_scalar(ve[:, k, :], mv[:, k, :, 1], EPS5 if i < 2 else EPS6, None, ALU.add).then_inc(ve_ready, 1)

                def normalise(i, k):
                    dve.wait_ge(rstd_ready, b * 2 * N_LN + 2 * i + k + 1)
                    for t in range(TB):
                        ins = dve.tensor_scalar(xhat[:, TB * k + t, :], x[:, TB * k + t, :], mv[:, k, t, 0:1], rstd[:, k, t:t + 1], ALU.subtract, ALU.mult)
                    ins.then_inc(xhat_ready, 1)

                def residual(i, k, bank=None):
                    bank = 4 * k if bank is None else bank
                    dve.wait_ge(y_turned, b * 2 * N_RES + 2 * i + k + 1)
                    return dve.tensor_tensor(x[:, TB * k:TB * (k + 1), :].rearrange("p t d -> p (t d)"),
                                             x[:, TB * k:TB * (k + 1), :].rearrange("p t d -> p (t d)"),
                                             ps[:, bank:bank + 2, :].rearrange("p a n -> p (a n)"), ALU.add)

                def residual_norm(i):
                    link(residual(i, 0))
                    statistics(i + 1, 0)
                    link(residual(i, 1))
                    normalise(i + 1, 0)
                    statistics(i + 1, 1)
                    normalise(i + 1, 1)

                def build_keys(i):
                    for c in range(KC):
                        dve.tensor_tensor(kblk[:, c, :, :], kT[:, i, c, :].unsqueeze(1).broadcast_to([P, HC, S]),
                                                head_mask[:, :].unsqueeze(2).broadcast_to([P, HC, S]), ALU.mult)
                    dve.tensor_copy(vx[:, :, 0:2 * HD], v_ctx[:, i, :, :])
                    dve.tensor_copy(vx[:, :, 2 * HD:], ones_ctx[:, :].unsqueeze(1).broadcast_to([P, HC, 64 - 2 * HD])).then_inc(kblk_ready, 1)

                def outputs(t, bank, u0, done, turned, ready):
                    dve.wait_ge(done, u0 + t + 1)
                    o = ps[:, bank, :].rearrange("p (j c) -> p j c", j=HC)
                    r = rs[:, t % 2 * H:(t % 2 + 1) * H].rearrange("p (j a) -> p j a", a=2)
                    link(dve.reciprocal(r, o[:, :, 2 * HD:2 * HD + 2]))
                    if t >= 2:
                        dve.wait_ge(turned, u0 + t - 1)
                    dve.tensor_tensor(o_tok[:, t % 2, :].rearrange("p (j a d) -> p j a d", j=HC, a=2), o[:, :, 0:2 * HD].rearrange("p j (a d) -> p j a d", a=2),
                                      r.unsqueeze(3).broadcast_to([P, HC, 2, HD]), ALU.mult).then_inc(ready, 1)

                def context_attention(i, step):
                    u0 = b * 2 * T + T * i

                    def heads(t):
                        return ps[:, 2 * (t % 2):2 * (t % 2) + 2, :].rearrange("p a (h s) -> p (a h) s", s=S)

                    def centre(t):
                        dve.wait_ge(s_ready, u0 + t + 1)
                        link(dve.tensor_reduce(mx[:, t % 2, :], heads(t), X, ALU.max))
                        if t >= 2:
                            dve.wait_ge(p_turned, u0 + t - 1)
                        dve.tensor_tensor(prob[:, t % 2, :].rearrange("p (h s) -> p h s", s=S), heads(t),
                                          mx[:, t % 2, :].unsqueeze(2).broadcast_to([P, H, S]), ALU.subtract).then_inc(s_read, 1)

                    def divide(t):
                        outputs(t, 6, u0, pv_done, o_turned, o_ready)

                    centre(0)
                    centre(1)
                    for t in range(T + 1):
                        if t + 2 < T:
                            centre(t + 2)
                        if t >= 1:
                            divide(t - 1)
                        if t == T - 1:
                            link(residual(step, 0))
                            statistics(step + 1, 0)
                    normalise(step + 1, 0)

                dve.wait_ge(x_ld[0], b * 16 + 16)
                statistics(0, 0)
                dve.wait_ge(set_act, 4)
                dve.tensor_copy(mod[:, :], mod2[:, b, :])
                dve.tensor_copy(v_ctx[:, :, :, :], v_ctx2[:, b, :, :, :])
                dve.tensor_copy(kT[:, :, :, :], kT2[:, :, :, b, :])
                dve.tensor_copy(kw[:, :, 0:S], kw2[:, :, b, :])
                dve.tensor_copy(rc[:, :], rc2[:, b, :]).then_inc(begun, 1)
                dve.wait_ge(begun, b + 1)
                normalise(0, 0)
                dve.wait_ge(x_ld[1], b * 48 + 48)
                statistics(0, 1)
                build_keys(0)
                normalise(0, 1)
                context_attention(0, 0)
                link(residual(0, 1))
                statistics(1, 1)

                def evidence(k):
                    return ps[:, 4 * k + 3, 0:TB * (S + E)].rearrange("p (t n) -> p t n", n=S + E)

                def evidence_centre(k):
                    dve.wait_ge(p1s_done, b * NB + k + 1)
                    sc = evidence(k)[:, :, 0:S]
                    link(dve.tensor_reduce(r1m[:, k, :], sc, X, ALU.max))
                    dve.tensor_tensor(p1[:, k, :, 0, :], sc, r1m[:, k, :].unsqueeze(2).broadcast_to([P, TB, S]), ALU.subtract).then_inc(p1_sub, 1)

                def evidence_divide(k):
                    dve.wait_ge(p1_exp, b * NB + k + 1)
                    link(dve.tensor_reduce(r1m[:, k, :], p1[:, k, :, 0, :], X, ALU.add))
                    link(dve.reciprocal(r1m[:, k, :], r1m[:, k, :]))
                    for copy in (1, 0):
                        ins = dve.tensor_tensor(p1[:, k, :, copy, :], p1[:, k, :, 0, :], r1m[:, k, :].unsqueeze(2).broadcast_to([P, TB, S]), ALU.mult)
                    ins.then_inc(p1_ready, 1)

                def evidence_lo(k):
                    dve.wait_ge(p1T_hi, b * NB + k + 1)
                    dve.tensor_tensor(p1lo[:, k, :], ps[0:S, 4 * k, :], p1T[0:S, k, :].bitcast(F32), ALU.subtract).then_inc(p1T_ready, 1)

                evidence_centre(0)
                normalise(1, 1)
                evidence_divide(0)
                evidence_lo(0)
                evidence_centre(1)
                evidence_divide(1)
                evidence_lo(1)
                for k in range(NB):
                    dve.wait_ge(lg_done, b * NB + k + 1)
                    link(dve.tensor_tensor(lg[:, k, :, :], ps[:, 4 * k, 0:TB * E].rearrange("p (t e) -> p t e", e=E),
                                           rc[:, :].unsqueeze(1).broadcast_to([P, TB, E]), ALU.add))
                    link(dve.tensor_tensor(lg[:, k, :, :], lg[:, k, :, :], evidence(k)[:, :, S:], ALU.add))
                    link(dve.tensor_reduce(rm[:, k, :], lg[:, k, :, :], X, ALU.max))
                    dve.tensor_tensor(lg[:, k, :, :], lg[:, k, :, :], rm[:, k, :].unsqueeze(2).broadcast_to([P, TB, E]), ALU.subtract).then_inc(lg_sub, 1)
                for k in range(NB):
                    dve.wait_ge(lg_exp, b * NB + k + 1)
                    link(dve.tensor_reduce(rm[:, k, :], lg[:, k, :, :], X, ALU.add))
                    link(dve.reciprocal(rm[:, k, :], rm[:, k, :]))
                    dve.tensor_tensor(lg[:, k, :, :], lg[:, k, :, :], rm[:, k, :].unsqueeze(2).broadcast_to([P, TB, E]), ALU.mult).then_inc(lg_ready, 1)
                dve.wait_ge(pbc_ready, b * NB + NB)
                n0 = b * NB * MC

                def gated(k):
                    dve.wait_ge(y_done, b * 12 + 2 + k + 1)
                    for m in range(KC):
                        ins = dve.scalar_tensor_tensor(yT[:, k, m, :], ps[:, 4 + 2 * k + m, :], colT[:, C_OUTB + m:C_OUTB + m + 1], gT[:, k, m, :], ALU.add, ALU.mult)
                    ins.then_inc(yT_ready, 1)

                def add_v2(k):
                    dve.wait_ge(v_done, b * NB + k + 1)
                    for j in range(2):
                        t = TB * k + 2 * j
                        ins = dve.tensor_tensor(v2[:, t:t + 2, 0:H * VS].rearrange("p t (h d) -> p t h d", d=VS)[:, :, :, 0:HD], ps[:, 4 * k + 2 + j, :].rearrange("p (t h d) -> p t h d", t=2, d=HD),
                                                vb2[:, :].rearrange("p (h d) -> p h d", d=HD).unsqueeze(1).broadcast_to([P, 2, H, HD]), ALU.add)
                    ins.then_inc(v_ready, 1)

                for n in range(NB * MC):
                    dve.wait_ge(h1_act, n0 + n + 1)
                    dve.tensor_tensor(ring[:, n % 4, :], ring[:, n % 4, :], p_bc[:, n // MC, n % MC // 4, :], ALU.mult).then_inc(h1_ready, 1)
                    if n == MC + 3:
                        gated(0)
                    if n == MC + 6:
                        link(residual(1, 0, 4))
                        statistics(2, 0)
                    if n == MC + 7:
                        normalise(2, 0)
                gated(1)
                dve.wait_ge(yT_ready, b * 2 * N_RES + 4)
                add_v2(0)
                link(residual(1, 1))
                statistics(2, 1)
                normalise(2, 1)

                add_v2(1)
                u0 = b * N_RING
                uses = [0]

                def place():
                    n = uses[0]
                    uses[0] += 1
                    dve.wait_ge(ring_ready, u0 + n + 1)
                    return ps[:, 2 * (n % 2):2 * (n % 2) + 2, :].rearrange("p a q -> p (a q)")

                def low_parts(qk):
                    dve.wait_ge(hi_ready, b * 2 * KC + qk + 1)
                    col = (C_BQ2, C_BK2)[qk]
                    dve.scalar_tensor_tensor(dense[2 * qk + 1][:, :], place(), colT[:, col:col + 1], dense[2 * qk][:, :].bitcast(F32),
                                             ALU.add, ALU.subtract).then_inc(ring_read, 1)

                def query_maximum(u):
                    e, t = 1 - u % 2, u // 2
                    return dve.tensor_reduce(mm[:, e, t:t + 1], place(), X, ALU.max).then_inc(ring_read, 1)

                def maxima(p):
                    dve.wait_ge(ring_read, b * N_SCORE + reads())
                    link(dve.tensor_copy(mh[:, :, :], mm[:, :, :]))
                    cols = mt[:, :, :].rearrange("p t (e c) -> p e t c", e=2)
                    dve.tensor_copy(cols[:, :, :, 48], mh[:, :, :].bitcast(F32))
                    dve.tensor_tensor(cols[:, :, :, 49], mm[:, :, :], mh[:, :, :].bitcast(F32), ALU.subtract).then_inc(mt_ready, 1)
                    dve.wait_ge(mt_ready, b * NP + p + 1)

                def add_maxima(p):
                    dve.tensor_tensor(qx[:, p % 4, :], place(), qx[:, p % 4, :].bitcast(F32), ALU.add).then_inc(ring_read, 1)

                def finish(p):
                    acc = place()[:, 0:BLK].rearrange("p (j e h c) -> p j e h c", j=TB, e=2, h=2)
                    link(dve.reciprocal(fr[:, p % 2, :, :].rearrange("p j (e h) -> p j e h", h=2), acc[:, :, :, :, HD]))
                    for half in range(2):
                        ins = dve.tensor_tensor(xhat[:, half * TB:(half + 1) * TB, 2 * HD * p:2 * HD * (p + 1)].rearrange("p t (e d) -> p t e d", d=HD),
                                                acc[:, :, :, half, 0:HD],
                                                fr[:, p % 2, :, :].rearrange("p j (e h) -> p j e h", h=2)[:, :, :, half].unsqueeze(3).broadcast_to([P, TB, 2, HD]), ALU.mult)
                    ins.then_inc(ring_read, 1)

                spreads = [0]

                def reads():
                    return uses[0] - spreads[0]

                for qk in range(2):
                    low_parts(qk)
                uses[0] += 2
                spreads[0] += 2
                dve.wait_ge(mt_clear, b + 1)
                for n in range(-LEAD, UNITS):
                    (p, u), m = divmod(n, 2 * T), n + LEAD
                    q, at_m = divmod(m, 2 * T)
                    if m < UNITS:
                        query_maximum(at_m)
                    if at_m == 2 and 1 <= q <= NP:
                        add_maxima(q - 1)
                    if at_m in (8, 12) and q + 1 < NP:
                        uses[0] += 1
                        spreads[0] += 1
                    if u == 13 and p >= 1:
                        finish(p - 1)
                    if m < UNITS and at_m == 2 * T - 1:
                        maxima(q)
                finish(NP - 1)
                assert uses[0] == N_RING and reads() == N_SCORE
                build_keys(1)
                residual_norm(2)

                context_attention(1, 3)
                n0 = b * NB * NC_HID

                def tokens_lo(k):
                    dve.wait_ge(hT_ready, b * (2 * N_LN + 2) + 10 + k + 1)
                    dve.tensor_tensor(hs[:, k, 1, :, :], hT[:, k, :, :], hs[:, k, 0, :, :].bitcast(F32), ALU.subtract).then_inc(hs_lo, 1)

                def hidden_lo(n):
                    dve.wait_ge(h2_ready, n0 + n + 1)
                    dve.tensor_tensor(gelus[1][:, n % 4, :], gelu[:, n % 4, :], gelus[0][:, n % 4, :].bitcast(F32), ALU.subtract).then_inc(h2_lo, 1)

                tokens_lo(0)
                for n in range(NB * NC_HID):
                    hidden_lo(n)
                    if n == 1:
                        link(residual(3, 1, 6))
                        statistics(4, 1)
                    if n == 2:
                        normalise(4, 1)
                    if n == 5:
                        tokens_lo(1)
                    if n == NC_HID + 3:
                        link(residual(4, 0, 4))
                        statistics(5, 0)
                    if n == NC_HID + 4:
                        normalise(5, 0)
                link(residual(4, 1))
                statistics(5, 1)

                def add_v3(k):
                    dve.wait_ge(v3_done, b * NB + k + 1)
                    for j in range(2):
                        t = TB * k + 2 * j
                        for odd in range(2):
                            o = HD * odd
                            ins = dve.tensor_tensor(
                                v3[:, t:t + 2, :, :].rearrange("p t (j o) d -> p t j o d", o=2)[:, :, :, odd, o:o + HD],
                                ps[:, 4 * k + j, :].rearrange("p (t j d) -> p t j d", t=2, d=2 * HD)[:, :, :, o:o + HD],
                                vb3[:, :].rearrange("p (j d) -> p j d", d=2 * HD)[:, :, o:o + HD].unsqueeze(1).broadcast_to([P, 2, H // 2, HD]), ALU.add)
                    ins.then_inc(v3_ready, 1)
                w0 = b * N_UNIT

                def window_centre(u):
                    dve.wait_ge(ws_ready, w0 + u + 1)
                    sc = ps[:, 2 * (u % 2):2 * (u % 2) + 2, :].rearrange("p a (h s) -> p (a h) s", s=P)
                    link(dve.tensor_reduce(mx[:, u % 2, 0:HC], sc, X, ALU.max))
                    if u >= 2:
                        dve.wait_ge(wp_turned, w0 + u - 1)
                    dve.tensor_tensor(prob[:, u % 2, :].rearrange("p (h s) -> p h s", s=P), sc,
                                      mx[:, u % 2, 0:HC].unsqueeze(2).broadcast_to([P, HC, P]), ALU.subtract).then_inc(ws_read, 1)

                def window_divide(u):
                    t, c = u // KC, u % KC
                    dve.wait_ge(wpv_done, w0 + u + 1)
                    r = rs[:, u % 2 * P:(u % 2 + 1) * P]
                    link(dve.reciprocal(r, ps[:, 6 + u % 2, P:2 * P]))
                    dve.tensor_tensor(oT[:, t // TB, c, t % TB * P:(t % TB + 1) * P], ps[:, 6 + u % 2, 0:P], r, ALU.mult).then_inc(wo_ready, 1)
                add_v3(0)
                normalise(5, 1)
                window_centre(0)
                window_centre(1)
                add_v3(1)
                for u in range(N_UNIT):
                    if u + 2 < N_UNIT:
                        window_centre(u + 2)
                    window_divide(u)
                link(residual(5, 0))
                statistics(6, 0)
                normalise(6, 0)
                link(residual(5, 1))
                statistics(6, 1)

                build_keys(2)
                normalise(6, 1)
                t0 = b * T

                def scores_by_head(t):
                    return prob3[:, t % 3, :].rearrange("p (h s) -> p h s", s=S)

                def taken_by_head(t):
                    return taken[:, t % 2, :].rearrange("p (h s) -> p h s", s=S)

                def best(t):
                    dve.wait_ge(ts_read, t0 + t + 1)
                    dve.sem_inc(passed, 1)
                    for h in range(H):
                        ins = dve.max(m8[:, t % 2, h, 0:8], scores_by_head(t)[:, h, :])
                    link(ins)

                def mark(t):
                    for h in range(H):
                        ins = dve.match_replace(taken_by_head(t)[:, h, :], m8[:, t % 2, h, 0:8], scores_by_head(t)[:, h, :], LOWEST)
                    ins.then_inc(top_marked, 1)
                    dve.wait_ge(top_marked, t0 + t + 1)
                    dve.sem_inc(passed, 1)

                def next_best(t):
                    for h in range(H):
                        ins = dve.max(m8[:, t % 2, h, 8:16], taken_by_head(t)[:, h, :])
                    link(ins)

                def mark_next(t):
                    for h in range(H):
                        ins = dve.match_replace(taken_by_head(t)[:, h, :], m8[:, t % 2, h, 8:16], taken_by_head(t)[:, h, :], LOWEST)
                    link(ins)

                def take_top(t):
                    best(t)
                    mark(t)
                    next_best(t)
                    mark_next(t)

                def mask(t):
                    dve.wait_ge(top_exp, t0 + t + 1)
                    dve.scalar_tensor_tensor(prob3[:, t % 3, :], taken[:, t % 2, :], LOWEST, prob3[:, t % 3, :], ALU.is_equal, ALU.mult).then_inc(top_ready, 1)

                def divide(t):
                    outputs(t, 3, t0, tpv_done, to_turned, to_ready)

                n0 = b * NB * NC_HID

                def times(n):
                    k, m = n // NC_HID, n % NC_HID
                    dve.wait_ge(h3_read, n0 + n + 1)
                    dve.tensor_tensor(gate3[k][:, m % 4, :], gate3[k][:, m % 4, :], up3[k][:, m % 4, :], ALU.mult).then_inc(h3_ready, 1)

                def add(k, bank):
                    link(residual(6, k, bank))
                    statistics(7, k)

                take_top(0)
                take_top(1)
                mask(0)
                take_top(2)
                divide(0)
                mask(1)
                take_top(3)
                divide(1)
                mask(2)
                best(4)
                mark(4)
                divide(2)
                mask(3)
                next_best(4)
                mark_next(4)
                best(5)
                divide(3)
                mask(4)
                mark(5)
                next_best(5)
                add(0, 6)
                mark_next(5)
                normalise(7, 0)
                best(6)
                divide(4)
                mask(5)
                mark(6)
                times(0)
                next_best(6)
                mark_next(6)
                times(1)
                divide(5)
                best(7)
                mask(6)
                mark(7)
                times(2)
                next_best(7)
                times(3)
                mark_next(7)
                divide(6)
                times(4)
                mask(7)
                times(5)
                divide(7)
                times(6)
                add(1, 2)
                times(7)
                normalise(7, 1)
                for n in range(NC_HID, 2 * NC_HID):
                    times(n)
                    if n == NC_HID + 1:
                        residual(7, 0, 6).then_inc(x_final, 1)
                residual(7, 1, 0).then_inc(x_final, 1)
                dve.wait_ge(x_final, b * NB + NB)

        @block.gpsimd
        def _(pool):
            pool.memset(s_silu[:, :, :], 0.0)
            pool.memset(s_cond[:, :, :], 0.0)
            pool.memset(minus_half[:, :], -0.5).then_inc(set_pool, 1)
            pool.wait_ge(set_pool, 1)
            pool.wait_ge(ctx_var, 1)
            pool.tensor_tensor(s_st[:, 10:12], s_st[:, 8:10], minus_half[:, 0:2], ALU.pow).then_inc(ctx_rstd, 1)
            with pool.Fori(0, B) as b:
                def ln(i, blocks=range(NB)):
                    for k in blocks:
                        pool.wait_ge(ve_ready, b * 2 * N_LN + 2 * i + k + 1)
                        pool.tensor_tensor(rstd[:, k, :], ve[:, k, :], minus_half[:, :], ALU.pow).then_inc(rstd_ready, 1)

                ln(0)
                pool.tensor_copy(vw[:, :], vw2[:, b, :]).then_inc(vw_hi, 1)
                pool.wait_ge(vw_hi, b + 1)
                pool.tensor_tensor(vw[S:2 * S, :], vw2[S:2 * S, b, :], vw[S:2 * S, :].bitcast(F32), ALU.subtract).then_inc(vw_ready, 1)
                pool.wait_ge(vw_ready, b + 1)
                ln(1)
                pool.wait_ge(y_done, b * 12 + 2)
                pool.sem_inc(passed, 1)
                pool.memset(mt[:, :, :], 0.0).then_inc(mt_clear, 1)
                ln(2)
                pool.wait_ge(y_turned, b * 2 * N_RES + 4)
                pool.sem_inc(passed, 1)
                pool.memset(v2[:, :, H * VS:], 0.0)
                pool.memset(v2[:, :, 0:H * VS].rearrange("p t (h d) -> p t h d", d=VS)[:, :, :, HD:VS], 1.0).then_inc(v2_clear, 1)
                for qk in range(2):
                    pool.wait_ge(hi_ready, b * 2 * KC + 2 + qk + 1)
                    pool.tensor_tensor(dense[2 * qk + 1][:, :], full[qk], dense[2 * qk][:, :].bitcast(F32), ALU.subtract).then_inc(lo_ready, 1)
                ln(3)
                pool.wait_ge(pv2_done, b * T * NP + T * NP)
                pool.sem_inc(passed, 1)
                pool.wait_ge(rc1_ld, 9 * 16)
                for i, (parts, w) in enumerate(((w1s, wm1), (w2s, wm2))):
                    pool.tensor_copy(parts[:, 0, :, :], w[:, :, :]).then_inc(w_hi, 1)
                    pool.wait_ge(w_hi, b * 2 + i + 1)
                    pool.tensor_tensor(parts[:, 1, :, :], w[:, :, :], parts[:, 0, :, :].bitcast(F32), ALU.subtract).then_inc(w_split, 1)
                ln(4)
                ln(5, (0,))
                pool.wait_ge(h2_done, b * NB * NC_HID + NB * NC_HID)
                pool.sem_inc(passed, 1)
                pairs = v3[:, :, :, :].rearrange("p t (j o) d -> p (t j) o d", o=2)
                pool.memset(pairs[:, :, 0, HD:2 * HD], 0.0)
                pool.memset(pairs[:, :, 1, 0:HD], 0.0).then_inc(v3_clear, 1)
                ln(5, (1,))
                u0 = b * N_UNIT
                for u in range(N_UNIT):
                    t, c = u // KC, u % KC
                    if u % N_UNIT in (0, N_UNIT // 2):
                        pool.wait_ge(qk3_ready, b * NB + t // TB + 1)
                    if u >= 2:
                        pool.wait_ge(ws_ready, u0 + u - 1)
                    pool.tensor_tensor(wkblk[:, u % 2, :, :], kT3[:, t // TB, c, t % TB * P:(t % TB + 1) * P].unsqueeze(1).broadcast_to([P, HC, P]),
                                       head_mask[:, :].unsqueeze(2).broadcast_to([P, HC, P]), ALU.mult).then_inc(wk_ready, 1)
                ln(6)
                t0 = b * T

                def centre(t):
                    pool.wait_ge(top_marked, t0 + t + 1)
                    sc = prob3[:, t % 3, :].rearrange("p (h s) -> p h s", s=S)
                    pool.tensor_tensor(sc, sc, m8[:, t % 2, :, 0].unsqueeze(2).broadcast_to([P, H, S]), ALU.subtract).then_inc(top_sub, 1)
                for t in range(6):
                    centre(t)
                ln(7, (0,))
                centre(6)
                centre(7)
                ln(7, (1,))


def constants():
    row = np.arange(P)
    head_mask = (row[:, None] // HD == np.arange(HC)).astype(np.float32)
    ones_ctx = (row[:, None] // S == np.arange(64 - 2 * HD)).astype(np.float32)
    ones_win = np.zeros((P, 2, 2 * HD), np.float32)
    ones_win[:, 0, :HD] = 1
    ones_win[:, 1, HD:] = 1
    sel = np.zeros((P, 4, 4, P), np.float32)
    d = np.arange(HD)
    for pp in range(4):
        for e in range(2):
            r = 32 * pp + HD * e + d
            for part, places in enumerate(((0, 2), (1,), (0, 1), (2,))):
                for place in places:
                    sel[r, pp, part, 64 * e + HD * place + d] = 1
    k_aug = np.zeros((P, 1), np.float32)
    k_aug[[48, 49, 64 + 48, 64 + 49]] = -1
    sel3 = np.zeros((E, E, P), np.float32)
    sel3[np.arange(E), np.arange(E)] = 1
    return {"c_ident": np.eye(P, dtype=np.float32), "c_head_mask": head_mask, "c_ones_ctx": ones_ctx,
            "c_ones_win": ones_win, "c_sel": sel, "c_k_aug": k_aug, "c_sel3": sel3}


def kernel(**inputs):
    import concourse.bacc as bacc
    from concourse.bass_utils import run_bass_kernel_spmd

    arrays = {n: np.ascontiguousarray(np.asarray(a)) for n, a in inputs.items()}
    arrays.update(constants())
    nc = bacc.Bacc("TRN2", target_bir_lowering=False, num_devices=1)
    handles = {n: nc.dram_tensor(f"in_{n}_dram", a.shape, mybir.dt.from_np(a.dtype), kind="ExternalInput") for n, a in arrays.items()}
    out = nc.dram_tensor("out_0_dram", (B, L, D), F32, kind="ExternalOutput")
    build(nc, out.ap(), {n: h.ap() for n, h in handles.items()})
    if not nc.is_finalized():
        nc.finalize()
    result = run_bass_kernel_spmd(nc, [{f"in_{n}_dram": a for n, a in arrays.items()}], core_ids=[0])
    return np.asarray(result.results[0]["out_0_dram"])
```
